# Optimizing a Trainium2 kernel written in Bass

```python
import numpy as np
import jax
import jax.numpy as jnp

def _softmax(x, axis=-1):
    return jax.nn.softmax(x, axis=axis)

def _gelu(x):
    return jax.nn.gelu(x, approximate=True)

def _silu(x):
    return jax.nn.silu(x)

def _sigmoid(x):
    return jax.nn.sigmoid(x)

def _layernorm(x, axis=-1, eps=1e-05):
    m = jnp.mean(x, axis=axis, keepdims=True)
    v = jnp.var(x, axis=axis, keepdims=True)
    return (x - m) / jnp.sqrt(v + eps)

def _scatter_add(tgt, idx, src, axis=0):
    return tgt.at[idx].add(src)

def _segment_sum(src, seg, n):
    return jax.ops.segment_sum(src, seg, n)
kernel_name = 'mk_adaln_d1_jaxref_r4_d90d5b'

def setup_inputs(seed: int=0):
    np.random.seed(seed)
    _w = jnp.asarray

    def _L0_attn_setup():
        import jax, jax.numpy as jnp
        import numpy as np
        from jax import lax

        def _phi(x):
            return jax.nn.elu(x) + 1.0
        key = jax.random.key(seed)
        ks = jax.random.split(key, 5)
        B, T, D, H = (8, 1024, 256, 64)
        x = jax.random.normal(ks[0], (B, T, D), dtype=jnp.float32)
        W_q = jax.random.normal(ks[1], (D, H), dtype=jnp.float32) * (1.0 / np.sqrt(D))
        W_k = jax.random.normal(ks[2], (D, H), dtype=jnp.float32) * (1.0 / np.sqrt(D))
        W_v = jax.random.normal(ks[3], (D, H), dtype=jnp.float32) * (1.0 / np.sqrt(D))
        W_o = jax.random.normal(ks[4], (H, D), dtype=jnp.float32) * (1.0 / np.sqrt(H))
        return {'x': x, 'W_q': W_q, 'W_k': W_k, 'W_v': W_v, 'W_o': W_o}
    _L0_attn_in = _L0_attn_setup()

    def _L0_ffn_setup():
        import jax, jax.numpy as jnp
        import numpy as np
        B, L, D, I, E, K = (2, 512, 256, 1024, 8, 2)
        LN_EPS = 1e-05

        def _layernorm(x, g, b):
            m = jnp.mean(x, axis=-1, keepdims=True)
            v = jnp.mean(jnp.square(x - m), axis=-1, keepdims=True)
            return (x - m) * jax.lax.rsqrt(v + LN_EPS) * g + b
        key = jax.random.key(seed)
        ks = jax.random.split(key, 4)
        return {'hidden_states': jax.random.normal(ks[0], (B, L, D), dtype=jnp.float32), 'rn_g': jnp.ones((D,), jnp.float32), 'rn_b': jnp.zeros((D,), jnp.float32), 'router_w': jax.random.normal(ks[1], (E, D), jnp.float32) * 0.02, 'router_b': jnp.zeros((E,), jnp.float32), 'ln_g': jnp.ones((E, D), jnp.float32), 'ln_b': jnp.zeros((E, D), jnp.float32), 'w1': jax.random.normal(ks[2], (E, D, I), jnp.float32) * 0.02, 'b1': jnp.zeros((E, I), jnp.float32), 'w2': jax.random.normal(ks[3], (E, I, D), jnp.float32) * 0.02, 'b2': jnp.zeros((E, D), jnp.float32)}
    _L0_ffn_in = _L0_ffn_setup()
    _L0_c = _w((lambda *s: np.random.randn(*s).astype(np.float32) * 0.05)(16, 256))
    _L0_wmod = _w((lambda *s: np.random.randn(*s).astype(np.float32) * 0.05)(256, 6 * 256) * 256 ** (-0.5))
    _d = {'L0_attn_x': _L0_attn_in['x'], 'L0_attn_W_q': _L0_attn_in['W_q'], 'L0_attn_W_k': _L0_attn_in['W_k'], 'L0_attn_W_v': _L0_attn_in['W_v'], 'L0_attn_W_o': _L0_attn_in['W_o'], 'L0_ffn_rn_g': _L0_ffn_in['rn_g'], 'L0_ffn_rn_b': _L0_ffn_in['rn_b'], 'L0_ffn_router_w': _L0_ffn_in['router_w'], 'L0_ffn_router_b': _L0_ffn_in['router_b'], 'L0_ffn_ln_g': _L0_ffn_in['ln_g'], 'L0_ffn_ln_b': _L0_ffn_in['ln_b'], 'L0_ffn_w1': _L0_ffn_in['w1'], 'L0_ffn_b1': _L0_ffn_in['b1'], 'L0_ffn_w2': _L0_ffn_in['w2'], 'L0_ffn_b2': _L0_ffn_in['b2'], 'L0_c': _L0_c, 'L0_wmod': _L0_wmod}
    _x0 = _d['L0_attn_x']
    _d['L0_attn_x'] = jax.random.normal(jax.random.fold_in(jax.random.key(seed), 1), (16, 512, 256), dtype=_x0.dtype)
    del _x0
    return _d

def reference(L0_attn_x, L0_attn_W_q, L0_attn_W_k, L0_attn_W_v, L0_attn_W_o, L0_ffn_rn_g, L0_ffn_rn_b, L0_ffn_router_w, L0_ffn_router_b, L0_ffn_ln_g, L0_ffn_ln_b, L0_ffn_w1, L0_ffn_b1, L0_ffn_w2, L0_ffn_b2, L0_c, L0_wmod):

    def _L0_attn_ref(x, W_q, W_k, W_v, W_o):
        import jax, jax.numpy as jnp
        import numpy as np
        from jax import lax

        def _phi(x):
            return jax.nn.elu(x) + 1.0
        B, T, D = x.shape
        H = W_q.shape[1]
        q = _phi(jnp.einsum('btd,dh->bth', x, W_q))
        k = _phi(jnp.einsum('btd,dh->bth', x, W_k))
        v = jnp.einsum('btd,dh->bth', x, W_v)
        qT = jnp.swapaxes(q, 0, 1)
        kT = jnp.swapaxes(k, 0, 1)
        vT = jnp.swapaxes(v, 0, 1)
        S0 = jnp.zeros((B, H, H), dtype=x.dtype)
        z0 = jnp.zeros((B, H), dtype=x.dtype)

        def step(carry, inp):
            S, z = carry
            q_t, k_t, v_t = inp
            S = S + k_t[:, :, None] * v_t[:, None, :]
            z = z + k_t
            o_t = jnp.einsum('bij,bj->bi', S, q_t)
            denom = jnp.maximum(jnp.sum(z * q_t, axis=-1, keepdims=True), 1e-06)
            return ((S, z), o_t / denom)
        (_, _), oT = lax.scan(step, (S0, z0), (qT, kT, vT))
        o = jnp.swapaxes(oT, 0, 1)
        return jnp.einsum('bth,hd->btd', o, W_o)

    def _L0_ffn_ref(hidden_states, rn_g, rn_b, router_w, router_b, ln_g, ln_b, w1, b1, w2, b2):
        import jax, jax.numpy as jnp
        import numpy as np
        B, L, D, I, E, K = (2, 512, 256, 1024, 8, 2)
        LN_EPS = 1e-05

        def _layernorm(x, g, b):
            m = jnp.mean(x, axis=-1, keepdims=True)
            v = jnp.mean(jnp.square(x - m), axis=-1, keepdims=True)
            return (x - m) * jax.lax.rsqrt(v + LN_EPS) * g + b
        normed = _layernorm(hidden_states, rn_g, rn_b)
        logits = (jnp.einsum('bld,ed->ble', normed, router_w) + router_b).astype(jnp.float32)
        top_w, top_idx = jax.lax.top_k(logits, K)
        top_w = jax.nn.softmax(top_w, axis=-1).astype(hidden_states.dtype)
        onehot = jax.nn.one_hot(top_idx, E, dtype=top_w.dtype)
        combine = jnp.einsum('blke,blk->ble', onehot, top_w)
        out = jnp.zeros_like(hidden_states)
        for e in range(E):
            h = _layernorm(hidden_states, ln_g[e], ln_b[e])
            h = jax.nn.gelu(jnp.einsum('bld,di->bli', h, w1[e]) + b1[e], approximate=False)
            h = jnp.einsum('bli,id->bld', h, w2[e]) + b2[e]
            out = out + combine[..., e:e + 1] * h
        return out
    x = L0_attn_x
    mod = (_silu(L0_c) @ L0_wmod).reshape(L0_c.shape[0], 6, 1, -1)
    sa, ca, ga, sb, cb, gb = (mod[:, 0], mod[:, 1], mod[:, 2], mod[:, 3], mod[:, 4], mod[:, 5])
    ga = (2 * (ga >= 0) - 1) * jnp.maximum(jnp.abs(ga), 0.25)
    gb = (2 * (gb >= 0) - 1) * jnp.maximum(jnp.abs(gb), 0.25)
    h = _layernorm(x, axis=-1) * (1 + ca) + sa
    x = x + ga * _L0_attn_ref(h, L0_attn_W_q, L0_attn_W_k, L0_attn_W_v, L0_attn_W_o)
    h = _layernorm(x, axis=-1) * (1 + cb) + sb
    x = x + gb * _L0_ffn_ref(h, L0_ffn_rn_g, L0_ffn_rn_b, L0_ffn_router_w, L0_ffn_router_b, L0_ffn_ln_g, L0_ffn_ln_b, L0_ffn_w1, L0_ffn_b1, L0_ffn_w2, L0_ffn_b2)
    return x

_drawn_inputs = setup_inputs


def setup_inputs(seed=0):
    import zlib

    import numpy as np

    out = dict(_drawn_inputs(seed))
    spreads = {'L0_ffn_rn_g': (1.0, 0.6),
     'L0_ffn_rn_b': (0.0, 0.8),
     'L0_ffn_router_b': (0.0, 0.622),
     'L0_ffn_ln_g': (1.0, 0.6),
     'L0_ffn_ln_b': (0.0, 0.8),
     'L0_ffn_b1': (0.0, 0.8),
     'L0_ffn_b2': (0.0, 0.445)}
    factors = {'L0_attn_W_q': 8.0,
     'L0_attn_W_k': 8.0,
     'L0_attn_W_v': 8.0,
     'L0_attn_W_o': 8.0,
     'L0_ffn_w1': 2.76}
    for name, (base, spread) in spreads.items():
        noise = np.random.default_rng([zlib.crc32(name.encode()), seed]).standard_normal(out[name].shape)
        drawn = base * np.exp(spread * noise) if base else spread * noise
        out[name] = jnp.asarray(drawn.astype(out[name].dtype))
    for name, factor in factors.items():
        out[name] = (out[name] * factor).astype(out[name].dtype)
    return out
```

```python
import concourse.bass as bass
from concourse import mybir
from contextlib import ExitStack


P = 128
NB, T, D = 16, 512, 256
H = 64
E, I = 8, 1024
NC, NK = T // P, D // P
NI = I // P
NTOK = NB * T
TOK = 384
TH = TOK // P
TILES = (2 * NTOK + E * (TOK - 1)) // TOK
CAP = NTOK + TOK
DUMMY = E * CAP
MAXT = -(-NTOK // TOK)
EPS = 1e-5
SA, CA, GA, SB, CB, GB = range(6)
VEC_B1, VEC_G, VEC_B, VEC_RG, VEC_RB = 0, E * NI, E * NI + 2 * E, E * NI + 4 * E, E * NI + 4 * E + 2
NVEC = VEC_RB + 2


def adaln_moe_kernel(nc, x_d, wq_d, wk_d, wv_d, wo_d, rng_d, rnb_d, rw_d, rb_d, lng_d, lnb_d,
                     w1_d, b1_d, w2_d, b2_d, c_d, wmod_d, mod_d, list_d, wsplit_d, b1f_d, y_d, out_d):
    f32, bf16, i32, u32 = mybir.dt.float32, mybir.dt.bfloat16, mybir.dt.int32, mybir.dt.uint32
    ALU, ACT, AX = mybir.AluOpType, mybir.ActivationFunctionType, mybir.AxisListType
    ds = bass.ds

    ctx = ExitStack()
    with ctx:
        def sb(name, shape, dt=f32):
            return ctx.enter_context(nc.sbuf_tensor(name, shape, dt))

        def sem(name):
            return ctx.enter_context(nc.semaphore(name))

        def sems(name, n=2):
            return [sem(f"{name}{i}") for i in range(n)]

        resid = sb("resid", [P, NB * NC, D])
        ident = sb("ident", [P, P])
        causal = sb("causal", [P, P])
        before = sb("before", [P, P], bf16)
        allone = sb("allone", [P, P], bf16)
        onesf = sb("onesf", [P, T])
        experts = sb("experts", [P, E])
        mhalf = sb("mhalf", [P, NC])
        wqk = sb("wqk", [P, NK, 2 * H])
        wv = sb("wv", [P, NK, H])
        wo = sb("wo", [H, D])
        wog = sb("wog", [H, 2, D])
        vrow = sb("vrow", [NVEC, P])
        vecs = sb("vecs", [P, NVEC])
        lngb = sb("lngb", [P, E, 4])
        rrow = sb("rrow", [E, D])
        rT = sb("rT", [P, NK, E])
        rTg = sb("rTg", [P, NK, E])
        rnbb = sb("rnbb", [P, NK, P])
        rbias = sb("rbias", [P, E])
        cin = sb("cin", [NB, D])
        cex = sb("cex", [NB, D])
        cT = sb("cT", [P, NK, NB])
        mod = sb("mod", [NB, 6 * D])
        modT = sb("modT", [P, NB, 4])
        modc = sb("modc", [P, 2, 4])
        gaB = sb("gaB", [H, 2, D])
        csB = sb("csB", [P, 2, 2 * D])
        st = sb("st", [P, NC, 6])
        mv1 = sb("mv1", [P, NC, 2]); ve1 = sb("ve1", [P, NC]); rs1 = sb("rs1", [P, NC]); nm1 = sb("nm1", [P, NC])
        mv2 = sb("mv2", [P, NC, 2]); ve2 = sb("ve2", [P, NC]); rs2 = sb("rs2", [P, NC]); nm2 = sb("nm2", [P, NC])
        mv3 = sb("mv3", [P, NC, 2]); ve3 = sb("ve3", [P, NC]); rs3 = sb("rs3", [P, NC]); nm3 = sb("nm3", [P, NC])
        rowbuf = sb("rowbuf", [P, 3 * NC * D])
        xc, xn2, h2 = (rowbuf[:, n * NC * D:(n + 1) * NC * D].rearrange("p (c d) -> p c d", c=NC) for n in range(3))
        gneg, gsgn = rowbuf[0:NB, 0:D], rowbuf[0:NB, D:2 * D]
        yt, xin = (rowbuf[:, n * 2 * TH * D:(n + 1) * 2 * TH * D].rearrange("p (r h d) -> p r h d", r=2, h=TH) for n in range(2))
        hT = sb("hT", [P, NK, T])
        ex = sb("ex", [P, T])
        qk = sb("qk", [P, 2, T])
        vT = sb("vT", [H, 2, T])
        ktok = sb("ktok", [P, 2, NC, H])
        zT = sb("zT", [H, T])
        qz = sb("qz", [H, T])
        PW = [T - a * P for a in range(NC)]
        PO = [a * T for a in range(NC)]
        pt = sb("pt", [P, NC * T])
        oT = sb("oT", [H, T])
        den = sb("den", [P, NC]); rden = sb("rden", [P, NC])
        nrm = sb("nrm", [P, 2, NC, D])
        nT = sb("nT", [P, NK, T])
        lg = sb("lg", [P, NC, E])
        mx = sb("mx", [P, NC, 8])
        ix = sb("ix", [P, NC, 8], u32)
        ef = sb("ef", [P, NC, 2])
        oh = sb("oh", [P, 2, NC, E])
        ohs = sb("ohs", [P, NC, E], bf16)
        dl = sb("dl", [P, NC]); dex = sb("dex", [P, NC]); d1 = sb("d1", [P, NC])
        rt = sb("rt", [P, NC * E + E])
        cnt = sb("cnt", [P, NC, E])
        pick = sb("pick", [P, 2, NC, E])
        base = sb("base", [P, E])
        slot = sb("slot", [P, 2, NC, 2], i32)
        w_all = sb("w_all", [P, NB * NC, 2])
        e_all = sb("e_all", [P, NB * NC, 2])
        s_all = sb("s_all", [P, NB * NC, 2])
        yrow = sb("yrow", [P, NB * NC, 2], i32)
        wbuf = sb("wbuf", [P, 2, 4 * NI * D], bf16)
        w1f = wbuf[:, 1, :].bitcast(f32)[:, 0:2048].rearrange("p (k i) -> p k i", k=NK)
        w2f = wbuf[:, 1, :].bitcast(f32)[:, 2048:4096]
        wmod = wbuf[:, 0, :].bitcast(f32)[:, 0:NK * 6 * D].rearrange("p (k n) -> p k n", k=NK)
        lge = sb("lge", [P, 4])
        b1f = sb("b1f", [P, E, NI])
        zero = sb("zero", [P, D])
        nh = sb("nh", [P, 2, NK, TOK], bf16)
        nl = sb("nl", [P, 2, NK, TOK], bf16)
        gf = sb("gf", [P, 2, TOK])
        gh = sb("gh", [P, 4, TOK], bf16)
        gl = sb("gl", [P, 4, TOK], bf16)
        b1t = sb("b1t", [P, 2, NI])
        b2t = sb("b2t", [P, 2, D])
        offs = sb("offs", [P, E]); count = sb("count", [P, E]); counti = sb("counti", [P, E], i32)
        steps = sb("steps", [P, E, MAXT]); need = sb("need", [P, E, MAXT])
        ntile = sb("ntile", [P, E]); tend = sb("tend", [P, E]); tstart = sb("tstart", [P, E])
        delta = sb("delta", [P, E])
        padrow = sb("padrow", [P, E], i32)
        tid = sb("tid", [1, TILES, E]); ge = sb("ge", [1, TILES, E]); gs = sb("gs", [1, TILES, E])
        tab_e = sb("tab_e", [1, TILES]); tab_r = sb("tab_r", [1, TILES]); tab_d = sb("tab_d", [1, TILES])
        table = sb("table", [1, 2, TILES], i32)
        rowf = sb("rowf", [P, NB * NC, 2]); rsel = sb("rsel", [P, NB * NC, 2])
        yidx = sb("yidx", [P, 2, NC, 2], i32)
        gbB = csB[:, :, 0:D]
        ya, yb, res = (wbuf[:, 0, :].bitcast(f32)[:, n * 4 * D:(n + 1) * 4 * D].rearrange("p (c d) -> p c d", c=4)
                       for n in range(3))
        ov = wbuf[:, 0, :].bitcast(f32)[:, 12 * D:14 * D].rearrange("p (c d) -> p c d", c=2)

        bank = [ctx.enter_context(nc.psum_tensor(f"bank{i}", [P, 512], f32)) for i in range(8)]
        TR, Q, V, S, O = bank[0:2], bank[2], bank[3], bank[4:7], bank[7]
        DEN = S[2][:, 384:388]
        LOG = S[2][:, 388:420]
        RANK = S[2][:, 420:452]
        TOT = S[2][:, 452:460]
        RT = S[2][:, 420:460]
        B1P = S[2][:, 460:468]
        ACC, MM = bank[2:5], bank[5:7]

        consts = sem("consts"); dconst = sem("dconst"); acon = sem("acon")
        got_c = sem("got_c"); got_wmod = sem("got_wmod"); got_w = sem("got_w"); got_vec = sem("got_vec")
        got_r = sem("got_r"); base_set = sem("base_set")
        c_exp = sem("c_exp"); c_step = sem("c_step"); cT_ps = sem("cT_ps"); cT_sb = sem("cT_sb")
        mod_ps = sem("mod_ps"); mod_step = sem("mod_step"); mod_out = sem("mod_out"); modT_ps = sem("modT_ps")
        vec_ps = sem("vec_ps"); set_step = sem("set_step"); rb_ps = sem("rb_ps"); setup_done = sem("setup_done")
        got_x = sems("got_x"); got_ga = sems("got_ga"); got_cs = sems("got_cs")
        st1 = sem("st1"); mv1_s = sem("mv1_s"); ve1_s = sem("ve1_s"); rs1_s = sem("rs1_s"); nm1_s = sem("nm1_s")
        st2 = sem("st2"); mv2_s = sem("mv2_s"); ve2_s = sem("ve2_s"); rs2_s = sem("rs2_s"); nm2_s = sem("nm2_s")
        st3 = sem("st3"); mv3_s = sem("mv3_s"); ve3_s = sem("ve3_s"); rs3_s = sem("rs3_s"); nm3_s = sem("nm3_s")
        xc_s = sem("xc_s"); xT_s = sem("xT_s"); modc_s = sem("modc_s"); hT_s = sem("hT_s")
        proj_s = sem("proj_s"); ex_s = sem("ex_s"); vT_s = sem("vT_s"); exm_s = sem("exm_s"); phi_s = sem("phi_s")
        ktr_s = sem("ktr_s"); ktok_s = sem("ktok_s"); scan_s = sem("scan_s"); qz_s = sem("qz_s")
        score_s = sem("score_s"); diag_s = sem("diag_s"); strip_s = sem("strip_s"); pv_s = sem("pv_s")
        oT_s = sem("oT_s"); small_s = sem("small_s"); small_read = sem("small_read"); dmax_s = sem("dmax_s"); rden_s = sem("rden_s")
        wog_s = sem("wog_s"); owo_s = sem("owo_s"); x2_s = sem("x2_s")
        xn2_s = sem("xn2_s"); h2m_s = sem("h2m_s"); h2_s = sem("h2_s"); nrm_s = sem("nrm_s")
        nTp_s = sem("nTp_s"); nT_s = sem("nT_s"); lg_s = sem("lg_s"); mx_s = sem("mx_s")
        ix_s = sem("ix_s"); ef_s = sem("ef_s"); oh_s = sem("oh_s"); ohs_s = sem("ohs_s"); dl_s = sem("dl_s")
        dex_s = sem("dex_s"); d1_s = sem("d1_s"); w0_s = sem("w0_s"); w1_s = sem("w1_s")
        rt_s = sem("rt_s"); cnt_s = sem("cnt_s"); pick_s = sem("pick_s"); slotf_s = sem("slotf_s")
        slot_s = sem("slot_s"); base_s = sem("base_s"); scat = sems("scat")
        got_we = sem("got_we"); lge_s = sem("lge_s"); head_s = sem("head_s"); rest_s = sem("rest_s")
        b1f_s = sem("b1f_s"); split_out = sem("split_out"); b1_out = sem("b1_out")
        tstep = sem("tstep"); tab_s = sem("tab_s"); pad_out = sem("pad_out"); zero_s = sem("zero_s")
        got_xin = sems("got_xin"); got_w1 = sems("got_w1"); got_w2 = sems("got_w2")
        got_b1 = sems("got_b1"); got_b2 = sems("got_b2")
        tr_s = sem("tr_s"); nh_s = sem("nh_s"); nl_s = sem("nl_s"); mm1_s = sem("mm1_s"); gf_s = sem("gf_s")
        gh_s = sem("gh_s"); gl_s = sem("gl_s"); mm2_s = sem("mm2_s"); yt_s = sem("yt_s"); y_out = sems("y_out")
        yidx_s = sem("yidx_s"); yrow_s = sem("yrow_s")
        got_gb = sems("got_gb"); got_ya = sems("got_ya", 4); got_yb = sems("got_yb", 4)
        ca_s = sem("ca_s"); cb_s = sem("cb_s"); cc_s = sem("cc_s"); res_s = sem("res_s"); o_out = sems("o_out", 4)
        held = {n: sem(f"held_{n}") for n in ("act", "dve", "pe", "pool")}

        def wait_past(eng, semaphore, value):
            if not isinstance(value, int) or value > 0:
                eng.wait_ge(semaphore, value)

        def hold(eng, name):
            eng.sem_inc(held[name], 1)

        def pipeline(eng, step):
            for i in range(4):
                step(i, i // 2, i % 2, True, i >= 1, i >= 2, i >= 3)
            with eng.Fori(2, NB // 2 - 1) as j:
                for r in range(2):
                    step(2 * j + r, j, r, True, True, True, True)
            for i in range(NB - 2, NB + 3):
                step(i, i // 2, i % 2, i < NB, i - 1 < NB, i - 2 < NB, True)

        block = ctx.enter_context(nc.Block())

        x_v = x_d.rearrange("b (c p) d -> b p c d", p=P)
        out_v = out_d.rearrange("b (c p) d -> (b c) p d", p=P)
        w1_v = w1_d.rearrange("e (k p) i -> e p k i", p=P)
        w2_v = w2_d.rearrange("e (c p) d -> e p c d", p=P)

        @block.sync
        def _(sp):
            sp.dma_start(cin[:, :], c_d).then_inc(got_c, 16)
            sp.dma_start(wmod, wmod_d.rearrange("(k p) n -> p k n", p=P)).then_inc(got_wmod, 16)
            for b in range(2):
                sp.dma_start(resid[:, b * NC:(b + 1) * NC, :], x_v[b]).then_inc(got_x[b], 16)
            sp.dma_start(wqk[:, :, 0:H], wq_d.rearrange("(k p) h -> p k h", p=P)).then_inc(got_w, 16)
            sp.dma_start(wqk[:, :, H:2 * H], wk_d.rearrange("(k p) h -> p k h", p=P)).then_inc(got_w, 16)
            sp.dma_start(wv[:, :, :], wv_d.rearrange("(k p) h -> p k h", p=P)).then_inc(got_w, 16)
            sp.dma_start(wo[:, :], wo_d).then_inc(got_w, 16)
            sp.dma_start(vrow[VEC_B1:VEC_G, :], b1_d.rearrange("e (i p) -> (e i) p", p=P)).then_inc(got_vec, 16)
            sp.dma_start(vrow[VEC_G:VEC_B, :], lng_d.rearrange("e (k p) -> (e k) p", p=P)).then_inc(got_vec, 16)
            sp.dma_start(vrow[VEC_B:VEC_RG, :], lnb_d.rearrange("e (k p) -> (e k) p", p=P)).then_inc(got_vec, 16)
            sp.dma_start(vrow[VEC_RG:VEC_RB, :], rng_d.rearrange("(k p) -> k p", p=P)).then_inc(got_vec, 16)
            sp.dma_start(vrow[VEC_RB:NVEC, :], rnb_d.rearrange("(k p) -> k p", p=P)).then_inc(got_vec, 16)
            sp.dma_start(rrow[:, :], rw_d).then_inc(got_r, 16)
            sp.dma_start(rbias[:, :], rb_d.partition_broadcast(P)).then_inc(got_r, 16)
            sp.wait_ge(mod_step, 8)
            sp.dma_start(mod_d, mod[:, :]).then_inc(mod_out, 16)
            sp.wait_ge(zero_s, 1)
            sp.dma_start(list_d[DUMMY:DUMMY + TOK, :].rearrange("(p r) d -> p r d", r=TH),
                         zero[:, :].unsqueeze(1).to_broadcast([P, TH, D])).then_inc(pad_out, 16)
            sp.wait_ge(mod_out, 16)
            sp.wait_ge(mod_ps, 1)

            def step(i, half, r, project, attend, route, place):
                if project:
                    if isinstance(i, int) and i == 0:
                        sp.dma_start(w1f, w1_v[0]).then_inc(got_we, 16)
                        sp.dma_start(w2f.rearrange("p (c d) -> p c d", c=NI), w2_v[0]).then_inc(got_we, 16)
                    wait_past(sp, wog_s, i - 1)
                    sp.dma_start(gaB[:, r, :], mod_d[ds(i, 1), GA * D:(GA + 1) * D].partition_broadcast(H)
                                 if not isinstance(i, int) else
                                 mod_d[i, GA * D:(GA + 1) * D].partition_broadcast(H)).then_inc(got_ga[r], 16)
                    wait_past(sp, h2_s, i - 1)
                    sp.dma_start(csB[:, r, :], mod_d[ds(i, 1), SB * D:(CB + 1) * D].partition_broadcast(P)
                                 if not isinstance(i, int) else
                                 mod_d[i, SB * D:(CB + 1) * D].partition_broadcast(P)).then_inc(got_cs[r], 16)
                    last = not isinstance(i, int) and r == 1
                    load_x(i, half, r)
                    if r == 1:
                        sp.wait_ge(rest_s, 3 * half + 3)
                        sp.wait_ge(head_s, 3 * half + 3)
                        sp.dma_start(wsplit_d[half] if isinstance(half, int) else wsplit_d[ds(half, 1)],
                                     wbuf[:, 0, :]).then_inc(split_out, 16)
                        sp.wait_ge(b1f_s, half + 1)
                        load_experts(half)

            def load_x(i, half, r):
                if isinstance(i, int):
                    if i + 2 < NB:
                        sp.wait_ge(got_x[r], 16 * (half + 1))
                        sp.dma_start(resid[:, (i + 2) * NC:(i + 3) * NC, :], x_v[i + 2]).then_inc(got_x[r], 16)
                else:
                    sp.wait_ge(got_x[r], 16 * half + 16)
                    sp.dma_start(resid[:, ds((i + 2) * NC, NC), :], x_v[ds(i + 2, 1)]).then_inc(got_x[r], 16)

            def load_experts(half):
                if isinstance(half, int):
                    if half + 1 < E:
                        sp.dma_start(w1f, w1_v[half + 1]).then_inc(got_we, 16)
                        sp.dma_start(w2f.rearrange("p (c d) -> p c d", c=NI), w2_v[half + 1]).then_inc(got_we, 16)
                else:
                    sp.dma_start(w1f, w1_v[ds(half + 1, 1)]).then_inc(got_we, 16)
                    sp.dma_start(w2f.rearrange("p (c d) -> p c d", c=NI), w2_v[ds(half + 1, 1)]).then_inc(got_we, 16)

            for i in range(2):
                step(i, 0, i, True, True, True, True)
            with nc.sync.Fori(1, NB // 2 - 1) as j:
                for r in range(2):
                    step(2 * j + r, j, r, True, True, True, True)
            for i in range(NB - 2, NB):
                step(i, NB // 2 - 1, i % 2, True, True, True, True)
            sp.wait_ge(b1f_s, E)
            sp.dma_start(b1f_d.rearrange("e p i -> p e i"), b1f[:, :, :]).then_inc(b1_out, 16)

            sp.wait_ge(tab_s, 1)
            for e in range(E):
                row = nc.sync.value_load(padrow[0:1, e:e + 1], min_val=0, max_val=DUMMY)
                sp.dma_start(list_d[ds(row, TOK), :].rearrange("(p r) d -> p r d", r=TH),
                         zero[:, :].unsqueeze(1).to_broadcast([P, TH, D])).then_inc(pad_out, 16)
            for r in range(2):
                sp.wait_ge(scat[r], 16 * 2 * NC * NB // 2)
            sp.wait_ge(pad_out, 16 * (E + 1))
            sp.wait_ge(split_out, 16 * E)
            sp.wait_ge(b1_out, 16)
            sp.wait_ge(tab_s, 2)

            def tile_loads(j, half, r):
                e = nc.sync.value_load(table[0:1, 0, ds(j, 1)], min_val=0, max_val=E - 1)
                row = nc.sync.value_load(table[0:1, 1, ds(j, 1)], min_val=0, max_val=DUMMY)
                wait_past(sp, tr_s, j - 1)
                sp.dma_start(xin[:, r, :, :].rearrange("p r d -> p (r d)"),
                             list_d[ds(row, TOK), :].rearrange("(p r) d -> p (r d)", r=TH)).then_inc(got_xin[r], 16)
                wait_past(sp, mm1_s, NI * (j - 1))
                sp.dma_start(wbuf[:, r, 0:4096], wsplit_d[ds(e, 1), :, 0:4096]).then_inc(got_w1[r], 16)
                wait_past(sp, gf_s, NI * (j - 1))
                sp.dma_start(b1t[:, r, :], b1f_d[ds(e, 1)]).then_inc(got_b1[r], 16)
                wait_past(sp, mm2_s, NI * (j - 1))
                sp.dma_start(wbuf[:, r, 4096:8192], wsplit_d[ds(e, 1), :, 4096:8192]).then_inc(got_w2[r], 16)
                wait_past(sp, yt_s, j - 1)
                sp.dma_start(b2t[:, r, :], b2_d[ds(e, 1), :].partition_broadcast(P)).then_inc(got_b2[r], 16)

            for j in range(2):
                tile_loads(j, 0, j)
            with nc.sync.Fori(1, TILES // 2) as h:
                for r in range(2):
                    tile_loads(2 * h + r, h, r)

            def gb_load(b, half, r):
                wait_past(sp, cc_s, NC * (b - 1))
                sp.dma_start(gbB[:, r, :], mod_d[ds(b, 1), GB * D:(GB + 1) * D].partition_broadcast(P)).then_inc(got_gb[r], 16)

            def store(b):
                for c in range(NC):
                    sp.wait_ge(res_s, NC * b + c + 1)
                    sp.dma_start(out_v[ds(NC * b + c, 1)], res[:, c, :]).then_inc(o_out[c], 16)

            for b in range(2):
                gb_load(b, 0, b)
            with nc.sync.Fori(0, NB // 2 - 1) as h:
                for r in range(2):
                    store(2 * h + r)
                    gb_load(2 * h + r + 2, h + 1, r)
            for b in range(NB - 2, NB):
                store(b)
            for c in range(NC):
                sp.wait_ge(o_out[c], 16 * NB)

        @block.gpsimd
        def _(pool):
            g = nc.gpsimd
            g.memset(ident[:, :], 0.0).then_inc(consts, 1)
            g.memset(causal[:, :], 1.0).then_inc(consts, 1)
            g.memset(before[:, :], 1.0).then_inc(consts, 1)
            g.memset(allone[:, :], 1.0).then_inc(consts, 1)
            g.memset(onesf[:, :], 1.0).then_inc(consts, 1)
            g.memset(mhalf[:, :], -0.5).then_inc(consts, 1)
            g.iota(experts[:, :], pattern=[[1, E]], base=0, channel_multiplier=0,
                   allow_small_or_imprecise_dtypes=True).then_inc(consts, 1)
            g.iota(offs[:, :], pattern=[[CAP, E]], base=0, channel_multiplier=0,
                   allow_small_or_imprecise_dtypes=True).then_inc(consts, 1)
            g.iota(steps[:, :, :], pattern=[[0, E], [TOK, MAXT]], base=0, channel_multiplier=0,
                   allow_small_or_imprecise_dtypes=True).then_inc(consts, 1)
            g.iota(tid[:, :, :], pattern=[[1, TILES], [0, E]], base=0, channel_multiplier=0,
                   allow_small_or_imprecise_dtypes=True).then_inc(consts, 1)
            pool.wait_ge(consts, 10)
            g.affine_select(out=ident[:, :], in_=ident[:, :], compare_op=ALU.not_equal, fill=1.0,
                            base=0, pattern=[[-1, P]], channel_multiplier=1).then_inc(consts, 1)
            g.affine_select(out=causal[:, :], in_=causal[:, :], compare_op=ALU.is_ge, fill=0.0,
                            base=0, pattern=[[1, P]], channel_multiplier=-1).then_inc(consts, 1)
            g.affine_select(out=before[:, :], in_=before[:, :], compare_op=ALU.is_ge, fill=0.0,
                            base=-1, pattern=[[1, P]], channel_multiplier=-1).then_inc(consts, 1)

            def inverse_root(ve, ve_s, rs, rs_s, nm_s, b):
                pool.wait_ge(ve_s, b + 1)
                wait_past(pool, nm_s, b)
                g.tensor_tensor(rs[:, :], ve[:, :], mhalf[:, :], ALU.pow).then_inc(rs_s, 1)

            inverse_root(ve1, ve1_s, rs1, rs1_s, xc_s, 0)

            def step(i, half, r, project, attend, route, place):
                if attend:
                    b, q = i - 1, 1 - r
                    pool.wait_ge(got_ga[q], 16 * (half if q == 1 else half + 1))
                    wait_past(pool, owo_s, b - 1)
                    g.tensor_tensor(wog[:, q, :], wo[:, :], gaB[:, q, :], ALU.mult).then_inc(wog_s, 1)
                if route:
                    b, q = i - 2, r
                    pool.wait_ge(got_cs[q], 16 * half)
                    pool.wait_ge(xn2_s, b + 1)
                    wait_past(pool, nrm_s, b)
                    g.tensor_tensor(h2[:, :, :], xn2[:, :, :],
                                    csB[:, q, D:2 * D].unsqueeze(1).to_broadcast([P, NC, D]), ALU.mult).then_inc(h2m_s, 1)
                    pool.wait_ge(h2m_s, b + 1)
                    g.tensor_tensor(h2[:, :, :], h2[:, :, :],
                                    csB[:, q, 0:D].unsqueeze(1).to_broadcast([P, NC, D]), ALU.add).then_inc(h2_s, 1)
                    inverse_root(ve3, ve3_s, rs3, rs3_s, nrm_s, b)
                if project:
                    b = i
                    pool.wait_ge(scan_s, b + 1)
                    wait_past(pool, small_s, b + 1)
                    g.tensor_tensor(qz[:, :], qk[0:H, r, :], zT[:, :], ALU.mult).then_inc(qz_s, 1)
                if place:
                    b, q = i - 3, 1 - r
                    pool.wait_ge(slot_s, b + 1)
                    hold(pool, "pool")
                    for c in range(NC):
                        for t in range(2):
                            g.indirect_dma_start(list_d, bass.IndirectOffsetOnAxis(ap=slot[:, q, c, t:t + 1], axis=0),
                                                 nrm[:, q, c, :], None).then_inc(scat[q], 16)
                if attend:
                    inverse_root(ve2, ve2_s, rs2, rs2_s, xn2_s, i - 1)
                if project and not (isinstance(i, int) and i == NB - 1):
                    ahead(i)

            def ahead(i):
                inverse_root(ve1, ve1_s, rs1, rs1_s, xc_s, i + 1)

            pipeline(g, step)

            def y_store(j, half, r):
                pool.wait_ge(yt_s, j + 1)
                hold(pool, "pool")
                g.dma_start(y_d[ds(j * TOK, TOK), :].rearrange("(p r) d -> p (r d)", r=TH),
                            yt[:, r, :, :].rearrange("p r d -> p (r d)")).then_inc(y_out[r], 16)

            with g.Fori(0, TILES // 2) as h:
                for r in range(2):
                    y_store(2 * h + r, h, r)
            pool.wait_ge(yrow_s, 1)
            for r in range(2):
                pool.wait_ge(y_out[r], 16 * TILES // 2)

            def gather(b, half, r):
                if not isinstance(b, int) or b >= 2:
                    for c in range(NC):
                        pool.wait_ge(got_ya[c], 16 * (b - 1))
                        pool.wait_ge(got_yb[c], 16 * (b - 1))
                hold(pool, "pool")
                g.tensor_copy(yidx[:, r, :, :], yrow[:, ds(NC * b, NC), :]).then_inc(yidx_s, 1)
                pool.wait_ge(yidx_s, b + 1)
                for c in range(NC):
                    wait_past(pool, cb_s, NC * (b - 1) + c + 1)
                    hold(pool, "pool")
                    g.indirect_dma_start(ya[:, c, :], None, y_d,
                                         bass.IndirectOffsetOnAxis(ap=yidx[:, r, c, 0:1], axis=0)).then_inc(got_ya[c], 16)
                    g.indirect_dma_start(yb[:, c, :], None, y_d,
                                         bass.IndirectOffsetOnAxis(ap=yidx[:, r, c, 1:2], axis=0)).then_inc(got_yb[c], 16)

            for b in range(2):
                gather(b, 0, b)
            with g.Fori(1, NB // 2) as h:
                for r in range(2):
                    gather(2 * h + r, h, r)

        @block.scalar
        def _(act):
            a = nc.scalar
            act.wait_ge(got_c, 16)
            a.activation(cex[:, :], cin[:, :], ACT.Exp, scale=-1.0).then_inc(c_exp, 1)
            act.wait_ge(setup_done, 1)

            def normalise(out, src, rs, nm, nm_s, done, b, free, regs):
                act.wait_ge(nm_s, b + 1)
                for s, v in free:
                    wait_past(act, s, v)
                hold(act, "act")
                for c in range(NC):
                    last = a.activation(out(c), src(c), ACT.Identity, bias=nm[:, c:c + 1], scale=rs[:, c:c + 1])
                last.then_inc(done, 1)

            def step(i, half, r, project, attend, route, place):
                if project:
                    act.wait_ge(got_x[r], 16 * half + 16)
                    normalise(lambda c: xc[:, c, :], lambda c: resid[:, ds(i * NC + c, 1), :] if not isinstance(i, int) else resid[:, i * NC + c, :],
                              rs1, nm1, nm1_s, xc_s, i, [(xT_s, i)], True)
                if route:
                    b = i - 2
                    normalise(lambda c: xn2[:, c, :], lambda c: resid[:, ds(b * NC + c, 1), :] if not isinstance(i, int) else resid[:, b * NC + c, :],
                              rs2, nm2, nm2_s, xn2_s, b, [(h2m_s, b)], True)
                if project:
                    act.wait_ge(xT_s, i + 1)
                    act.wait_ge(modc_s, i + 1)
                    wait_past(act, proj_s, i)
                    hold(act, "act")
                    for k in range(NK):
                        last = a.activation(hT[:, k, :], TR[k][:, :], ACT.Identity,
                                            bias=modc[:, r, 2 + k:3 + k], scale=modc[:, r, k:k + 1])
                    last.then_inc(hT_s, 1)
                if attend:
                    b = i - 1
                    act.wait_ge(score_s, b + 1)
                    wait_past(act, pv_s, b)
                    for s in range(NC):
                        last = a.activation(pt[:, PO[s]:PO[s] + PW[s]],
                                            S[2][:, 256:384] if s == 3 else S[s][:, 0:PW[s]], ACT.Copy)
                    last.then_inc(strip_s, 1)
                if route:
                    b = i - 2
                    wait_past(act, nTp_s, b - 1)
                    if not isinstance(i, int) or b >= 2:
                        act.wait_ge(scat[r], 16 * 2 * NC * (half - 1))
                    normalise(lambda c: nrm[:, r, c, :], lambda c: h2[:, c, :], rs3, nm3, nm3_s, nrm_s, b, [], False)
                if project:
                    act.wait_ge(proj_s, i + 1)
                    wait_past(act, phi_s, i)
                    a.activation(ex[:, :], Q[:, :], ACT.Exp).then_inc(ex_s, 1)
                    wait_past(act, score_s, i - 1)
                    a.activation(vT[:, r, :], V[0:H, :], ACT.Copy).then_inc(vT_s, 1)
                if attend:
                    b = i - 1
                    act.wait_ge(pv_s, b + 1)
                    wait_past(act, owo_s, b)
                    a.activation(oT[:, :], O[0:H, :], ACT.Copy).then_inc(oT_s, 1)
                if route:
                    b = i - 2
                    act.wait_ge(nTp_s, b + 1)
                    wait_past(act, small_s, b + 2)
                    for k in range(NK):
                        last = a.activation(nT[:, k, :], TR[k][:, :], ACT.Copy)
                    last.then_inc(nT_s, 1)
                if project:
                    act.wait_ge(ktr_s, i + 1)
                    wait_past(act, pv_s, i - 1)
                    a.activation(ktok[:, r, :, :].rearrange("p c h -> p (c h)"), V[:, 0:NC * H], ACT.Copy).then_inc(ktok_s, 1)
                if route:
                    b = i - 2
                    act.wait_ge(dl_s, b + 1)
                    a.activation(dex[:, :], dl[:, :], ACT.Exp).then_inc(dex_s, 1)
                if project and r == 0:
                    act.wait_ge(got_we, 32 * half + 32)
                    act.wait_ge(lge_s, half + 1)
                    wait_past(act, split_out, 16 * half)
                    hold(act, "act")
                    for k in range(NK):
                        a.activation(wbuf[:, 0, k * 1024:(k + 1) * 1024], w1f[:, k, :], ACT.Copy,
                                     scale=lge[:, k:k + 1]).then_inc(head_s, 1)
                    a.activation(wbuf[:, 0, 4096:6144], w2f, ACT.Copy).then_inc(head_s, 1)

            pipeline(a, step)

            def gelu(j, half, r):
                act.wait_ge(got_b1[r], 16 * half + 16)
                for c in range(NI):
                    act.wait_ge(mm1_s, NI * j + c + 1)
                    wait_past(act, gl_s, NI * j + c - 1)
                    a.activation(gf[:, c % 2, :], MM[c % 2][:, 0:TOK], ACT.Gelu, bias=b1t[:, r, c:c + 1]).then_inc(gf_s, 1)

            for j in range(2):
                gelu(j, 0, j)
            with a.Fori(1, TILES // 2) as h:
                for r in range(2):
                    gelu(2 * h + r, h, r)

        @block.vector
        def _(dve):
            v = nc.vector
            setc = [0]

            def chain(ins, s=None):
                setc[0] += 1
                ins.then_inc(set_step, 1)
                dve.wait_ge(set_step, setc[0])

            v.memset(zero[:, :], 0.0).then_inc(zero_s, 1)
            dve.wait_ge(c_exp, 1)
            chain(v.tensor_scalar_add(cex[:, :], cex[:, :], 1.0))
            chain(v.reciprocal(cex[:, :], cex[:, :]))
            v.tensor_tensor(cin[:, :], cin[:, :], cex[:, :], ALU.mult).then_inc(c_step, 1)
            dve.wait_ge(cT_ps, 1)
            v.tensor_copy(cT[:, :, :], Q[:, 0:NK * NB].rearrange("p (k b) -> p k b", k=NK)).then_inc(cT_sb, 1)
            dve.wait_ge(mod_ps, 1)
            for s in range(3):
                v.tensor_copy(mod[:, s * 512:(s + 1) * 512], S[s][0:NB, :]).then_inc(mod_step, 1)
            dve.wait_ge(mod_step, 3)
            v.tensor_scalar_add(mod[:, CA * D:(CA + 1) * D], mod[:, CA * D:(CA + 1) * D], 1.0).then_inc(mod_step, 1)
            v.tensor_scalar_add(mod[:, CB * D:(CB + 1) * D], mod[:, CB * D:(CB + 1) * D], 1.0).then_inc(mod_step, 1)
            for n, sel in enumerate((GA, GB)):
                gg = mod[:, sel * D:(sel + 1) * D]
                chain(v.tensor_scalar(gneg[:, :], gg, -1.0, None, ALU.mult))
                chain(v.tensor_tensor(gneg[:, :], gneg[:, :], gg, ALU.max))
                chain(v.tensor_scalar(gneg[:, :], gneg[:, :], 0.25, None, ALU.max))
                chain(v.tensor_scalar(gsgn[:, :], gg, 0.0, 2.0, ALU.is_ge, ALU.mult))
                chain(v.scalar_tensor_tensor(gg, gsgn[:, :], -1.0, gneg[:, :], ALU.add, ALU.mult))
            chain(v.tensor_copy(gneg[:, 0:1], gsgn[:, 0:1]))
            v.tensor_copy(gsgn[:, 1:2], gneg[:, 0:1]).then_inc(mod_step, 3)
            dve.wait_ge(modT_ps, 1)
            v.tensor_copy(modT[:, :, :].rearrange("p b s -> p s b"),
                          Q[:, 64:64 + 4 * NB].rearrange("p (s b) -> p s b", b=NB)).then_inc(set_step, 1)
            setc[0] += 1
            dve.wait_ge(vec_ps, 1)
            chain(v.tensor_copy(vecs[:, :], V[:, 0:NVEC]))
            chain(v.tensor_copy(rT[:, :, :], V[:, 128:128 + NK * E].rearrange("p (k e) -> p k e", k=NK)))
            chain(v.tensor_copy(lngb[:, :, 0:2], vecs[:, VEC_G:VEC_B].rearrange("p (e k) -> p e k", k=NK)))
            chain(v.tensor_copy(lngb[:, :, 2:4], vecs[:, VEC_B:VEC_RG].rearrange("p (e k) -> p e k", k=NK)))
            dve.wait_ge(consts, 13)
            for k in range(NK):
                chain(v.tensor_scalar(rTg[:, k, :], rT[:, k, :], vecs[:, VEC_RG + k:VEC_RG + k + 1], None, ALU.mult))
                chain(v.tensor_scalar(rnbb[:, k, :], onesf[:, 0:P], vecs[:, VEC_RB + k:VEC_RB + k + 1], None, ALU.mult))
            chain(v.tensor_copy(base[:, :], offs[:, :]))
            v.tensor_copy(ef[:, 0, 0:1], base[:, 0:1]).then_inc(base_set, 1)
            dve.wait_ge(rb_ps, 1)
            dve.wait_ge(got_r, 32)
            dve.wait_ge(base_set, 1)
            v.tensor_tensor(rbias[:, :], rbias[:, :], V[:, 256:256 + E], ALU.add).then_inc(setup_done, 1)
            dve.wait_ge(setup_done, 1)

            def stats(src, mv, ve, rs, nm, st_s, mv_s, ve_s, rs_s, nm_s, used, b, first):
                for c in range(NC):
                    last = v.bn_stats(st[:, c, :], src(c))
                last.then_inc(st_s, 1)
                dve.wait_ge(st_s, b + 1)
                wait_past(dve, used, b)
                hold(dve, "dve")
                for c in range(NC):
                    last = v.bn_aggr(mv[:, c, :], st[:, c, :])
                last.then_inc(mv_s, 1)
                dve.wait_ge(mv_s, b + 1)
                v.tensor_scalar(ve[:, :], mv[:, :, 1], EPS, None, ALU.add).then_inc(ve_s, 1)

            def neg_mean(mv, rs, nm, rs_s, nm_s, b):
                dve.wait_ge(rs_s, b + 1)
                v.scalar_tensor_tensor(nm[:, :], mv[:, :, 0], -1.0, rs[:, :], ALU.mult, ALU.mult).then_inc(nm_s, 1)

            def rows(b):
                return lambda c: resid[:, b * NC + c, :] if isinstance(b, int) else resid[:, ds(b * NC + c, 1), :]

            def stats1(b, half, r):
                dve.wait_ge(got_x[r], 16 * half + 16)
                wait_past(dve, mv3_s, b - 3)
                hold(dve, "dve")
                stats(rows(b), mv1, ve1, rs1, nm1, st1, mv1_s, ve1_s, rs1_s, nm1_s, xc_s, b, False)

            v.tensor_copy(lge[:, :], lngb[:, 0, :]).then_inc(lge_s, 1)
            stats1(0, 0, 0)
            neg_mean(mv1, rs1, nm1, rs1_s, nm1_s, 0)

            def step(i, half, r, project, attend, route, place):
                if project:
                    wait_past(dve, hT_s, i - 1)
                    hold(dve, "dve")
                    v.tensor_copy(modc[:, r, :], modT[:, i, :] if isinstance(i, int) else modT[:, ds(i, 1), :]).then_inc(modc_s, 1)
                if route:
                    b = i - 2
                    dve.wait_ge(h2_s, b + 1)
                    hold(dve, "dve")
                    stats(lambda c: h2[:, c, :], mv3, ve3, rs3, nm3, st3, mv3_s, ve3_s, rs3_s, nm3_s, nrm_s, b, False)
                if attend:
                    b, q = i - 1, 1 - r
                    dve.wait_ge(strip_s, b + 1)
                    diag = pt[:, :].rearrange("p (a t) -> p a t", a=NC)[:, :, 0:P]
                    v.tensor_tensor(diag, diag, causal[:, :].unsqueeze(1).to_broadcast([P, NC, P]), ALU.mult).then_inc(diag_s, 1)
                if route:
                    neg_mean(mv3, rs3, nm3, rs3_s, nm3_s, i - 2)
                if project:
                    dve.wait_ge(ex_s, i + 1)
                    v.tensor_scalar(ex[:, :], ex[:, :], 1.0, None, ALU.min).then_inc(exm_s, 1)
                    dve.wait_ge(exm_s, i + 1)
                    wait_past(dve, score_s, i - 1)
                    wait_past(dve, ktr_s, i - 1)
                    wait_past(dve, qz_s, i - 1)
                    v.scalar_tensor_tensor(qk[:, r, :], Q[:, :], 1.0, ex[:, :], ALU.add, ALU.max).then_inc(phi_s, 1)
                if project:
                    dve.wait_ge(phi_s, i + 1)
                    wait_past(dve, qz_s, i)
                    v.tensor_tensor_scan(zT[:, :], onesf[H:2 * H, :], qk[H:2 * H, r, :], 0.0, ALU.mult, ALU.add).then_inc(scan_s, 1)
                dve.wait_ge(small_s, i + 1)
                if place:
                    wait_past(dve, cnt_s, i - 3)
                    hold(dve, "dve")
                    last = v.tensor_copy(rt[:, :], RT)
                    last.then_inc(rt_s, 1)
                if route:
                    wait_past(dve, mx_s, i - 2)
                    last = v.tensor_tensor(lg[:, :, :], LOG.rearrange("p (c e) -> p c e", c=NC),
                                           rbias[:, :].unsqueeze(1).to_broadcast([P, NC, E]), ALU.add)
                    last.then_inc(lg_s, 1)
                if attend:
                    last = v.tensor_scalar(den[:, :], DEN, 1e-6, None, ALU.max)
                    last.then_inc(dmax_s, 1)
                if project and r == 0:
                    src = vecs[:, VEC_B1:VEC_G].rearrange("p (e i) -> p e i", e=E)
                    if isinstance(half, int):
                        last = v.tensor_tensor(b1f[:, half, :], src[:, half, :], B1P, ALU.add)
                    else:
                        last = v.tensor_tensor(b1f[:, ds(half, 1), :], src[:, ds(half, 1), :], B1P.unsqueeze(1), ALU.add)
                    last.then_inc(b1f_s, 1)
                if place:
                    dve.wait_ge(rt_s, i - 2)
                if route:
                    dve.wait_ge(lg_s, i - 1)
                if attend:
                    dve.wait_ge(dmax_s, i)
                if project and r == 0:
                    dve.wait_ge(b1f_s, half + 1)
                dve.sem_inc(small_read, 1)
                if attend:
                    b = i - 1
                    wait_past(dve, x2_s, b)
                    v.reciprocal(rden[:, :], den[:, :]).then_inc(rden_s, 1)
                if place:
                    slots(i - 3, half, 1 - r)
                if project and r == 1:
                    rests(half)
                    if not (isinstance(i, int) and i == NB - 1):
                        dve.wait_ge(rest_s, 3 * half + 3)
                        hold(dve, "dve")
                        v.tensor_copy(lge[:, :], lngb[:, half + 1, :] if isinstance(half, int) else lngb[:, ds(half + 1, 1), :]).then_inc(lge_s, 1)
                if route:
                    choose(i - 2)
                if attend:
                    b = i - 1
                    dve.wait_ge(owo_s, b + 1)
                    dve.wait_ge(rden_s, b + 1)
                    wait_past(dve, xc_s, b + 1)
                    for c in range(NC):
                        last = v.scalar_tensor_tensor(rows(b)(c), S[c // 2][:, (c % 2) * D:(c % 2 + 1) * D],
                                                      rden[:, c:c + 1], rows(b)(c), ALU.mult, ALU.add)
                    last.then_inc(x2_s, 1)
                    dve.wait_ge(x2_s, b + 1)
                    hold(dve, "dve")
                    stats(rows(b), mv2, ve2, rs2, nm2, st2, mv2_s, ve2_s, rs2_s, nm2_s, xn2_s, b, False)
                if project and not (isinstance(i, int) and i == NB - 1):
                    stats1_ahead(i, half, r)
                if attend:
                    neg_mean(mv2, rs2, nm2, rs2_s, nm2_s, i - 1)
                if project and not (isinstance(i, int) and i == NB - 1):
                    neg_mean(mv1, rs1, nm1, rs1_s, nm1_s, i + 1)

            def stats1_ahead(i, half, r):
                stats1(i + 1, half + r, 1 - r)

            def rests(e):
                dve.wait_ge(head_s, 3 * e + 3)
                wait_past(dve, split_out, 16 * e)
                for k in range(NK):
                    v.scalar_tensor_tensor(wbuf[:, 0, 2048 + k * 1024:2048 + (k + 1) * 1024], w1f[:, k, :], lge[:, k:k + 1],
                                           wbuf[:, 0, k * 1024:(k + 1) * 1024], ALU.mult, ALU.subtract).then_inc(rest_s, 1)
                v.tensor_tensor(wbuf[:, 0, 6144:8192], w2f, wbuf[:, 0, 4096:6144], ALU.subtract).then_inc(rest_s, 1)

            def cols(t, b):
                return t[:, b * NC:(b + 1) * NC, :] if isinstance(b, int) else t[:, ds(b * NC, NC), :]

            def choose(b):
                wait_past(dve, dex_s, b)
                hold(dve, "dve")
                for c in range(NC):
                    last = v.max(mx[:, c, :], lg[:, c, :])
                last.then_inc(mx_s, 1)
                dve.wait_ge(mx_s, b + 1)
                v.tensor_tensor(dl[:, :], mx[:, :, 1], mx[:, :, 0], ALU.subtract).then_inc(dl_s, 1)
                for c in range(NC):
                    last = v.max_index(ix[:, c, :], mx[:, c, :], lg[:, c, :])
                last.then_inc(ix_s, 1)
                dve.wait_ge(ix_s, b + 1)
                v.tensor_copy(ef[:, :, :], ix[:, :, 0:2]).then_inc(ef_s, 1)
                dve.wait_ge(ef_s, b + 1)
                wait_past(dve, cnt_s, b)
                for t in range(2):
                    last = v.tensor_tensor(oh[:, t, :, :], experts[:, :].unsqueeze(1).to_broadcast([P, NC, E]),
                                           ef[:, :, t:t + 1].to_broadcast([P, NC, E]), ALU.is_equal)
                last.then_inc(oh_s, 1)
                dve.wait_ge(oh_s, b + 1)
                v.tensor_tensor(ohs[:, :, :], oh[:, 0, :, :], oh[:, 1, :, :], ALU.add).then_inc(ohs_s, 1)
                v.tensor_copy(cols(e_all, b), ef[:, :, :])
                dve.wait_ge(dex_s, b + 1)
                v.tensor_scalar(d1[:, :], dex[:, :], 1.0, None, ALU.add).then_inc(d1_s, 1)
                dve.wait_ge(d1_s, b + 1)
                v.reciprocal(d1[:, :], d1[:, :]).then_inc(w0_s, 1)
                dve.wait_ge(w0_s, b + 1)
                hold(dve, "dve")
                v.tensor_copy(cols(w_all, b)[:, :, 0], d1[:, :])
                v.tensor_tensor(cols(w_all, b)[:, :, 1], d1[:, :], dex[:, :], ALU.mult).then_inc(w1_s, 1)
                dve.wait_ge(w1_s, b + 1)

            def slots(b, half, q):
                v.tensor_tensor(cnt[:, :, :], rt[:, 0:NC * E].rearrange("p (c e) -> p c e", c=NC),
                                base[:, :].unsqueeze(1).to_broadcast([P, NC, E]), ALU.add).then_inc(cnt_s, 1)
                dve.wait_ge(cnt_s, b + 1)
                v.tensor_tensor(base[:, :], base[:, :], rt[:, NC * E:NC * E + E], ALU.add).then_inc(base_s, 1)
                for t in range(2):
                    last = v.tensor_tensor(pick[:, t, :, :], oh[:, t, :, :], cnt[:, :, :], ALU.mult)
                last.then_inc(pick_s, 1)
                dve.wait_ge(pick_s, b + 1)
                hold(dve, "dve")
                for t in range(2):
                    last = v.tensor_reduce(cols(s_all, b)[:, :, t], pick[:, t, :, :], axis=AX.X, op=ALU.add)
                last.then_inc(slotf_s, 1)
                dve.wait_ge(slotf_s, b + 1)
                hold(dve, "dve")
                v.tensor_copy(slot[:, q, :, :], cols(s_all, b)).then_inc(slot_s, 1)

            pipeline(v, step)

            tc = [0]

            def tchain(ins):
                tc[0] += 1
                ins.then_inc(tstep, 1)
                dve.wait_ge(tstep, tc[0])

            dve.wait_ge(base_s, NB)
            tchain(v.tensor_copy(padrow[:, :], base[:, :]))
            v.tensor_copy(counti[:, :], padrow[:, :]).then_inc(tab_s, 1)
            tchain(v.tensor_tensor(count[:, :], base[:, :], offs[:, :], ALU.subtract))
            tchain(v.tensor_tensor(need[:, :, :], count[:, :].unsqueeze(2).to_broadcast([P, E, MAXT]), steps[:, :, :], ALU.is_gt))
            tchain(v.tensor_reduce(ntile[:, :], need[:, :, :], axis=AX.X, op=ALU.add))
            tchain(v.tensor_tensor_scan(tend[:, :], onesf[:, 0:E], ntile[:, :], 0.0, ALU.mult, ALU.add))
            tchain(v.tensor_tensor(tstart[:, :], tend[:, :], ntile[:, :], ALU.subtract))
            tchain(v.scalar_tensor_tensor(delta[:, :], tstart[:, :], float(TOK), offs[:, :], ALU.mult, ALU.subtract))
            tchain(v.tensor_tensor(ge[:, :, :], tid[:, :, :], tend[0:1, :].unsqueeze(1).to_broadcast([1, TILES, E]), ALU.is_ge))
            tchain(v.tensor_tensor(gs[:, :, :], tid[:, :, :], tstart[0:1, :].unsqueeze(1).to_broadcast([1, TILES, E]), ALU.is_ge))
            tchain(v.tensor_reduce(tab_e[:, :], ge[:, :, :], axis=AX.X, op=ALU.add))
            tchain(v.tensor_scalar(tab_e[:, :], tab_e[:, :], float(E - 1), None, ALU.min))
            tchain(v.tensor_tensor(gs[:, :, :], gs[:, :, :], ge[:, :, :], ALU.subtract))
            tchain(v.tensor_tensor(gs[:, :, :], gs[:, :, :], delta[0:1, :].unsqueeze(1).to_broadcast([1, TILES, E]), ALU.mult))
            tchain(v.tensor_reduce(tab_r[:, :], gs[:, :, :], axis=AX.X, op=ALU.add))
            tchain(v.scalar_tensor_tensor(tab_r[:, :], tid[:, :, 0], float(TOK), tab_r[:, :], ALU.mult, ALU.subtract))
            tchain(v.tensor_scalar(tab_d[:, :], tab_r[:, :], -1.0, float(DUMMY), ALU.mult, ALU.add))
            tchain(v.tensor_tensor(tab_d[:, :], tab_d[:, :], ge[:, :, E - 1], ALU.mult))
            tchain(v.tensor_tensor(tab_r[:, :], tab_r[:, :], tab_d[:, :], ALU.add))
            tchain(v.tensor_copy(table[:, 0, :], tab_e[:, :]))
            v.tensor_copy(table[:, 1, :], tab_r[:, :]).then_inc(tab_s, 1)
            tchain(v.tensor_copy(rowf[:, :, :], s_all[:, :, :]))
            for e in range(E):
                tchain(v.tensor_scalar(rsel[:, :, :], e_all[:, :, :], float(e), delta[:, e:e + 1], ALU.is_equal, ALU.mult))
                tchain(v.tensor_tensor(rowf[:, :, :], rowf[:, :, :], rsel[:, :, :], ALU.add))
            v.tensor_copy(yrow[:, :, :], rowf[:, :, :]).then_inc(yrow_s, 1)

            def split_rows(j, r):
                dve.wait_ge(tr_s, j + 1)
                wait_past(dve, mm1_s, NI * (j - 1))
                for k in range(NK):
                    last = v.tensor_copy(nh[:, r, k, :], TR[k][:, 0:TOK])
                last.then_inc(nh_s, 1)
                dve.wait_ge(nh_s, j + 1)
                for k in range(NK):
                    last = v.tensor_tensor(nl[:, r, k, :], TR[k][:, 0:TOK], nh[:, r, k, :], ALU.subtract)
                last.then_inc(nl_s, 1)

            def evacuate(j, half, r):
                dve.wait_ge(mm2_s, NI * j + NI)
                dve.wait_ge(got_b2[r], 16 * half + 16)
                if not isinstance(j, int) or j >= 2:
                    dve.wait_ge(y_out[r], 16 * half)
                for h in range(TH):
                    last = v.tensor_tensor(yt[:, r, h, :], ACC[h][:, 0:D], b2t[:, r, :], ALU.add)
                last.then_inc(yt_s, 1)

            def tile(j, half, r, first, last_tile):
                for c in range(NI):
                    n = NI * j + c
                    dve.wait_ge(gf_s, n + 1)
                    wait_past(dve, mm2_s, n - 3)
                    v.tensor_copy(gh[:, c % 4, :], gf[:, c % 2, :]).then_inc(gh_s, 1)
                    dve.wait_ge(gh_s, n + 1)
                    v.tensor_tensor(gl[:, c % 4, :], gf[:, c % 2, :], gh[:, c % 4, :], ALU.subtract).then_inc(gl_s, 1)
                    if c == 1 and not first:
                        evacuate(j - 1, half - 1 + r, 1 - r)
                    if c == 5 and not last_tile:
                        split_rows(j + 1, 1 - r)

            split_rows(0, 0)
            tile(0, 0, 0, True, False)
            for j in range(1, 3):
                tile(j, j // 2, j % 2, False, False)
            with v.Fori(1, TILES // 2 - 1) as h:
                tile(2 * h + 1, h, 1, False, False)
                tile(2 * h + 2, h + 1, 0, False, False)
            tile(TILES - 1, TILES // 2 - 1, 1, False, True)
            evacuate(TILES - 1, TILES // 2 - 1, 1)

            def mix(b, half, r):
                dve.wait_ge(got_gb[r], 16 * half + 16)
                for c in range(NC):
                    n = NC * b + c
                    w = lambda t: w_all[:, ds(n, 1), t]
                    dve.wait_ge(got_ya[c], 16 * b + 16)
                    v.tensor_scalar(ya[:, c, :], ya[:, c, :], w(0), None, ALU.mult).then_inc(ca_s, 1)
                    dve.wait_ge(ca_s, n + 1)
                    dve.wait_ge(got_yb[c], 16 * b + 16)
                    wait_past(dve, cc_s, n - 1)
                    v.scalar_tensor_tensor(ov[:, c % 2, :], yb[:, c, :], w(1), ya[:, c, :], ALU.mult, ALU.add).then_inc(cb_s, 1)
                    dve.wait_ge(cb_s, n + 1)
                    if not isinstance(b, int) or b >= 1:
                        dve.wait_ge(o_out[c], 16 * b)
                    v.tensor_tensor(res[:, c, :], ov[:, c % 2, :], gbB[:, r, :], ALU.mult).then_inc(cc_s, 1)
                    dve.wait_ge(cc_s, n + 1)
                    v.tensor_tensor(res[:, c, :], res[:, c, :], resid[:, ds(n, 1), :].rearrange("p a d -> p (a d)"), ALU.add).then_inc(res_s, 1)

            for b in range(2):
                mix(b, 0, b)
            with v.Fori(1, NB // 2) as h:
                for r in range(2):
                    mix(2 * h + r, h, r)

        @block.tensor
        def _(pe):
            t = nc.tensor
            pe.wait_ge(consts, 13)
            pe.wait_ge(c_step, 1)
            for k in range(NK):
                last = t.transpose(Q[:, k * NB:(k + 1) * NB], cin[:, k * P:(k + 1) * P], ident[0:NB, 0:NB])
            last.then_inc(cT_ps, 1)
            pe.wait_ge(cT_sb, 1)
            pe.wait_ge(got_wmod, 16)
            for s in range(3):
                for k in range(NK):
                    last = t.matmul(S[s][0:NB, :], cT[:, k, :], wmod[:, k, s * 512:(s + 1) * 512], start=k == 0, stop=k == NK - 1)
            last.then_inc(mod_ps, 1)
            pe.wait_ge(mod_step, 8)
            for n, (sel, k) in enumerate(((CA, 0), (CA, 1), (SA, 0), (SA, 1))):
                last = t.transpose(Q[:, 64 + n * NB:64 + (n + 1) * NB], mod[:, sel * D + k * P:sel * D + (k + 1) * P], ident[0:NB, 0:NB])
            last.then_inc(modT_ps, 1)
            pe.wait_ge(got_vec, 80)
            pe.wait_ge(got_r, 32)
            t.transpose(V[:, 0:NVEC], vrow[:, :], ident[0:NVEC, 0:NVEC])
            for k in range(NK):
                last = t.transpose(V[:, 128 + k * E:128 + (k + 1) * E], rrow[:, k * P:(k + 1) * P], ident[0:E, 0:E])
            last.then_inc(vec_ps, 1)
            pe.wait_ge(base_set, 1)
            for k in range(NK):
                last = t.matmul(V[:, 256:256 + E], rnbb[:, k, :], rT[:, k, :], start=k == 0, stop=k == NK - 1)
            last.then_inc(rb_ps, 1)
            pe.wait_ge(got_w, 64)
            pe.wait_ge(setup_done, 1)

            def step(i, half, r, project, attend, route, place):
                if project:
                    pe.wait_ge(xc_s, i + 1)
                    wait_past(pe, nT_s, i - 2)
                    for k in range(NK):
                        for c in range(NC):
                            last = t.transpose(TR[k][:, c * P:(c + 1) * P], xc[:, c, k * P:(k + 1) * P], ident[:, :])
                    last.then_inc(xT_s, 1)
                if attend:
                    b, q = i - 1, 1 - r
                    pe.wait_ge(phi_s, b + 1)
                    pe.wait_ge(vT_s, b + 1)
                    wait_past(pe, x2_s, b)
                    pe.wait_ge(small_read, i)
                    for s in range(NC):
                        dst = S[2][:, 256:384] if s == 3 else S[s][:, 0:PW[s]]
                        last = t.matmul(dst, vT[:, q, s * P:(s + 1) * P], qk[0:H, q, s * P:T], start=True, stop=True)
                    last.then_inc(score_s, 1)
                if project:
                    pe.wait_ge(hT_s, i + 1)
                    wait_past(pe, phi_s, i)
                    wait_past(pe, ktok_s, i)
                    for k in range(NK):
                        t.matmul(Q[:, :], wqk[:, k, :], hT[:, k, :], start=k == 0, stop=k == NK - 1)
                    for k in range(NK):
                        last = t.matmul(V[0:H, :], wv[:, k, :], hT[:, k, :], start=k == 0, stop=k == NK - 1)
                    last.then_inc(proj_s, 1)
                if route:
                    b = i - 2
                    pe.wait_ge(nrm_s, b + 1)
                    wait_past(pe, hT_s, b + 3 if project else 0)
                    for k in range(NK):
                        for c in range(NC):
                            last = t.transpose(TR[k][:, c * P:(c + 1) * P], nrm[:, r, c, k * P:(k + 1) * P], ident[:, :])
                    last.then_inc(nTp_s, 1)
                if attend:
                    b, q = i - 1, 1 - r
                    pe.wait_ge(diag_s, b + 1)
                    pe.wait_ge(strip_s, b + 1)
                    pe.wait_ge(ktok_s, b + 1)
                    wait_past(pe, oT_s, b)
                    for s in range(NC):
                        last = t.matmul(O[0:H, s * P:T], ktok[:, q, s, :], pt[:, PO[s]:PO[s] + PW[s]], start=s == 0, stop=s == NC - 1)
                    last.then_inc(pv_s, 1)
                if project:
                    pe.wait_ge(phi_s, i + 1)
                    pe.wait_ge(vT_s, i + 1)
                    hold(pe, "pe")
                    for c in range(NC):
                        last = t.transpose(V[:, c * H:(c + 1) * H], qk[H:2 * H, r, c * P:(c + 1) * P], ident[H:2 * H, H:2 * H])
                    last.then_inc(ktr_s, 1)
                wait_past(pe, small_read, i)
                if attend:
                    pe.wait_ge(qz_s, i)
                    pe.wait_ge(strip_s, i)
                    for c in range(NC):
                        last = t.matmul(DEN[:, c:c + 1], qz[:, c * P:(c + 1) * P], onesf[0:H, 0:1], start=True, stop=True)
                if place:
                    b = i - 3
                    pe.wait_ge(ohs_s, b + 1)
                    flat = ohs[:, :, :].rearrange("p c e -> p (c e)")
                    t.matmul(RANK, before[:, :], flat, start=True, stop=False)
                    for back in range(1, NC):
                        t.matmul(S[2][:, 420 + back * E:452], allone[:, :], flat[:, 0:(NC - back) * E], start=False, stop=back == NC - 1)
                    for c in range(NC):
                        last = t.matmul(TOT, allone[:, :], flat[:, c * E:(c + 1) * E], start=c == 0, stop=c == NC - 1)
                if route:
                    b = i - 2
                    pe.wait_ge(nT_s, b + 1)
                    for c in range(NC):
                        for k in range(NK):
                            last = t.matmul(LOG[:, c * E:(c + 1) * E], nT[:, k, c * P:(c + 1) * P], rTg[:, k, :], start=k == 0, stop=k == NK - 1)
                if project and r == 0:
                    pe.wait_ge(got_we, 32 * half + 32)
                    pe.wait_ge(lge_s, half + 1)
                    for n in range(NI):
                        for k in range(NK):
                            last = t.matmul(B1P[:, n:n + 1], w1f[:, k, n * P:(n + 1) * P], lge[:, 2 + k:3 + k], start=k == 0, stop=k == NK - 1)
                last.then_inc(small_s, 1)
                if attend:
                    b, q = i - 1, 1 - r
                    pe.wait_ge(oT_s, b + 1)
                    pe.wait_ge(wog_s, b + 1)
                    for c in range(NC):
                        last = t.matmul(S[c // 2][:, (c % 2) * D:(c % 2 + 1) * D], oT[:, c * P:(c + 1) * P], wog[:, q, :], start=True, stop=True)
                    last.then_inc(owo_s, 1)

            pipeline(t, step)

            def turn(j, half, r):
                pe.wait_ge(got_xin[r], 16 * half + 16)
                wait_past(pe, nl_s, j)
                for k in range(NK):
                    for h in range(TH):
                        last = t.transpose(TR[k][:, h * P:(h + 1) * P], xin[:, r, h, k * P:(k + 1) * P], ident[:, :])
                last.then_inc(tr_s, 1)

            def first(j, r, c):
                wait_past(pe, gf_s, NI * j + c - 1)
                n = 0
                for k in range(NK):
                    head = wbuf[:, r, k * I + c * P:k * I + (c + 1) * P]
                    rest = wbuf[:, r, 2048 + k * I + c * P:2048 + k * I + (c + 1) * P]
                    for w, m in ((head, nh), (head, nl), (rest, nh)):
                        last = t.matmul(MM[c % 2][:, 0:TOK], w, m[:, r, k, :], start=n == 0, stop=n == 5)
                        n += 1
                last.then_inc(mm1_s, 1)

            def second(j, r, c):
                pe.wait_ge(gl_s, NI * j + c + 1)
                head = wbuf[:, r, 4096 + c * D:4096 + (c + 1) * D]
                rest = wbuf[:, r, 6144 + c * D:6144 + (c + 1) * D]
                for h in range(TH):
                    n = 0
                    for g, w in ((gh, head), (gh, rest), (gl, head)):
                        last = t.matmul(ACC[h][:, 0:D], g[:, c % 4, h * P:(h + 1) * P], w,
                                        start=c == 0 and n == 0, stop=c == NI - 1 and n == 2)
                        n += 1
                last.then_inc(mm2_s, 1)

            def tile(j, half, r, is_first, is_last):
                pe.wait_ge(nl_s, j + 1)
                pe.wait_ge(got_w1[r], 16 * half + 16)
                for c in range(NI):
                    first(j, r, c)
                    if c >= 2:
                        if c == 2:
                            pe.wait_ge(got_w2[r], 16 * half + 16)
                            wait_past(pe, yt_s, j)
                        second(j, r, c - 2)
                    elif not is_first:
                        second(j - 1, 1 - r, NI - 2 + c)
                    if c == 4 and not is_last:
                        turn(j + 1, half + r, 1 - r)

            turn(0, 0, 0)
            tile(0, 0, 0, True, False)
            with t.Fori(0, TILES // 2 - 1) as h:
                tile(2 * h + 1, h, 1, False, False)
                tile(2 * h + 2, h + 1, 0, False, False)
            tile(TILES - 1, TILES // 2 - 1, 1, False, True)
            second(TILES - 1, 1, NI - 2)
            second(TILES - 1, 1, NI - 1)


_INS = ['L0_attn_x', 'L0_attn_W_q', 'L0_attn_W_k', 'L0_attn_W_v', 'L0_attn_W_o', 'L0_ffn_rn_g', 'L0_ffn_rn_b',
        'L0_ffn_router_w', 'L0_ffn_router_b', 'L0_ffn_ln_g', 'L0_ffn_ln_b', 'L0_ffn_w1', 'L0_ffn_b1',
        'L0_ffn_w2', 'L0_ffn_b2', 'L0_c', 'L0_wmod']


def kernel(**inputs):
    import numpy as _np
    import concourse.bacc as _bacc
    from concourse import mybir as _mybir
    from concourse.bass_utils import run_bass_kernel_spmd as _run

    nc = _bacc.Bacc("TRN2", target_bir_lowering=False, num_devices=1)
    f32, bf16 = _mybir.dt.float32, _mybir.dt.bfloat16
    arrays, args = {}, []
    for name in _INS:
        a = _np.ascontiguousarray(inputs[name])
        arrays[f"in_{name}"] = a
        args.append(nc.dram_tensor(f"in_{name}", a.shape, _mybir.dt.from_np(a.dtype), kind="ExternalInput").ap())
    for name, shape, dt in (("mod_rows", (NB, 6 * D), f32), ("lists", (DUMMY + TOK, D), f32),
                            ("wsplit", (E, P, 4 * NI * D), bf16), ("b1_folded", (E, P, NI), f32),
                            ("y_rows", (TILES * TOK, D), f32)):
        args.append(nc.dram_tensor(name, shape, dt, kind="Internal").ap())
    args.append(nc.dram_tensor("out_0", (NB, T, D), f32, kind="ExternalOutput").ap())
    adaln_moe_kernel(nc, *args)
    r = _run(nc, [arrays], core_ids=[0])
    return r.results[0]["out_0"]
```

```python
import concourse.bass as bass
from concourse import mybir
from contextlib import ExitStack


P = 128
NB, T, D = 16, 512, 256
H = 64
E, I = 8, 1024
NC, NK = T // P, D // P
NI = I // P
NTOK = NB * T
TOK = 256
TH = TOK // P
TILES = (2 * NTOK + E * (TOK - 1)) // TOK
CAP = NTOK + TOK
RW = D + 4
DUMP = 3 * NTOK
DUMMY = E * CAP
MAXT = -(-NTOK // TOK)
EPS = 1e-5
SA, CA, GA, SB, CB, GB = range(6)
VEC_B1, VEC_G, VEC_B, VEC_RG, VEC_RB = 0, E * NI, E * NI + 2 * E, E * NI + 4 * E, E * NI + 4 * E + 2
NVEC = VEC_RB + 2


def adaln_moe_kernel(nc, x_d, wq_d, wk_d, wv_d, wo_d, rng_d, rnb_d, rw_d, rb_d, lng_d, lnb_d,
                     w1_d, b1_d, w2_d, b2_d, c_d, wmod_d, mod_d, list_d, wsplit_d, b1r_d, b1f_d, y_d, out_d):
    f32, bf16, i32, u32 = mybir.dt.float32, mybir.dt.bfloat16, mybir.dt.int32, mybir.dt.uint32
    ALU, ACT, AX = mybir.AluOpType, mybir.ActivationFunctionType, mybir.AxisListType
    ds = bass.ds

    ctx = ExitStack()
    with ctx:
        def sb(name, shape, dt=f32):
            return ctx.enter_context(nc.sbuf_tensor(name, shape, dt))

        def sem(name):
            return ctx.enter_context(nc.semaphore(name))

        def sems(name, n=2):
            return [sem(f"{name}{i}") for i in range(n)]

        resid = sb("resid", [P, NB * NC, D])
        ident = sb("ident", [P, P])
        causal = sb("causal", [P, P])
        before = sb("before", [P, P], bf16)
        allone = sb("allone", [P, P], bf16)
        onesf = sb("onesf", [P, T])
        experts = sb("experts", [P, E])
        mhalf = sb("mhalf", [P, 3, NC])
        wqk = sb("wqk", [P, NK, 2 * H])
        wv = sb("wv", [P, NK, H])
        wo = sb("wo", [H, D])
        wog = sb("wog", [H, 2, D])
        vrow = sb("vrow", [NVEC, P])
        vecs = sb("vecs", [P, NVEC])
        lngb = sb("lngb", [P, E, 4])
        rrow = sb("rrow", [E, D])
        rT = sb("rT", [P, NK, E])
        rTg = sb("rTg", [P, NK, E])
        rnbb = sb("rnbb", [P, NK, P])
        rbias = sb("rbias", [P, E])
        cin = sb("cin", [NB, D])
        cex = sb("cex", [NB, D])
        cT = sb("cT", [P, NK, NB])
        mod = sb("mod", [NB, 6 * D])
        modT = sb("modT", [P, NB, 4])
        modc = sb("modc", [P, 2, 4])
        gaB = sb("gaB", [H, 2, D])
        csB = sb("csB", [P, 2, 2 * D])
        st = sb("st", [P, NC, 6])
        mv = sb("mv", [P, 3, NC, 2]); ve = sb("ve", [P, 3, NC]); rs = sb("rs", [P, 2, 3, NC]); nm = sb("nm", [P, 2, 3, NC])
        rowbuf = sb("rowbuf", [P, 4 * NC * D])
        xc, xn2, *h2 = (rowbuf[:, n * NC * D:(n + 1) * NC * D].rearrange("p (c d) -> p c d", c=NC) for n in range(4))
        gneg, gsgn = rowbuf[0:NB, 0:D], rowbuf[0:NB, D:2 * D]
        yt = rowbuf[:, 0:2 * TH * D].rearrange("p (r h d) -> p r h d", r=2, h=TH)
        xin = rowbuf[:, 2 * NC * D:2 * NC * D + 2 * TH * RW].rearrange("p (r h d) -> p r h d", r=2, h=TH)
        hT = sb("hT", [P, NK, T])
        ex = sb("ex", [P, T])
        qk = sb("qk", [P, 2, T])
        vT = sb("vT", [H, 2, T])
        ktok = sb("ktok", [P, 2, NC, H])
        zT = sb("zT", [H, T])
        qz = sb("qz", [H, 2, T])
        PW = [T - a * P for a in range(NC)]
        PO = [a * T for a in range(NC)]
        pt = sb("pt", [P, NC * T])
        oT = sb("oT", [H, T])
        den = sb("den", [P, NC]); rden = sb("rden", [P, NC])
        nrm = sb("nrm", [P, 2, NC, RW])
        nT = sb("nT", [P, NK, T])
        lg = sb("lg", [P, NC, E])
        mx = sb("mx", [P, NC, 8])
        ix = sb("ix", [P, NC, 8], u32)
        ef = sb("ef", [P, NC, 2])
        oh = sb("oh", [P, 2, NC, E])
        ohs = sb("ohs", [P, NC, E], bf16)
        dl = sb("dl", [P, NC]); dex = sb("dex", [P, NC]); d1 = sb("d1", [P, NC])
        rt = sb("rt", [P, NC * E + E])
        cnt = sb("cnt", [P, NC, E])
        pick = sb("pick", [P, 2, NC, E])
        base = sb("base", [P, E])
        slot = sb("slot", [P, 2, NC, 2], i32)
        w_all = sb("w_all", [P, NB * NC, 2])
        slotf = sb("slotf", [P, NC, 2])
        token = sb("token", [P, NC])
        wbuf = sb("wbuf", [P, 2, 4 * NI * D], bf16)
        w1f = wbuf[:, 1, :].bitcast(f32)[:, 0:2048].rearrange("p (k i) -> p k i", k=NK)
        w2f = wbuf[:, 1, :].bitcast(f32)[:, 2048:4096]
        wmod = wbuf[:, 0, :].bitcast(f32)[:, 0:NK * 6 * D].rearrange("p (k n) -> p k n", k=NK)
        lge = sb("lge", [P, 4])
        b1f = sb("b1f", [P, E, NI])
        nh = sb("nh", [P, 2, NK, TOK], bf16)
        nl = sb("nl", [P, 2, NK, TOK], bf16)
        b1row = [t[:, :, :, :].bitcast(f32).rearrange("p r k n -> p (r k n)")[0:1, :] for t in (nh, nl)]
        pad = sb("pad", [P, TH, RW])
        ydf = sb("ydf", [P, 2, TH]); ydp = sb("ydp", [P, 2, TH]); ydst = sb("ydst", [P, 2, TH], i32)
        gf = sb("gf", [P, 2, TOK])
        gh = sb("gh", [P, 4, TOK], bf16)
        gl = sb("gl", [P, 4, TOK], bf16)
        b1t = sb("b1t", [P, 2, NI])
        b2t = sb("b2t", [P, 2, D])
        offs = sb("offs", [P, E]); count = sb("count", [P, E]); counti = sb("counti", [P, E], i32)
        steps = sb("steps", [P, E, MAXT]); need = sb("need", [P, E, MAXT])
        ntile = sb("ntile", [P, E]); tend = sb("tend", [P, E]); tstart = sb("tstart", [P, E])
        delta = sb("delta", [P, E])
        padrow = sb("padrow", [P, E], i32)
        tid = sb("tid", [P, TILES, E])
        ge, gs = (pt[:, n * TILES * E:(n + 1) * TILES * E].rearrange("p (j e) -> p j e", e=E) for n in range(2))
        tab_e = sb("tab_e", [P, TILES]); tab_r = sb("tab_r", [P, TILES]); tab_d = sb("tab_d", [P, TILES]); hop = sb("hop", [P, E])
        table = sb("table", [P, 3, TILES], i32)
        gbB = pt[:, 0:4 * D].rearrange("p (r d) -> p r d", r=4)
        R = 4
        ya, yb = (wbuf[:, n, :].bitcast(f32).rearrange("p (r c d) -> p r c d", r=R, c=NC) for n in range(2))

        bank = [ctx.enter_context(nc.psum_tensor(f"bank{i}", [P, 512], f32)) for i in range(8)]
        TR, Q, V, S, O = bank[0:2], bank[2], bank[3], bank[4:7], bank[7]
        DEN = S[2][:, 384:388]
        LOG = S[2][:, 388:420]
        RANK, TOT, RT = O[:, 0:32], O[:, 32:40], O[:, 0:40]
        ACC = [bank[2:4], bank[4:6]]
        MM = bank[6:8]

        consts = sem("consts"); dconst = sem("dconst"); acon = sem("acon")
        got_c = sem("got_c"); got_wmod = sem("got_wmod"); got_w = sem("got_w"); got_vec = sem("got_vec")
        got_r = sem("got_r"); base_set = sem("base_set")
        c_exp = sem("c_exp"); c_step = sem("c_step"); cT_ps = sem("cT_ps"); cT_sb = sem("cT_sb")
        mod_ps = sem("mod_ps"); mod_step = sem("mod_step"); mod_out = sem("mod_out"); modT_ps = sem("modT_ps")
        vec_ps = sem("vec_ps"); set_step = sem("set_step"); rb_ps = sem("rb_ps"); setup_done = sem("setup_done")
        got_x = sems("got_x"); got_ga = sems("got_ga"); got_cs = sems("got_cs")
        st_s = sem("st_s"); mv_s = sem("mv_s"); ve_s = sem("ve_s"); rs_s = sem("rs_s"); nm_s = sem("nm_s")
        stat_set = sem("stat_set"); rank_s = sem("rank_s"); tok_s = sem("tok_s"); pad_s = sem("pad_s")
        xc_s = sem("xc_s"); xT_s = sem("xT_s"); modc_s = sem("modc_s"); hT_s = sem("hT_s")
        proj_s = sem("proj_s"); ex_s = sem("ex_s"); vT_s = sem("vT_s"); exn_s = sem("exn_s"); phi_s = sem("phi_s")
        ktr_s = sem("ktr_s"); ktok_s = sem("ktok_s"); scan_s = sem("scan_s"); qz_s = sem("qz_s")
        score_s = sem("score_s"); diag_s = sem("diag_s"); strip_s = sem("strip_s"); pv_s = sem("pv_s")
        oT_s = sem("oT_s"); small_s = sem("small_s"); small_read = sem("small_read"); dmax_s = sem("dmax_s"); rden_s = sem("rden_s")
        wog_s = sem("wog_s"); owo_s = sem("owo_s"); x2_s = sem("x2_s")
        xn2_s = sem("xn2_s"); h2m_s = sem("h2m_s"); h2_s = sem("h2_s"); nrm_s = sem("nrm_s")
        nTp_s = sem("nTp_s"); nT_s = sem("nT_s"); lg_s = sem("lg_s"); mx_s = sem("mx_s")
        ix_s = sem("ix_s"); ef_s = sem("ef_s"); oh_s = sem("oh_s"); ohs_s = sem("ohs_s"); dl_s = sem("dl_s")
        dex_s = sem("dex_s"); d1_s = sem("d1_s"); w0_s = sem("w0_s"); w1_s = sem("w1_s")
        rt_s = sem("rt_s"); cnt_s = sem("cnt_s"); pick_s = sem("pick_s"); slotf_s = sem("slotf_s")
        slot_s = sem("slot_s"); base_s = sem("base_s"); scat = sems("scat")
        got_we = sem("got_we"); lge_s = sem("lge_s"); head_s = sem("head_s"); rest_s = sem("rest_s")
        b1f_s = sem("b1f_s"); b1p_s = sem("b1p_s"); b1r_s = sem("b1r_s"); got_b1v = sem("got_b1v"); b1v_ps = sem("b1v_ps"); split_out = sem("split_out"); b1_out = sem("b1_out")
        tstep = sem("tstep"); tab_s = sem("tab_s"); pad_out = sem("pad_out")
        got_xin = sems("got_xin"); got_w1 = sems("got_w1"); got_w2 = sems("got_w2")
        got_b1 = sems("got_b1"); got_b2 = sems("got_b2")
        tr_s = sem("tr_s"); nh_s = sem("nh_s"); nl_s = sem("nl_s"); mm1_s = sem("mm1_s"); gf_s = sem("gf_s")
        gh_s = sem("gh_s"); gl_s = sem("gl_s"); mm2_s = sem("mm2_s"); yt_s = sem("yt_s"); y_out = sems("y_out")
        yd_a = sem("yd_a"); yd_b = sem("yd_b"); yd_s = sem("yd_s")
        got_gb = sems("got_gb", R); got_ya = sems("got_ya", R); got_yb = sems("got_yb", R)
        ca_s = sem("ca_s"); cb_s = sem("cb_s"); cc_s = sem("cc_s"); res_s = sem("res_s"); o_out = sem("o_out")
        held = {n: sem(f"held_{n}") for n in ("act", "dve", "pe", "pool", "sp")}

        def wait_past(eng, semaphore, value):
            if not isinstance(value, int) or value > 0:
                eng.wait_ge(semaphore, value)

        def upto(n):
            return min(n, NB) if isinstance(n, int) else n

        def hold(eng, name):
            eng.sem_inc(held[name], 1)

        def pipeline(eng, step):
            for i in range(5):
                step(i, i // 2, i % 2, *(i >= n for n in range(6)))
            with eng.Fori(2, NB // 2 - 1) as j:
                step(2 * j + 1, j, 1, *(True,) * 6)
                step(2 * j + 2, j + 1, 0, *(True,) * 6)
            for i in range(NB - 1, NB + 5):
                step(i, i // 2, i % 2, *(i - n < NB for n in range(6)))

        block = ctx.enter_context(nc.Block())

        x_v = x_d.rearrange("b (c p) d -> b p c d", p=P)
        out_v = out_d.rearrange("b (c p) d -> b p c d", p=P)
        w1_v = w1_d.rearrange("e (k p) i -> e p k i", p=P)
        w2_v = w2_d.rearrange("e (c p) d -> e p c d", p=P)

        @block.sync
        def _(sp):
            sp.dma_start(cin[:, :], c_d).then_inc(got_c, 16)
            sp.dma_start(wmod, wmod_d.rearrange("(k p) n -> p k n", p=P)).then_inc(got_wmod, 16)
            for b in range(2):
                sp.dma_start(resid[:, b * NC:(b + 1) * NC, :], x_v[b]).then_inc(got_x[b], 16)
            sp.dma_start(wqk[:, :, 0:H], wq_d.rearrange("(k p) h -> p k h", p=P)).then_inc(got_w, 16)
            sp.dma_start(wqk[:, :, H:2 * H], wk_d.rearrange("(k p) h -> p k h", p=P)).then_inc(got_w, 16)
            sp.dma_start(wv[:, :, :], wv_d.rearrange("(k p) h -> p k h", p=P)).then_inc(got_w, 16)
            sp.dma_start(wo[:, :], wo_d).then_inc(got_w, 16)
            sp.dma_start(vrow[VEC_B1:VEC_G, :], b1_d.rearrange("e (i p) -> (e i) p", p=P)).then_inc(got_vec, 16)
            sp.dma_start(vrow[VEC_G:VEC_B, :], lng_d.rearrange("e (k p) -> (e k) p", p=P)).then_inc(got_vec, 16)
            sp.dma_start(vrow[VEC_B:VEC_RG, :], lnb_d.rearrange("e (k p) -> (e k) p", p=P)).then_inc(got_vec, 16)
            sp.dma_start(vrow[VEC_RG:VEC_RB, :], rng_d.rearrange("(k p) -> k p", p=P)).then_inc(got_vec, 16)
            sp.dma_start(vrow[VEC_RB:NVEC, :], rnb_d.rearrange("(k p) -> k p", p=P)).then_inc(got_vec, 16)
            sp.dma_start(rrow[:, :], rw_d).then_inc(got_r, 16)
            sp.dma_start(rbias[:, :], rb_d.partition_broadcast(P)).then_inc(got_r, 16)
            sp.wait_ge(mod_step, 8)
            sp.dma_start(mod_d, mod[:, :]).then_inc(mod_out, 16)
            sp.wait_ge(pad_s, 3)
            sp.dma_start(list_d[DUMMY:DUMMY + TOK, :].rearrange("(p r) d -> p r d", r=TH), pad[:, :, :]).then_inc(pad_out, 16)
            sp.wait_ge(mod_out, 16)
            sp.wait_ge(mod_ps, 1)

            def load_cs(s, q):
                wait_past(sp, h2_s, s - 1)
                sp.dma_start(csB[:, q, :], mod_d[ds(s, 1), SB * D:(CB + 1) * D].partition_broadcast(P)
                             if not isinstance(s, int) else
                             mod_d[s, SB * D:(CB + 1) * D].partition_broadcast(P)).then_inc(got_cs[q], 16)

            def step(i, half, r):
                if isinstance(i, int) and i == 0:
                    sp.dma_start(w1f, w1_v[0]).then_inc(got_we, 16)
                    sp.dma_start(w2f.rearrange("p (c d) -> p c d", c=NI), w2_v[0]).then_inc(got_we, 16)
                load_x(i, half, r)
                wait_past(sp, wog_s, i - 1)
                sp.dma_start(gaB[:, r, :], mod_d[ds(i, 1), GA * D:(GA + 1) * D].partition_broadcast(H)
                             if not isinstance(i, int) else
                             mod_d[i, GA * D:(GA + 1) * D].partition_broadcast(H)).then_inc(got_ga[r], 16)
                if not isinstance(i, int) or i >= 1:
                    load_cs(i - 1, 1 - r)
                if r == 1:
                    sp.wait_ge(rest_s, 3 * half + 3)
                    hold(sp, "sp")
                    sp.wait_ge(b1p_s, half + 1)
                    load_experts(half)
                    sp.wait_ge(b1r_s, half + 1)
                    for n in range(2):
                        sp.dma_start(b1r_d[half, n:n + 1, :] if isinstance(half, int) else b1r_d[ds(half, 1), n, :], b1row[n]).then_inc(b1_out, 16)
                    sp.dma_start(wsplit_d[half] if isinstance(half, int) else wsplit_d[ds(half, 1)],
                                 wbuf[:, 0, :]).then_inc(split_out, 16)

            def load_x(i, half, r):
                if isinstance(i, int):
                    if i + 2 < NB:
                        sp.wait_ge(got_x[r], 16 * (half + 1))
                        sp.dma_start(resid[:, (i + 2) * NC:(i + 3) * NC, :], x_v[i + 2]).then_inc(got_x[r], 16)
                else:
                    sp.wait_ge(got_x[r], 16 * half + 16)
                    sp.dma_start(resid[:, ds((i + 2) * NC, NC), :], x_v[ds(i + 2, 1)]).then_inc(got_x[r], 16)

            def load_experts(half):
                if isinstance(half, int):
                    if half + 1 < E:
                        sp.dma_start(w1f, w1_v[half + 1]).then_inc(got_we, 16)
                        sp.dma_start(w2f.rearrange("p (c d) -> p c d", c=NI), w2_v[half + 1]).then_inc(got_we, 16)
                else:
                    sp.dma_start(w1f, w1_v[ds(half + 1, 1)]).then_inc(got_we, 16)
                    sp.dma_start(w2f.rearrange("p (c d) -> p c d", c=NI), w2_v[ds(half + 1, 1)]).then_inc(got_we, 16)

            for i in range(2):
                step(i, 0, i)
            with nc.sync.Fori(1, NB // 2 - 1) as j:
                for r in range(2):
                    step(2 * j + r, j, r)
            for i in range(NB - 2, NB):
                step(i, NB // 2 - 1, i % 2)
            load_cs(NB - 1, 1)
            sp.wait_ge(b1_out, 32 * E)
            sp.dma_start(vrow[0:E * NI, :], b1r_d.rearrange("e n (i p) -> (e n i) p", p=P)).then_inc(got_b1v, 16)
            sp.wait_ge(b1f_s, 1)
            sp.dma_start(b1f_d.rearrange("e p i -> p e i"), b1f[:, :, :]).then_inc(b1_out, 16)

            sp.wait_ge(tab_s, 1)
            for e in range(E):
                row = nc.sync.value_load(padrow[0:1, e:e + 1], min_val=0, max_val=DUMMY)
                sp.dma_start(list_d[ds(row, TOK), :].rearrange("(p r) d -> p r d", r=TH), pad[:, :, :]).then_inc(pad_out, 16)
            sp.wait_ge(split_out, 16 * E)
            sp.wait_ge(b1_out, 32 * E + 16)
            sp.wait_ge(tab_s, 2)

            def rows_load(j, r):
                row = nc.sync.value_load(table[0:1, 1, ds(j, 1)], min_val=0, max_val=DUMMY)
                wait_past(sp, tr_s, j - 1)
                wait_past(sp, yd_s, j - 1)
                sp.dma_start(xin[:, r, :, :].rearrange("p r d -> p (r d)"),
                             list_d[ds(row, TOK), :].rearrange("(p r) d -> p (r d)", r=TH)).then_inc(got_xin[r], 16)

            def weights_load(j, r):
                e = nc.sync.value_load(table[0:1, 0, ds(j, 1)], min_val=0, max_val=E - 1)
                new = nc.sync.value_load(table[0:1, 2, ds(j, 1)], min_val=0, max_val=1)
                wait_past(sp, mm1_s, NI * (j - 1))
                sp.dma_start(wbuf[:, r, 0:4096], wsplit_d[ds(e, 1), :, 0:4096], cond=new).then_inc(got_w1[r], 16)
                wait_past(sp, gf_s, NI * (j - 1))
                sp.dma_start(b1t[:, r, :], b1f_d[ds(e, 1)]).then_inc(got_b1[r], 16)
                wait_past(sp, mm2_s, NI * (j - 1))
                sp.dma_start(wbuf[:, r, 4096:8192], wsplit_d[ds(e, 1), :, 4096:8192], cond=new).then_inc(got_w2[r], 16)
                wait_past(sp, yt_s, j - 1)
                sp.dma_start(b2t[:, r, :], b2_d[ds(e, 1), :].partition_broadcast(P)).then_inc(got_b2[r], 16)

            for j in range(2):
                weights_load(j, j)
            for r in range(2):
                sp.wait_ge(scat[r], 16 * 2 * NC * NB // 2)
            sp.wait_ge(pad_out, 16 * (E + 1))
            for j in range(2):
                rows_load(j, j)
            with nc.sync.Fori(1, TILES // 2) as h:
                for r in range(2):
                    rows_load(2 * h + r, r)
                    weights_load(2 * h + r, r)
            for j in range(TILES // 2 * 2, TILES):
                rows_load(j, j % 2)
                weights_load(j, j % 2)

            for r in range(2):
                sp.wait_ge(y_out[r], 16 * TH * ((TILES + 1 - r) // 2))

            def rows_in(b, r):
                wait_past(sp, res_s, b - R + 1)
                for t, (dst, got) in enumerate(((ya, got_ya), (yb, got_yb))):
                    sp.dma_start(dst[:, r, :, :], y_d[ds(t * NTOK + b * T, T), :].rearrange("(c p) d -> p c d", p=P)).then_inc(got[r], 16)
                sp.dma_start(gbB[:, r, :], mod_d[ds(b, 1), GB * D:(GB + 1) * D].partition_broadcast(P)).then_inc(got_gb[r], 16)

            def store(b):
                sp.wait_ge(res_s, b + 1)
                sp.dma_start(out_v[ds(b, 1)], resid[:, ds(NC * b, NC), :]).then_inc(o_out, 16)

            for b in range(R):
                rows_in(b, b)
            with nc.sync.Fori(0, NB // R - 1) as h:
                for r in range(R):
                    store(R * h + r)
                    rows_in(R * h + r + R, r)
            for b in range(NB - R, NB):
                store(b)
            sp.wait_ge(o_out, 16 * NB)

        @block.gpsimd
        def _(pool):
            g = nc.gpsimd
            g.memset(ident[:, :], 0.0).then_inc(consts, 1)
            g.memset(causal[:, :], 1.0).then_inc(consts, 1)
            g.memset(before[:, :], 1.0).then_inc(consts, 1)
            g.memset(allone[:, :], 1.0).then_inc(consts, 1)
            g.memset(onesf[:, :], 1.0).then_inc(consts, 1)
            g.memset(mhalf[:, :], -0.5).then_inc(consts, 1)
            g.iota(experts[:, :], pattern=[[1, E]], base=0, channel_multiplier=0,
                   allow_small_or_imprecise_dtypes=True).then_inc(consts, 1)
            g.iota(offs[:, :], pattern=[[CAP, E]], base=0, channel_multiplier=0,
                   allow_small_or_imprecise_dtypes=True).then_inc(consts, 1)
            g.iota(steps[:, :, :], pattern=[[0, E], [TOK, MAXT]], base=0, channel_multiplier=0,
                   allow_small_or_imprecise_dtypes=True).then_inc(consts, 1)
            g.iota(tid[:, :, :], pattern=[[1, TILES], [0, E]], base=0, channel_multiplier=0,
                   allow_small_or_imprecise_dtypes=True).then_inc(consts, 1)
            g.iota(token[:, :], pattern=[[P, NC]], base=-T, channel_multiplier=1,
                   allow_small_or_imprecise_dtypes=True).then_inc(tok_s, 1)
            g.memset(pad[:, :, :], 0.0).then_inc(pad_s, 1)
            pool.wait_ge(pad_s, 1)
            g.iota(pad[:, :, D:D + 1], pattern=[[1, TH], [0, 1]], base=DUMP - NTOK, channel_multiplier=TH,
                   allow_small_or_imprecise_dtypes=True).then_inc(pad_s, 1)
            g.memset(pad[:, :, D + 1:D + 2], -1.0).then_inc(pad_s, 1)
            pool.wait_ge(consts, 10)
            g.affine_select(out=ident[:, :], in_=ident[:, :], compare_op=ALU.not_equal, fill=1.0,
                            base=0, pattern=[[-1, P]], channel_multiplier=1).then_inc(consts, 1)
            g.affine_select(out=causal[:, :], in_=causal[:, :], compare_op=ALU.is_ge, fill=0.0,
                            base=0, pattern=[[1, P]], channel_multiplier=-1).then_inc(consts, 1)
            g.affine_select(out=before[:, :], in_=before[:, :], compare_op=ALU.is_ge, fill=0.0,
                            base=-1, pattern=[[1, P]], channel_multiplier=-1).then_inc(consts, 1)

            def inverse_root(i, r):
                pool.wait_ge(ve_s, i + 1)
                wait_past(pool, xc_s, upto(i - 1))
                wait_past(pool, xn2_s, upto(i - 4))
                wait_past(pool, nrm_s, upto(i - 5))
                wait_past(pool, nm_s, i - 1)
                g.tensor_tensor(rs[:, r, :, :], ve[:, :, :], mhalf[:, :, :], ALU.pow).then_inc(rs_s, 1)

            inverse_root(0, 0)

            def scatter(q, chunks):
                for c in chunks:
                    for t in range(2):
                        g.indirect_dma_start(list_d, bass.IndirectOffsetOnAxis(ap=slot[:, q, c, t:t + 1], axis=0),
                                             nrm[:, q, c, :], None).then_inc(scat[q], 16)

            def step(i, half, r, project, attend, settle, norm, route, place):
                if attend:
                    b, q = i - 1, 1 - r
                    pool.wait_ge(got_ga[q], 16 * (half if q == 1 else half + 1))
                    wait_past(pool, owo_s, b - 1)
                    g.tensor_tensor(wog[:, q, :], wo[:, :], gaB[:, q, :], ALU.mult).then_inc(wog_s, 1)
                if norm and (project or attend):
                    b, q = i - 3, 1 - r
                    pool.wait_ge(got_cs[q], 16 * (half if q == 0 else half - 1))
                    pool.wait_ge(xn2_s, b + 1)
                    wait_past(pool, nrm_s, b - 1)
                    g.tensor_tensor(h2[q], xn2, csB[:, q, D:2 * D].unsqueeze(1).to_broadcast([P, NC, D]), ALU.mult).then_inc(h2m_s, 1)
                    pool.wait_ge(h2m_s, b + 1)
                    g.tensor_tensor(h2[q], h2[q], csB[:, q, 0:D].unsqueeze(1).to_broadcast([P, NC, D]), ALU.add).then_inc(h2_s, 1)
                if place:
                    pool.wait_ge(slot_s, i - 4)
                    hold(pool, "pool")
                    scatter(1 - r, (0, 1))
                if project or attend or norm:
                    inverse_root(i + 1, 1 - r)
                if place:
                    scatter(1 - r, (2, 3))

            pipeline(g, step)

            def y_scatter(j, half, r):
                pool.wait_ge(yt_s, j + 1)
                pool.wait_ge(yd_s, j + 1)
                hold(pool, "pool")
                for h in range(TH):
                    g.indirect_dma_start(y_d, bass.IndirectOffsetOnAxis(ap=ydst[:, r, h:h + 1], axis=0),
                                         yt[:, r, h, :], None).then_inc(y_out[r], 16)

            with g.Fori(0, TILES // 2) as h:
                for r in range(2):
                    y_scatter(2 * h + r, h, r)
            for j in range(TILES // 2 * 2, TILES):
                y_scatter(j, j // 2, j % 2)

            def times_gb(b, turn, r):
                pool.wait_ge(got_gb[r], 16 * turn + 16)
                pool.wait_ge(cb_s, b + 1)
                g.tensor_tensor(ya[:, r, :, :], ya[:, r, :, :], gbB[:, r, :].unsqueeze(1).to_broadcast([P, NC, D]), ALU.mult).then_inc(cc_s, 1)

            with g.Fori(0, NB // R) as h:
                for r in range(R):
                    times_gb(R * h + r, h, r)

        @block.scalar
        def _(act):
            a = nc.scalar
            act.wait_ge(got_c, 16)
            a.activation(cex[:, :], cin[:, :], ACT.Exp, scale=-1.0).then_inc(c_exp, 1)
            act.wait_ge(setup_done, 1)

            def rows(b):
                return lambda c: resid[:, b * NC + c, :] if isinstance(b, int) else resid[:, ds(b * NC + c, 1), :]

            def normalise(out, src, r, n, done):
                hold(act, "act")
                for c in range(NC):
                    last = a.activation(out(c), src(c), ACT.Identity, bias=nm[:, r, n, c:c + 1], scale=rs[:, r, n, c:c + 1])
                last.then_inc(done, 1)

            def step(i, half, r, project, attend, settle, norm, route, place):
                if project or norm or route:
                    act.wait_ge(nm_s, i + 1)
                if norm:
                    b = i - 3
                    wait_past(act, h2m_s, b)
                    normalise(lambda c: xn2[:, c, :], rows(b), r, 1, xn2_s)
                if project:
                    act.wait_ge(got_x[r], 16 * half + 16)
                    wait_past(act, xT_s, i)
                    normalise(lambda c: xc[:, c, :], rows(i), r, 0, xc_s)
                if project and r == 1:
                    act.wait_ge(b1p_s, half + 1)
                    wait_past(act, b1_out, 32 * half)
                    hold(act, "act")
                    a.activation(b1row[0], Q[0:1, :], ACT.Copy)
                    a.activation(b1row[1], V[0:1, :], ACT.Copy).then_inc(b1r_s, 1)
                if project:
                    act.wait_ge(xT_s, i + 1)
                    act.wait_ge(modc_s, i + 1)
                    wait_past(act, proj_s, i)
                    hold(act, "act")
                    for k in range(NK):
                        last = a.activation(hT[:, k, :], TR[k][:, :], ACT.Identity,
                                            bias=modc[:, r, 2 + k:3 + k], scale=modc[:, r, k:k + 1])
                    last.then_inc(hT_s, 1)
                if attend:
                    b = i - 1
                    act.wait_ge(score_s, b + 1)
                    wait_past(act, pv_s, b)
                    for s in range(NC):
                        last = a.activation(pt[:, PO[s]:PO[s] + PW[s]],
                                            S[2][:, 256:384] if s == 3 else S[s][:, 0:PW[s]], ACT.Copy)
                    last.then_inc(strip_s, 1)
                if route:
                    b = i - 4
                    if not isinstance(i, int) or b >= 2:
                        act.wait_ge(scat[r], 16 * 2 * NC * (half - 2))
                    normalise(lambda c: nrm[:, r, c, 0:D], lambda c: h2[r][:, c, :], r, 2, nrm_s)
                if place:
                    b = i - 5
                    act.wait_ge(dl_s, b + 1)
                    wait_past(act, w1_s, b)
                    a.activation(dex[:, :], dl[:, :], ACT.Exp).then_inc(dex_s, 1)
                if project and r == 1:
                    a.activation(wbuf[:, 0, 4096:6144], w2f, ACT.Copy).then_inc(head_s, 1)
                if project:
                    act.wait_ge(proj_s, i + 1)
                    wait_past(act, phi_s, i)
                    a.activation(ex[:, :], Q[:, :], ACT.Relu, scale=-1.0).then_inc(exn_s, 1)
                    wait_past(act, score_s, i - 1)
                    a.activation(vT[:, r, :], V[0:H, :], ACT.Copy).then_inc(vT_s, 1)
                    act.wait_ge(exn_s, i + 1)
                    a.activation(ex[:, :], ex[:, :], ACT.Exp, scale=-1.0).then_inc(ex_s, 1)
                if attend:
                    b = i - 1
                    act.wait_ge(pv_s, b + 1)
                    wait_past(act, owo_s, b)
                    a.activation(oT[:, :], O[0:H, :], ACT.Copy).then_inc(oT_s, 1)
                if route:
                    b = i - 4
                    act.wait_ge(nTp_s, b + 1)
                    act.wait_ge(small_s, i - 1)
                    for k in range(NK):
                        last = a.activation(nT[:, k, :], TR[k][:, :], ACT.Copy)
                    last.then_inc(nT_s, 1)
                if project:
                    act.wait_ge(ktr_s, i + 1)
                    wait_past(act, pv_s, i - 1)
                    a.activation(ktok[:, r, :, :].rearrange("p c h -> p (c h)"), V[:, 0:NC * H], ACT.Copy).then_inc(ktok_s, 1)
                if project and r == 0:
                    act.wait_ge(got_we, 32 * half + 32)
                    act.wait_ge(lge_s, half + 1)
                    wait_past(act, split_out, 16 * half)
                    hold(act, "act")
                    for k in range(NK):
                        a.activation(wbuf[:, 0, k * 1024:(k + 1) * 1024], w1f[:, k, :], ACT.Copy,
                                     scale=lge[:, k:k + 1]).then_inc(head_s, 1)

            pipeline(a, step)

            def gelu(j, half, r):
                act.wait_ge(got_b1[r], 16 * half + 16)
                for c in range(NI):
                    act.wait_ge(mm1_s, NI * j + c + 1)
                    wait_past(act, gl_s, NI * j + c - 1)
                    a.activation(gf[:, c % 2, :], MM[c % 2][:, 0:TOK], ACT.Gelu, bias=b1t[:, r, c:c + 1]).then_inc(gf_s, 1)

            for j in range(2):
                gelu(j, 0, j)
            with a.Fori(1, TILES // 2) as h:
                for r in range(2):
                    gelu(2 * h + r, h, r)
            for j in range(TILES // 2 * 2, TILES):
                gelu(j, j // 2, j % 2)

            def weigh(b, turn, r):
                act.wait_ge(got_ya[r], 16 * turn + 16)
                hold(act, "act")
                for c in range(NC):
                    last = a.activation(ya[:, r, c, :], ya[:, r, c, :], ACT.Copy, scale=w_all[:, ds(NC * b + c, 1), 0])
                last.then_inc(ca_s, 1)

            with a.Fori(0, NB // R) as h:
                for r in range(R):
                    weigh(R * h + r, h, r)

        @block.vector
        def _(dve):
            v = nc.vector
            setc = [0]

            def chain(ins, s=None):
                setc[0] += 1
                ins.then_inc(set_step, 1)
                dve.wait_ge(set_step, setc[0])

            v.memset(mv[:, :, :, :], 0.0).then_inc(stat_set, 1)
            v.memset(nrm[:, :, :, :], 0.0).then_inc(stat_set, 1)
            dve.wait_ge(c_exp, 1)
            chain(v.tensor_scalar_add(cex[:, :], cex[:, :], 1.0))
            chain(v.reciprocal(cex[:, :], cex[:, :]))
            v.tensor_tensor(cin[:, :], cin[:, :], cex[:, :], ALU.mult).then_inc(c_step, 1)
            dve.wait_ge(cT_ps, 1)
            v.tensor_copy(cT[:, :, :], Q[:, 0:NK * NB].rearrange("p (k b) -> p k b", k=NK)).then_inc(cT_sb, 1)
            dve.wait_ge(mod_ps, 1)
            for s in range(3):
                v.tensor_copy(mod[:, s * 512:(s + 1) * 512], S[s][0:NB, :]).then_inc(mod_step, 1)
            dve.wait_ge(mod_step, 3)
            v.tensor_scalar_add(mod[:, CA * D:(CA + 1) * D], mod[:, CA * D:(CA + 1) * D], 1.0).then_inc(mod_step, 1)
            v.tensor_scalar_add(mod[:, CB * D:(CB + 1) * D], mod[:, CB * D:(CB + 1) * D], 1.0).then_inc(mod_step, 1)
            for n, sel in enumerate((GA, GB)):
                gg = mod[:, sel * D:(sel + 1) * D]
                chain(v.tensor_scalar(gneg[:, :], gg, -1.0, None, ALU.mult))
                chain(v.tensor_tensor(gneg[:, :], gneg[:, :], gg, ALU.max))
                chain(v.tensor_scalar(gneg[:, :], gneg[:, :], 0.25, None, ALU.max))
                chain(v.tensor_scalar(gsgn[:, :], gg, 0.0, 2.0, ALU.is_ge, ALU.mult))
                chain(v.scalar_tensor_tensor(gg, gsgn[:, :], -1.0, gneg[:, :], ALU.add, ALU.mult))
            chain(v.tensor_copy(gneg[:, 0:1], gsgn[:, 0:1]))
            v.tensor_copy(gsgn[:, 1:2], gneg[:, 0:1]).then_inc(mod_step, 3)
            dve.wait_ge(modT_ps, 1)
            v.tensor_copy(modT[:, :, :].rearrange("p b s -> p s b"),
                          Q[:, 64:64 + 4 * NB].rearrange("p (s b) -> p s b", b=NB)).then_inc(set_step, 1)
            setc[0] += 1
            dve.wait_ge(vec_ps, 1)
            chain(v.tensor_copy(vecs[:, :], V[:, 0:NVEC]))
            chain(v.tensor_copy(rT[:, :, :], V[:, 128:128 + NK * E].rearrange("p (k e) -> p k e", k=NK)))
            chain(v.tensor_copy(lngb[:, :, 0:2], vecs[:, VEC_G:VEC_B].rearrange("p (e k) -> p e k", k=NK)))
            chain(v.tensor_copy(lngb[:, :, 2:4], vecs[:, VEC_B:VEC_RG].rearrange("p (e k) -> p e k", k=NK)))
            dve.wait_ge(consts, 13)
            for k in range(NK):
                chain(v.tensor_scalar(rTg[:, k, :], rT[:, k, :], vecs[:, VEC_RG + k:VEC_RG + k + 1], None, ALU.mult))
                chain(v.tensor_scalar(rnbb[:, k, :], onesf[:, 0:P], vecs[:, VEC_RB + k:VEC_RB + k + 1], None, ALU.mult))
            chain(v.tensor_copy(base[:, :], offs[:, :]))
            v.tensor_copy(ef[:, 0, 0:1], base[:, 0:1]).then_inc(base_set, 1)
            dve.wait_ge(rb_ps, 1)
            dve.wait_ge(got_r, 32)
            dve.wait_ge(base_set, 1)
            v.tensor_tensor(rbias[:, :], rbias[:, :], V[:, 256:256 + E], ALU.add).then_inc(setup_done, 1)
            dve.wait_ge(setup_done, 1)

            def rows(b):
                return lambda c: resid[:, b * NC + c, :] if isinstance(b, int) else resid[:, ds(b * NC + c, 1), :]

            sets = [0]

            def stats(src, n, k):
                for c in range(NC):
                    last = v.bn_stats(st[:, c, :], src(c))
                last.then_inc(st_s, 1)
                dve.wait_ge(st_s, k + 1)
                hold(dve, "dve")
                for c in range(NC):
                    last = v.bn_aggr(mv[:, n, c, :], st[:, c, :])
                last.then_inc(mv_s, 1)
                dve.wait_ge(mv_s, k + 1)

            def var_eps(i):
                v.tensor_scalar(ve[:, :, :], mv[:, :, :, 1], EPS, None, ALU.add).then_inc(ve_s, 1)

            def stats_before(i):
                if not isinstance(i, int):
                    return 3 * i - 4
                return min(i + 1, NB) + min(max(i - 2, 0), NB) + min(max(i - 3, 0), NB)

            def neg_mean_rstd(i, r):
                dve.wait_ge(rs_s, i + 1)
                wait_past(dve, xc_s, upto(i - 1))
                wait_past(dve, xn2_s, upto(i - 4))
                wait_past(dve, nrm_s, upto(i - 5))
                hold(dve, "dve")
                v.scalar_tensor_tensor(nm[:, r, :, :], mv[:, :, :, 0], -1.0, rs[:, r, :, :], ALU.mult, ALU.mult).then_inc(nm_s, 1)

            v.tensor_copy(lge[:, :], lngb[:, 0, :]).then_inc(lge_s, 1)
            dve.wait_ge(stat_set, 2)
            dve.wait_ge(got_x[0], 16)
            stats(rows(0), 0, 0)
            var_eps(0)
            neg_mean_rstd(0, 0)

            def step(i, half, r, project, attend, settle, norm, route, place):
                taken = stats_before(i)
                if project:
                    wait_past(dve, hT_s, i - 1)
                    hold(dve, "dve")
                    v.tensor_copy(modc[:, r, :], modT[:, i, :] if isinstance(i, int) else modT[:, ds(i, 1), :]).then_inc(modc_s, 1)
                dve.wait_ge(nm_s, i + 1 if not isinstance(i, int) else min(i + 1, NB + 4))
                if settle:
                    dve.wait_ge(x2_s, i - 1)
                    hold(dve, "dve")
                    stats(rows(i - 2), 1, taken)
                    taken = taken + 1
                if project and not (isinstance(i, int) and i == NB - 1):
                    if r == 0:
                        dve.wait_ge(got_x[1], 16 * half + 16)
                    else:
                        dve.wait_ge(got_x[0], 16 * half + 32)
                    hold(dve, "dve")
                    stats(rows(i + 1), 0, taken)
                    taken = taken + 1
                if project and r == 1:
                    dve.wait_ge(head_s, 3 * half + 2)
                    hold(dve, "dve")
                    for k in range(NK):
                        v.scalar_tensor_tensor(wbuf[:, 0, 2048 + k * 1024:2048 + (k + 1) * 1024], w1f[:, k, :], lge[:, k:k + 1],
                                               wbuf[:, 0, k * 1024:(k + 1) * 1024], ALU.mult, ALU.subtract).then_inc(rest_s, 1)
                if place:
                    slots(i - 5, 1 - r)
                if attend:
                    b = i - 1
                    dve.wait_ge(strip_s, b + 1)
                    diag = pt[:, :].rearrange("p (a t) -> p a t", a=NC)[:, :, 0:P]
                    v.tensor_tensor(diag, diag, causal[:, :].unsqueeze(1).to_broadcast([P, NC, P]), ALU.mult).then_inc(diag_s, 1)
                if norm and not project and not attend:
                    b, q = i - 3, 1 - r
                    dve.wait_ge(got_cs[q], 16 * (b // 2 + 1))
                    dve.wait_ge(xn2_s, b + 1)
                    dve.wait_ge(nrm_s, b - 1)
                    v.tensor_tensor(h2[q], xn2, csB[:, q, D:2 * D].unsqueeze(1).to_broadcast([P, NC, D]), ALU.mult).then_inc(h2m_s, 1)
                    dve.wait_ge(h2m_s, b + 1)
                    v.tensor_tensor(h2[q], h2[q], csB[:, q, 0:D].unsqueeze(1).to_broadcast([P, NC, D]), ALU.add).then_inc(h2_s, 1)
                if norm:
                    dve.wait_ge(h2_s, i - 2)
                    hold(dve, "dve")
                    stats(lambda c: h2[1 - r][:, c, :], 2, taken)
                if project or attend or norm:
                    var_eps(i + 1)
                if place:
                    weights(i - 5)
                if project:
                    dve.wait_ge(ex_s, i + 1)
                    wait_past(dve, score_s, i - 1)
                    wait_past(dve, ktr_s, i - 1)
                    v.scalar_tensor_tensor(qk[:, r, :], Q[:, :], 1.0, ex[:, :], ALU.add, ALU.max).then_inc(phi_s, 1)
                    dve.wait_ge(phi_s, i + 1)
                    wait_past(dve, qz_s, i)
                    v.tensor_tensor_scan(zT[:, :], onesf[H:2 * H, :], qk[H:2 * H, r, :], 0.0, ALU.mult, ALU.add).then_inc(scan_s, 1)
                    dve.wait_ge(scan_s, i + 1)
                    v.tensor_tensor(qz[:, r, :], qk[0:H, r, :], zT[:, :], ALU.mult).then_inc(qz_s, 1)
                if project or attend or norm:
                    neg_mean_rstd(i + 1, 1 - r)
                if project and r == 1:
                    dve.wait_ge(head_s, 3 * half + 3)
                    hold(dve, "dve")
                    v.tensor_tensor(wbuf[:, 0, 6144:8192], w2f, wbuf[:, 0, 4096:6144], ALU.subtract).then_inc(rest_s, 1)
                if attend or route:
                    dve.wait_ge(small_s, i)
                    if attend:
                        v.tensor_scalar(den[:, :], DEN, 1e-6, None, ALU.max).then_inc(dmax_s, 1)
                    if route:
                        wait_past(dve, ix_s, i - 4)
                        v.tensor_tensor(lg[:, :, :], LOG.rearrange("p (c e) -> p c e", c=NC),
                                        rbias[:, :].unsqueeze(1).to_broadcast([P, NC, E]), ALU.add).then_inc(lg_s, 1)
                    if attend:
                        dve.wait_ge(dmax_s, i)
                    if route:
                        dve.wait_ge(lg_s, i - 3)
                    dve.sem_inc(small_read, 1)
                if attend:
                    b = i - 1
                    wait_past(dve, x2_s, b)
                    v.reciprocal(rden[:, :], den[:, :]).then_inc(rden_s, 1)
                    dve.wait_ge(owo_s, b + 1)
                    dve.wait_ge(rden_s, b + 1)
                    for c in range(NC):
                        last = v.scalar_tensor_tensor(rows(b)(c), S[c // 2][:, (c % 2) * D:(c % 2 + 1) * D],
                                                      rden[:, c:c + 1], rows(b)(c), ALU.mult, ALU.add)
                    last.then_inc(x2_s, 1)
                if route:
                    choose(i - 4, r)
                if project and r == 1 and not (isinstance(i, int) and i == NB - 1):
                    dve.wait_ge(rest_s, 3 * half + 2)
                    dve.wait_ge(b1p_s, half + 1)
                    hold(dve, "dve")
                    v.tensor_copy(lge[:, :], lngb[:, half + 1, :] if isinstance(half, int) else lngb[:, ds(half + 1, 1), :]).then_inc(lge_s, 1)

            def cols(t, b):
                return t[:, b * NC:(b + 1) * NC, :] if isinstance(b, int) else t[:, ds(b * NC, NC), :]

            def choose(b, q):
                wait_past(dve, dex_s, b)
                hold(dve, "dve")
                for c in range(NC):
                    last = v.max(mx[:, c, :], lg[:, c, :])
                last.then_inc(mx_s, 1)
                dve.wait_ge(mx_s, b + 1)
                v.tensor_tensor(dl[:, :], mx[:, :, 1], mx[:, :, 0], ALU.subtract).then_inc(dl_s, 1)
                for c in range(NC):
                    last = v.max_index(ix[:, c, :], mx[:, c, :], lg[:, c, :])
                last.then_inc(ix_s, 1)
                dve.wait_ge(ix_s, b + 1)
                v.tensor_copy(ef[:, :, :], ix[:, :, 0:2]).then_inc(ef_s, 1)
                dve.wait_ge(ef_s, b + 1)
                dve.wait_ge(pick_s, b) if not isinstance(b, int) or b > 0 else None
                for t in range(2):
                    last = v.tensor_tensor(oh[:, t, :, :], experts[:, :].unsqueeze(1).to_broadcast([P, NC, E]),
                                           ef[:, :, t:t + 1].to_broadcast([P, NC, E]), ALU.is_equal)
                last.then_inc(oh_s, 1)
                dve.wait_ge(oh_s, b + 1)
                v.tensor_tensor(ohs[:, :, :], oh[:, 0, :, :], oh[:, 1, :, :], ALU.add).then_inc(ohs_s, 1)
                v.tensor_scalar(token[:, :], token[:, :], float(T), None, ALU.add).then_inc(tok_s, 1)
                v.tensor_copy(nrm[:, q, :, D + 1], ef[:, :, 0])
                dve.wait_ge(tok_s, b + 2)
                hold(dve, "dve")
                v.tensor_copy(nrm[:, q, :, D], token[:, :])

            def weights(b):
                dve.wait_ge(dex_s, b + 1)
                v.tensor_scalar(d1[:, :], dex[:, :], 1.0, None, ALU.add).then_inc(d1_s, 1)
                dve.wait_ge(d1_s, b + 1)
                v.reciprocal(d1[:, :], d1[:, :]).then_inc(w0_s, 1)
                dve.wait_ge(w0_s, b + 1)
                hold(dve, "dve")
                v.tensor_copy(cols(w_all, b)[:, :, 0], d1[:, :])
                v.tensor_tensor(cols(w_all, b)[:, :, 1], d1[:, :], dex[:, :], ALU.mult).then_inc(w1_s, 1)

            def slots(b, q):
                dve.wait_ge(rank_s, b + 1)
                wait_past(dve, base_s, b)
                hold(dve, "dve")
                v.tensor_copy(rt[:, :], RT).then_inc(rt_s, 1)
                dve.wait_ge(rt_s, b + 1)
                v.tensor_tensor(cnt[:, :, :], rt[:, 0:NC * E].rearrange("p (c e) -> p c e", c=NC),
                                base[:, :].unsqueeze(1).to_broadcast([P, NC, E]), ALU.add).then_inc(cnt_s, 1)
                dve.wait_ge(cnt_s, b + 1)
                v.tensor_tensor(base[:, :], base[:, :], rt[:, NC * E:NC * E + E], ALU.add).then_inc(base_s, 1)
                for t in range(2):
                    last = v.tensor_tensor(pick[:, t, :, :], oh[:, t, :, :], cnt[:, :, :], ALU.mult)
                last.then_inc(pick_s, 1)
                dve.wait_ge(pick_s, b + 1)
                hold(dve, "dve")
                for t in range(2):
                    last = v.tensor_reduce(slotf[:, :, t], pick[:, t, :, :], axis=AX.X, op=ALU.add)
                last.then_inc(slotf_s, 1)
                dve.wait_ge(slotf_s, b + 1)
                v.tensor_copy(slot[:, q, :, :], slotf[:, :, :]).then_inc(slot_s, 1)

            pipeline(v, step)

            tc = [0]

            def tchain(ins):
                tc[0] += 1
                ins.then_inc(tstep, 1)
                dve.wait_ge(tstep, tc[0])

            dve.wait_ge(base_s, NB)
            tchain(v.tensor_copy(padrow[:, :], base[:, :]))
            v.tensor_copy(counti[:, :], padrow[:, :]).then_inc(tab_s, 1)
            tchain(v.tensor_tensor(count[:, :], base[:, :], offs[:, :], ALU.subtract))
            tchain(v.tensor_tensor(need[:, :, :], count[:, :].unsqueeze(2).to_broadcast([P, E, MAXT]), steps[:, :, :], ALU.is_gt))
            dve.wait_ge(b1v_ps, 1)
            v.tensor_tensor(b1f[:, :, :].rearrange("p e i -> p (e i)"), vecs[:, VEC_B1:VEC_G], V[:, 0:E * NI], ALU.add).then_inc(b1f_s, 1)
            tchain(v.tensor_reduce(ntile[:, :], need[:, :, :], axis=AX.X, op=ALU.add))
            tchain(v.tensor_tensor_scan(tend[:, :], onesf[:, 0:E], ntile[:, :], 0.0, ALU.mult, ALU.add))
            tchain(v.tensor_tensor(tstart[:, :], tend[:, :], ntile[:, :], ALU.subtract))
            tchain(v.scalar_tensor_tensor(delta[:, :], tstart[:, :], float(TOK), offs[:, :], ALU.mult, ALU.subtract))
            tchain(v.tensor_tensor(ge[:, :, :], tid[:, :, :], tend[:, :].unsqueeze(1).to_broadcast([P, TILES, E]), ALU.is_ge))
            tchain(v.tensor_tensor(hop[:, 0:E - 1], delta[:, 1:E], delta[:, 0:E - 1], ALU.subtract))
            tchain(v.tensor_tensor(hop[:, E - 1:E], delta[:, 0:1], delta[:, 0:1], ALU.subtract))
            tchain(v.tensor_reduce(tab_e[:, :], ge[:, :, :], axis=AX.X, op=ALU.add))
            tchain(v.tensor_scalar(tab_e[:, :], tab_e[:, :], float(E - 1), None, ALU.min))
            tchain(v.tensor_tensor(gs[:, :, :], ge[:, :, :], hop[:, :].unsqueeze(1).to_broadcast([P, TILES, E]), ALU.mult))
            tchain(v.tensor_reduce(tab_r[:, :], gs[:, :, :], axis=AX.X, op=ALU.add))
            tchain(v.scalar_tensor_tensor(tab_r[:, :], tid[:, :, 0], float(TOK), tab_r[:, :], ALU.mult, ALU.subtract))
            tchain(v.tensor_scalar(tab_d[:, :], tab_r[:, :], -1.0, float(DUMMY), ALU.mult, ALU.add))
            tchain(v.tensor_tensor(tab_d[:, :], tab_d[:, :], ge[:, :, E - 1], ALU.mult))
            tchain(v.tensor_tensor(tab_r[:, :], tab_r[:, :], tab_d[:, :], ALU.add))
            tchain(v.tensor_copy(table[:, 0, :], tab_e[:, :]))
            tchain(v.tensor_copy(table[:, 1, :], tab_r[:, :]))
            tchain(v.memset(table[:, 2, 0:2], 1))
            v.tensor_tensor(table[:, 2, 2:TILES], tab_e[:, 2:TILES], tab_e[:, 0:TILES - 2], ALU.not_equal).then_inc(tab_s, 1)
            dve.wait_ge(tab_s, 2)

            def split_rows(j, half, r):
                dve.wait_ge(tr_s, j + 1)
                wait_past(dve, mm1_s, NI * (j - 1))
                both = TR[r][:, :].rearrange("p (k n) -> p k n", k=NK)
                v.tensor_copy(nh[:, r, :, :], both).then_inc(nh_s, 1)
                dve.wait_ge(nh_s, j + 1)
                v.tensor_tensor(nl[:, r, :, :], both, nh[:, r, :, :], ALU.subtract).then_inc(nl_s, 1)
                if not isinstance(j, int) or j >= 2:
                    dve.wait_ge(y_out[r], 16 * TH * half)
                hold(dve, "dve")
                v.tensor_scalar(ydf[:, r, :], xin[:, r, :, D + 1], tab_e[:, ds(j, 1)], float(NTOK), ALU.not_equal, ALU.mult)
                v.tensor_scalar(ydp[:, r, :], xin[:, r, :, D + 1], -1.0, float(TOK * r), ALU.is_equal, ALU.mult).then_inc(yd_a, 1)
                dve.wait_ge(yd_a, j + 1)
                v.tensor_tensor(ydf[:, r, :], ydf[:, r, :], ydp[:, r, :], ALU.add).then_inc(yd_b, 1)
                dve.wait_ge(yd_b, j + 1)
                v.tensor_tensor(ydst[:, r, :], ydf[:, r, :], xin[:, r, :, D], ALU.add).then_inc(yd_s, 1)

            def evacuate(j, half, r):
                dve.wait_ge(mm2_s, NI * j + NI)
                dve.wait_ge(got_b2[r], 16 * half + 16)
                if not isinstance(j, int) or j >= 2:
                    dve.wait_ge(y_out[r], 16 * TH * half)
                for h in range(TH):
                    last = v.tensor_tensor(yt[:, r, h, :], ACC[r][h][:, 0:D], b2t[:, r, :], ALU.add)
                last.then_inc(yt_s, 1)

            def tile(j, half, r, first, last_tile):
                for c in range(NI):
                    n = NI * j + c
                    dve.wait_ge(gf_s, n + 1)
                    wait_past(dve, mm2_s, n - 3)
                    v.tensor_copy(gh[:, c % 4, :], gf[:, c % 2, :]).then_inc(gh_s, 1)
                    dve.wait_ge(gh_s, n + 1)
                    v.tensor_tensor(gl[:, c % 4, :], gf[:, c % 2, :], gh[:, c % 4, :], ALU.subtract).then_inc(gl_s, 1)
                    if c == 1 and not first:
                        evacuate(j - 1, half - 1 + r, 1 - r)
                    if c == 5 and not last_tile:
                        split_rows(j + 1, half + r, 1 - r)

            split_rows(0, 0, 0)
            tile(0, 0, 0, True, False)
            for j in range(1, 3):
                tile(j, j // 2, j % 2, False, False)
            with v.Fori(1, (TILES - 1) // 2 - 1) as h:
                tile(2 * h + 1, h, 1, False, False)
                tile(2 * h + 2, h + 1, 0, False, False)
            for j in range((TILES - 1) // 2 * 2 - 1, TILES):
                tile(j, j // 2, j % 2, False, j == TILES - 1)
            evacuate(TILES - 1, (TILES - 1) // 2, (TILES - 1) % 2)

            def mix(b, turn, r):
                dve.wait_ge(ca_s, b + 1)
                dve.wait_ge(got_yb[r], 16 * turn + 16)
                hold(dve, "dve")
                for c in range(NC):
                    last = v.scalar_tensor_tensor(ya[:, r, c, :], yb[:, r, c, :], w_all[:, ds(NC * b + c, 1), 1],
                                                  ya[:, r, c, :], ALU.mult, ALU.add)
                last.then_inc(cb_s, 1)

            def add(b, r):
                dve.wait_ge(cc_s, b + 1)
                hold(dve, "dve")
                v.tensor_tensor(resid[:, ds(NC * b, NC), :], ya[:, r, :, :], resid[:, ds(NC * b, NC), :], ALU.add).then_inc(res_s, 1)

            mix(0, 0, 0)
            with v.Fori(0, NB // R - 1) as h:
                for r in range(R):
                    mix(R * h + r + 1, h if r + 1 < R else h + 1, (r + 1) % R)
                    add(R * h + r, r)
            for b in range(NB - R, NB):
                if b + 1 < NB:
                    mix(b + 1, NB // R - 1, (b + 1) % R)
                add(b, b % R)

        @block.tensor
        def _(pe):
            t = nc.tensor
            pe.wait_ge(consts, 13)
            pe.wait_ge(c_step, 1)
            for k in range(NK):
                last = t.transpose(Q[:, k * NB:(k + 1) * NB], cin[:, k * P:(k + 1) * P], ident[0:NB, 0:NB])
            last.then_inc(cT_ps, 1)
            pe.wait_ge(cT_sb, 1)
            pe.wait_ge(got_wmod, 16)
            for s in range(3):
                for k in range(NK):
                    last = t.matmul(S[s][0:NB, :], cT[:, k, :], wmod[:, k, s * 512:(s + 1) * 512], start=k == 0, stop=k == NK - 1)
            last.then_inc(mod_ps, 1)
            pe.wait_ge(mod_step, 8)
            for n, (sel, k) in enumerate(((CA, 0), (CA, 1), (SA, 0), (SA, 1))):
                last = t.transpose(Q[:, 64 + n * NB:64 + (n + 1) * NB], mod[:, sel * D + k * P:sel * D + (k + 1) * P], ident[0:NB, 0:NB])
            last.then_inc(modT_ps, 1)
            pe.wait_ge(got_vec, 80)
            pe.wait_ge(got_r, 32)
            t.transpose(V[:, 0:NVEC], vrow[:, :], ident[0:NVEC, 0:NVEC])
            for k in range(NK):
                last = t.transpose(V[:, 128 + k * E:128 + (k + 1) * E], rrow[:, k * P:(k + 1) * P], ident[0:E, 0:E])
            last.then_inc(vec_ps, 1)
            pe.wait_ge(base_set, 1)
            for k in range(NK):
                last = t.matmul(V[:, 256:256 + E], rnbb[:, k, :], rT[:, k, :], start=k == 0, stop=k == NK - 1)
            last.then_inc(rb_ps, 1)
            pe.wait_ge(got_w, 64)
            pe.wait_ge(setup_done, 1)

            def step(i, half, r, project, attend, settle, norm, route, place):
                if project and r == 1:
                    pe.wait_ge(got_we, 32 * half + 32)
                    pe.wait_ge(lge_s, half + 1)
                    pe.wait_ge(phi_s, i)
                    pe.wait_ge(ktok_s, i)
                    hold(pe, "pe")
                    for n, row in enumerate((Q, V)):
                        for k in range(NK):
                            last = t.matmul(row[0:1, :], lge[:, 2 + k:3 + k], w1f[:, k, n * 512:(n + 1) * 512], start=k == 0, stop=k == NK - 1)
                    last.then_inc(b1p_s, 1)
                if project:
                    pe.wait_ge(xc_s, i + 1)
                    wait_past(pe, nT_s, i - 4)
                    for k in range(NK):
                        for c in range(NC):
                            last = t.transpose(TR[k][:, c * P:(c + 1) * P], xc[:, c, k * P:(k + 1) * P], ident[:, :])
                    last.then_inc(xT_s, 1)
                if attend:
                    b, q = i - 1, 1 - r
                    pe.wait_ge(phi_s, b + 1)
                    pe.wait_ge(vT_s, b + 1)
                    wait_past(pe, x2_s, b)
                    wait_past(pe, small_read, i - 1)
                    for s in range(NC):
                        dst = S[2][:, 256:384] if s == 3 else S[s][:, 0:PW[s]]
                        last = t.matmul(dst, vT[:, q, s * P:(s + 1) * P], qk[0:H, q, s * P:T], start=True, stop=True)
                    last.then_inc(score_s, 1)
                if place:
                    b = i - 5
                    pe.wait_ge(ohs_s, b + 1)
                    pe.wait_ge(oT_s, upto(i - 1))
                    flat = ohs[:, :, :].rearrange("p c e -> p (c e)")
                    t.matmul(RANK, before[:, :], flat, start=True, stop=False)
                    for back in range(1, NC):
                        t.matmul(O[:, back * E:NC * E], allone[:, :], flat[:, 0:(NC - back) * E], start=False, stop=back == NC - 1)
                    for c in range(NC):
                        last = t.matmul(TOT, allone[:, :], flat[:, c * E:(c + 1) * E], start=c == 0, stop=c == NC - 1)
                    last.then_inc(rank_s, 1)
                if project:
                    pe.wait_ge(hT_s, i + 1)
                    if r == 0:
                        wait_past(pe, phi_s, i)
                        wait_past(pe, ktok_s, i)
                    else:
                        pe.wait_ge(b1r_s, half + 1)
                    for k in range(NK):
                        t.matmul(Q[:, :], wqk[:, k, :], hT[:, k, :], start=k == 0, stop=k == NK - 1)
                    for k in range(NK):
                        last = t.matmul(V[0:H, :], wv[:, k, :], hT[:, k, :], start=k == 0, stop=k == NK - 1)
                    last.then_inc(proj_s, 1)
                if attend:
                    b, q = i - 1, 1 - r
                    pe.wait_ge(diag_s, b + 1)
                    pe.wait_ge(ktok_s, b + 1)
                    wait_past(pe, oT_s, b)
                    if place:
                        pe.wait_ge(rt_s, i - 4)
                    for s in range(NC):
                        last = t.matmul(O[0:H, s * P:T], ktok[:, q, s, :], pt[:, PO[s]:PO[s] + PW[s]], start=s == 0, stop=s == NC - 1)
                    last.then_inc(pv_s, 1)
                if route:
                    b = i - 4
                    pe.wait_ge(nrm_s, b + 1)
                    wait_past(pe, hT_s, i + 1 if project else NB)
                    wait_past(pe, nT_s, b)
                    for k in range(NK):
                        for c in range(NC):
                            last = t.transpose(TR[k][:, c * P:(c + 1) * P], nrm[:, r, c, k * P:(k + 1) * P], ident[:, :])
                    last.then_inc(nTp_s, 1)
                if project:
                    pe.wait_ge(phi_s, i + 1)
                    pe.wait_ge(vT_s, i + 1)
                    hold(pe, "pe")
                    for c in range(NC):
                        last = t.transpose(V[:, c * H:(c + 1) * H], qk[H:2 * H, r, c * P:(c + 1) * P], ident[H:2 * H, H:2 * H])
                    last.then_inc(ktr_s, 1)
                if attend:
                    b, q = i - 1, 1 - r
                    pe.wait_ge(qz_s, i)
                    pe.wait_ge(strip_s, i)
                    for c in range(NC):
                        small = t.matmul(DEN[:, c:c + 1], qz[:, q, c * P:(c + 1) * P], onesf[0:H, 0:1], start=True, stop=True)
                    if not route:
                        small.then_inc(small_s, 1)
                    pe.wait_ge(oT_s, b + 1)
                    pe.wait_ge(wog_s, b + 1)
                    for c in range(NC):
                        last = t.matmul(S[c // 2][:, (c % 2) * D:(c % 2 + 1) * D], oT[:, c * P:(c + 1) * P], wog[:, q, :], start=True, stop=True)
                    last.then_inc(owo_s, 1)
                if route:
                    b = i - 4
                    if not attend:
                        pe.wait_ge(small_read, i - 1)
                    pe.wait_ge(nT_s, b + 1)
                    for c in range(NC):
                        for k in range(NK):
                            small = t.matmul(LOG[:, c * E:(c + 1) * E], nT[:, k, c * P:(c + 1) * P], rTg[:, k, :], start=k == 0, stop=k == NK - 1)
                    small.then_inc(small_s, 1)

            pipeline(t, step)
            pe.wait_ge(got_b1v, 16)
            t.transpose(V[:, 0:E * NI], vrow[0:E * NI, :], ident[0:E * NI, 0:E * NI]).then_inc(b1v_ps, 1)

            def turn(j, half, r):
                pe.wait_ge(got_xin[r], 16 * half + 16)
                wait_past(pe, nl_s, j - 1)
                for k in range(NK):
                    for h in range(TH):
                        last = t.transpose(TR[r][:, k * TOK + h * P:k * TOK + (h + 1) * P], xin[:, r, h, k * P:(k + 1) * P], ident[:, :])
                last.then_inc(tr_s, 1)

            def first(j, r, c):
                wait_past(pe, gf_s, NI * j + c - 1)
                n = 0
                for k in range(NK):
                    head = wbuf[:, r, k * I + c * P:k * I + (c + 1) * P]
                    rest = wbuf[:, r, 2048 + k * I + c * P:2048 + k * I + (c + 1) * P]
                    for w, m in ((head, nh), (head, nl), (rest, nh)):
                        last = t.matmul(MM[c % 2][:, 0:TOK], w, m[:, r, k, :], start=n == 0, stop=n == 5)
                        n += 1
                last.then_inc(mm1_s, 1)

            def second(j, r, c):
                pe.wait_ge(gl_s, NI * j + c + 1)
                head = wbuf[:, r, 4096 + c * D:4096 + (c + 1) * D]
                rest = wbuf[:, r, 6144 + c * D:6144 + (c + 1) * D]
                for h in range(TH):
                    n = 0
                    for g, w in ((gh, head), (gh, rest), (gl, head)):
                        last = t.matmul(ACC[r][h][:, 0:D], g[:, c % 4, h * P:(h + 1) * P], w,
                                        start=c == 0 and n == 0, stop=c == NI - 1 and n == 2)
                        n += 1
                last.then_inc(mm2_s, 1)

            def tile(j, half, r, is_first, is_last):
                pe.wait_ge(nl_s, j + 1)
                pe.wait_ge(got_w1[r], 16 * half + 16)
                for c in range(NI):
                    first(j, r, c)
                    if c >= 2:
                        if c == 2:
                            pe.wait_ge(got_w2[r], 16 * half + 16)
                            wait_past(pe, yt_s, j - 1)
                        second(j, r, c - 2)
                    elif not is_first:
                        second(j - 1, 1 - r, NI - 2 + c)
                    if c == 4 and not is_last:
                        turn(j + 1, half + r, 1 - r)

            turn(0, 0, 0)
            for j in range(3):
                tile(j, j // 2, j % 2, j == 0, False)
            with t.Fori(1, (TILES - 1) // 2 - 1) as h:
                tile(2 * h + 1, h, 1, False, False)
                tile(2 * h + 2, h + 1, 0, False, False)
            for j in range((TILES - 1) // 2 * 2 - 1, TILES):
                tile(j, j // 2, j % 2, False, j == TILES - 1)
            second(TILES - 1, (TILES - 1) % 2, NI - 2)
            second(TILES - 1, (TILES - 1) % 2, NI - 1)


_INS = ['L0_attn_x', 'L0_attn_W_q', 'L0_attn_W_k', 'L0_attn_W_v', 'L0_attn_W_o', 'L0_ffn_rn_g', 'L0_ffn_rn_b',
        'L0_ffn_router_w', 'L0_ffn_router_b', 'L0_ffn_ln_g', 'L0_ffn_ln_b', 'L0_ffn_w1', 'L0_ffn_b1',
        'L0_ffn_w2', 'L0_ffn_b2', 'L0_c', 'L0_wmod']


def kernel(**inputs):
    import numpy as _np
    import concourse.bacc as _bacc
    from concourse import mybir as _mybir
    from concourse.bass_utils import run_bass_kernel_spmd as _run

    nc = _bacc.Bacc("TRN2", target_bir_lowering=False, num_devices=1)
    f32, bf16 = _mybir.dt.float32, _mybir.dt.bfloat16
    arrays, args = {}, []
    for name in _INS:
        a = _np.ascontiguousarray(inputs[name])
        arrays[f"in_{name}"] = a
        args.append(nc.dram_tensor(f"in_{name}", a.shape, _mybir.dt.from_np(a.dtype), kind="ExternalInput").ap())
    for name, shape, dt in (("mod_rows", (NB, 6 * D), f32), ("lists", (DUMMY + TOK, RW), f32),
                            ("wsplit", (E, P, 4 * NI * D), bf16), ("b1_rows", (E, 2, I // 2), f32), ("b1_folded", (E, P, NI), f32),
                            ("y_rows", (DUMP + 2 * TOK, D), f32)):
        args.append(nc.dram_tensor(name, shape, dt, kind="Internal").ap())
    args.append(nc.dram_tensor("out_0", (NB, T, D), f32, kind="ExternalOutput").ap())
    adaln_moe_kernel(nc, *args)
    r = _run(nc, [arrays], core_ids=[0])
    return r.results[0]["out_0"]
```

```python
import concourse.bass as bass
from concourse import mybir
from contextlib import ExitStack


P = 128
NB, T, D = 16, 512, 256
H = 64
E, I = 8, 1024
NC, NK = T // P, D // P
NI = I // P
NTOK = NB * T
TOK = 256
TH = TOK // P
TILES = (2 * NTOK + E * (TOK - 1)) // TOK
CAP = NTOK + TOK
RW = D + 4
DUMP = 3 * NTOK
DUMMY = E * CAP
MAXT = -(-NTOK // TOK)
EPS = 1e-5
SA, CA, GA, SB, CB, GB = range(6)
VEC_B1, VEC_G, VEC_B, VEC_RG, VEC_RB = 0, E * NI, E * NI + 2 * E, E * NI + 4 * E, E * NI + 4 * E + 2
NVEC = VEC_RB + 2


def adaln_moe_kernel(nc, x_d, wq_d, wk_d, wv_d, wo_d, rng_d, rnb_d, rw_d, rb_d, lng_d, lnb_d,
                     w1_d, b1_d, w2_d, b2_d, c_d, wmod_d, mod_d, list_d, wsplit_d, b1r_d, b1f_d, y_d, out_d):
    f32, bf16, i32, u32 = mybir.dt.float32, mybir.dt.bfloat16, mybir.dt.int32, mybir.dt.uint32
    ALU, ACT, AX = mybir.AluOpType, mybir.ActivationFunctionType, mybir.AxisListType
    ds = bass.ds

    ctx = ExitStack()
    with ctx:
        def sb(name, shape, dt=f32):
            return ctx.enter_context(nc.sbuf_tensor(name, shape, dt))

        def sem(name):
            return ctx.enter_context(nc.semaphore(name))

        def sems(name, n=2):
            return [sem(f"{name}{i}") for i in range(n)]

        resid = sb("resid", [P, NB * NC, D])
        ident = sb("ident", [P, P])
        causal = sb("causal", [P, P])
        before = sb("before", [P, P], bf16)
        allone = sb("allone", [P, P], bf16)
        onesf = sb("onesf", [P, T])
        experts = sb("experts", [P, E])
        mhalf = sb("mhalf", [P, 3, NC])
        wqk = sb("wqk", [P, NK, 2 * H])
        wv = sb("wv", [P, NK, H])
        wo = sb("wo", [H, D])
        wog = sb("wog", [P, 2, D + 1])
        vrow = sb("vrow", [NVEC, P])
        vecs = sb("vecs", [P, NVEC])
        lngb = sb("lngb", [P, E, 4])
        rrow = sb("rrow", [E, D])
        rT = sb("rT", [P, NK, E])
        rTg = sb("rTg", [P, NK, E])
        rnbb = sb("rnbb", [P, NK, P])
        rbias = sb("rbias", [P, E])
        cin = sb("cin", [NB, D])
        cex = sb("cex", [NB, D])
        cT = sb("cT", [P, NK, NB])
        mod = sb("mod", [NB, 6 * D])
        modT = sb("modT", [P, NB, 4])
        modc = sb("modc", [P, 2, 4])
        gaB = sb("gaB", [H, 2, D])
        csB = sb("csB", [P, 2, 2 * D])
        st = sb("st", [P, NC, 6])
        mv = sb("mv", [P, 3, NC, 2]); ve = sb("ve", [P, 3, NC]); rs = sb("rs", [P, 2, 3, NC]); nm = sb("nm", [P, 2, 3, NC])
        rowbuf = sb("rowbuf", [P, 4 * NC * D])
        xc, xn2, *h2 = (rowbuf[:, n * NC * D:(n + 1) * NC * D].rearrange("p (c d) -> p c d", c=NC) for n in range(4))
        gneg, gsgn = h2[0][0:NB, 0, :], h2[0][0:NB, 1, :]
        yt = rowbuf[:, 0:2 * TH * D].rearrange("p (r h d) -> p r h d", r=2, h=TH)
        xin = rowbuf[:, 2 * NC * D:2 * NC * D + 2 * TH * RW].rearrange("p (r h d) -> p r h d", r=2, h=TH)
        hT = sb("hT", [P, NK, T])
        ex = sb("ex", [P, T])
        qk = sb("qk", [P, 2, T])
        vT = sb("vT", [H, 2, T])
        ktok = sb("ktok", [P, 2, NC, H])
        zT = sb("zT", [H, T])
        oz = sb("oz", [P, 2, T])
        PW = [T - a * P for a in range(NC)]
        PO = [a * T for a in range(NC)]
        pt = sb("pt", [P, NC * T])
        den = sb("den", [P, NC]); rden = sb("rden", [P, NC])
        nrm = sb("nrm", [P, 2, NC, RW])
        nT = sb("nT", [P, NK, T])
        lg = sb("lg", [P, NC, E])
        mx = sb("mx", [P, NC, 8])
        ix = sb("ix", [P, NC, 8], u32)
        ef = sb("ef", [P, NC, 2])
        oh = sb("oh", [P, 2, NC, E])
        ohs = sb("ohs", [P, NC, E], bf16)
        dl = sb("dl", [P, NC]); dex = sb("dex", [P, NC]); d1 = sb("d1", [P, NC])
        rt = sb("rt", [P, NC * E + E])
        cnt = sb("cnt", [P, NC, E])
        pick = sb("pick", [P, 2, NC, E])
        base = sb("base", [P, E])
        slot = sb("slot", [P, 2, NC, 2], i32)
        w_all = sb("w_all", [P, NB * NC, 2])
        slotf = sb("slotf", [P, NC, 2])
        token = sb("token", [P, NC])
        wbuf = sb("wbuf", [P, 2, 4 * NI * D], bf16)
        w1f = wbuf[:, 1, :].bitcast(f32)[:, 0:2048].rearrange("p (k i) -> p k i", k=NK)
        w2f = wbuf[:, 1, :].bitcast(f32)[:, 2048:4096]
        wmod = wbuf[:, 0, :].bitcast(f32)[:, 0:NK * 6 * D].rearrange("p (k n) -> p k n", k=NK)
        lge = sb("lge", [P, 4])
        b1f = sb("b1f", [P, E, NI])
        nh = sb("nh", [P, 2, NK, TOK], bf16)
        nl = sb("nl", [P, 2, NK, TOK], bf16)
        b1row = [t[:, :, :, :].bitcast(f32).rearrange("p r k n -> p (r k n)")[0:1, :] for t in (nh, nl)]
        pad = sb("pad", [P, TH, RW])
        ydf = sb("ydf", [P, 2, TH]); ydp = sb("ydp", [P, 2, TH]); ydst = sb("ydst", [P, 2, TH], i32)
        gf = sb("gf", [P, 2, TOK])
        gh = sb("gh", [P, 4, TOK], bf16)
        gl = sb("gl", [P, 4, TOK], bf16)
        b1t = sb("b1t", [P, 2, NI])
        b2t = sb("b2t", [P, 2, D])
        offs = sb("offs", [P, E]); count = sb("count", [P, E]); counti = sb("counti", [P, E], i32)
        steps = sb("steps", [P, E, MAXT]); need = sb("need", [P, E, MAXT])
        ntile = sb("ntile", [P, E]); tend = sb("tend", [P, E]); tstart = sb("tstart", [P, E])
        delta = sb("delta", [P, E])
        padrow = sb("padrow", [P, E], i32)
        tid = sb("tid", [P, TILES, E])
        ge, gs = (pt[:, n * TILES * E:(n + 1) * TILES * E].rearrange("p (j e) -> p j e", e=E) for n in range(2))
        tab_e = sb("tab_e", [P, TILES]); tab_r = sb("tab_r", [P, TILES]); tab_d = sb("tab_d", [P, TILES]); hop = sb("hop", [P, E])
        table = sb("table", [P, 3, TILES], i32)
        gbB = pt[:, 0:4 * D].rearrange("p (r d) -> p r d", r=4)
        R = 4
        ya, yb = (wbuf[:, n, :].bitcast(f32).rearrange("p (r c d) -> p r c d", r=R, c=NC) for n in range(2))

        bank = [ctx.enter_context(nc.psum_tensor(f"bank{i}", [P, 512], f32)) for i in range(8)]
        TR, Q, V, S, O = bank[0:2], bank[2], bank[3], bank[4:7], bank[7]
        SO = (S[0], S[1], O, S[2])
        LOG = S[2][:, 384:384 + NC * E]
        RANK, TOT, RT = O[:, 0:32], O[:, 32:40], O[:, 0:40]
        ACC = [bank[2:4], bank[4:6]]
        MM = bank[6:8]

        consts = sem("consts"); dconst = sem("dconst"); acon = sem("acon")
        got_c = sem("got_c"); got_wmod = sem("got_wmod"); got_w = sem("got_w"); got_vec = sem("got_vec")
        got_r = sem("got_r"); base_set = sem("base_set")
        c_exp = sem("c_exp"); c_step = sem("c_step"); cT_ps = sem("cT_ps"); cT_sb = sem("cT_sb")
        mod_ps = sem("mod_ps"); mod_step = sem("mod_step"); mod_out = sem("mod_out"); modT_ps = sem("modT_ps")
        vec_ps = sem("vec_ps"); set_step = sem("set_step"); rb_ps = sem("rb_ps"); setup_done = sem("setup_done")
        got_x = sems("got_x"); got_ga = sems("got_ga"); got_cs = sems("got_cs")
        st_s = sem("st_s"); mv_s = sem("mv_s"); ve_s = sem("ve_s"); rs_s = sem("rs_s"); nm_s = sem("nm_s")
        stat_set = sem("stat_set"); rank_s = sem("rank_s"); tok_s = sem("tok_s"); pad_s = sem("pad_s")
        xc_s = sem("xc_s"); xT_s = sem("xT_s"); modc_s = sem("modc_s"); hT_s = sem("hT_s")
        proj_s = sem("proj_s"); ex_s = sem("ex_s"); vT_s = sem("vT_s"); exn_s = sem("exn_s"); phi_s = sem("phi_s")
        ktr_s = sem("ktr_s"); ktok_s = sem("ktok_s"); scan_s = sem("scan_s"); qz_s = sem("qz_s")
        score_s = sem("score_s"); diag_s = sem("diag_s"); strip_s = sem("strip_s"); pv_s = sem("pv_s")
        oT_s = sem("oT_s"); log_s = sem("log_s"); den_s = sem("den_s"); rden_s = sem("rden_s")
        wog_s = sem("wog_s"); owo_s = sem("owo_s"); x2_s = sem("x2_s")
        xn2_s = sem("xn2_s"); h2m_s = sem("h2m_s"); h2_s = sem("h2_s"); nrm_s = sem("nrm_s")
        nTp_s = sem("nTp_s"); nT_s = sem("nT_s"); lg_s = sem("lg_s"); mx_s = sem("mx_s")
        ix_s = sem("ix_s"); ef_s = sem("ef_s"); oh_s = sem("oh_s"); ohs_s = sem("ohs_s"); dl_s = sem("dl_s")
        dex_s = sem("dex_s"); d1_s = sem("d1_s"); w0_s = sem("w0_s"); w1_s = sem("w1_s")
        rt_s = sem("rt_s"); cnt_s = sem("cnt_s"); pick_s = sem("pick_s"); slotf_s = sem("slotf_s")
        slot_s = sem("slot_s"); base_s = sem("base_s"); scat = sems("scat")
        got_w1e = sem("got_w1e"); got_w2e = sem("got_w2e"); lge_s = sem("lge_s"); head1_s = sem("head1_s"); head2_s = sem("head2_s"); rest1_s = sem("rest1_s"); rest2_s = sem("rest2_s")
        b1f_s = sem("b1f_s"); b1p_s = sem("b1p_s"); b1r_s = sem("b1r_s"); got_b1v = sem("got_b1v"); b1v_ps = sem("b1v_ps"); w1_out = sem("w1_out"); w2_out = sem("w2_out"); b1_out = sem("b1_out")
        tstep = sem("tstep"); tab_s = sem("tab_s"); pad_out = sem("pad_out")
        got_xin = sems("got_xin"); got_w1 = sems("got_w1"); got_w2 = sems("got_w2")
        got_b1 = sems("got_b1"); got_b2 = sems("got_b2")
        tr_s = sem("tr_s"); nh_s = sem("nh_s"); nl_s = sem("nl_s"); mm1_s = sem("mm1_s"); gf_s = sem("gf_s")
        gh_s = sem("gh_s"); gl_s = sem("gl_s"); mm2_s = sem("mm2_s"); yt_s = sem("yt_s"); y_out = sems("y_out")
        yd_a = sem("yd_a"); yd_b = sem("yd_b"); yd_s = sem("yd_s")
        got_gb = sems("got_gb", R); got_ya = sems("got_ya", R); got_yb = sems("got_yb", R)
        ca_s = sem("ca_s"); cb_s = sem("cb_s"); cc_s = sem("cc_s"); res_s = sem("res_s"); o_out = sem("o_out")
        held = {n: sem(f"held_{n}") for n in ("act", "dve", "pe", "pool", "sp")}

        def wait_past(eng, semaphore, value):
            if not isinstance(value, int) or value > 0:
                eng.wait_ge(semaphore, value)

        def upto(n):
            return min(n, NB) if isinstance(n, int) else n

        def used(i):
            if not isinstance(i, int):
                return slice(0, 3)
            return slice(0 if i < NB else 1 if i - 3 < NB else 2, 1 if i < 3 else 2 if i < 4 else 3)

        def hold(eng, name):
            eng.sem_inc(held[name], 1)

        def pipeline(eng, step):
            for i in range(5):
                step(i, i // 2, i % 2, *(i >= n for n in range(6)))
            with eng.Fori(2, NB // 2 - 1) as j:
                step(2 * j + 1, j, 1, *(True,) * 6)
                step(2 * j + 2, j + 1, 0, *(True,) * 6)
            for i in range(NB - 1, NB + 5):
                step(i, i // 2, i % 2, *(i - n < NB for n in range(6)))

        block = ctx.enter_context(nc.Block())

        x_v = x_d.rearrange("b (c p) d -> b p c d", p=P)
        out_v = out_d.rearrange("b (c p) d -> b p c d", p=P)
        w1_v = w1_d.rearrange("e (k p) i -> e p k i", p=P)
        w2_v = w2_d.rearrange("e (c p) d -> e p c d", p=P)

        @block.sync
        def _(sp):
            sp.dma_start(cin[:, :], c_d).then_inc(got_c, 16)
            sp.dma_start(wmod, wmod_d.rearrange("(k p) n -> p k n", p=P)).then_inc(got_wmod, 16)
            for b in range(2):
                sp.dma_start(resid[:, b * NC:(b + 1) * NC, :], x_v[b]).then_inc(got_x[b], 16)
            sp.dma_start(wqk[:, :, 0:H], wq_d.rearrange("(k p) h -> p k h", p=P)).then_inc(got_w, 16)
            sp.dma_start(wqk[:, :, H:2 * H], wk_d.rearrange("(k p) h -> p k h", p=P)).then_inc(got_w, 16)
            sp.dma_start(wv[:, :, :], wv_d.rearrange("(k p) h -> p k h", p=P)).then_inc(got_w, 16)
            sp.dma_start(wo[:, :], wo_d).then_inc(got_w, 16)
            sp.dma_start(vrow[VEC_B1:VEC_G, :], b1_d.rearrange("e (i p) -> (e i) p", p=P)).then_inc(got_vec, 16)
            sp.dma_start(vrow[VEC_G:VEC_B, :], lng_d.rearrange("e (k p) -> (e k) p", p=P)).then_inc(got_vec, 16)
            sp.dma_start(vrow[VEC_B:VEC_RG, :], lnb_d.rearrange("e (k p) -> (e k) p", p=P)).then_inc(got_vec, 16)
            sp.dma_start(vrow[VEC_RG:VEC_RB, :], rng_d.rearrange("(k p) -> k p", p=P)).then_inc(got_vec, 16)
            sp.dma_start(vrow[VEC_RB:NVEC, :], rnb_d.rearrange("(k p) -> k p", p=P)).then_inc(got_vec, 16)
            sp.dma_start(rrow[:, :], rw_d).then_inc(got_r, 16)
            sp.dma_start(rbias[:, :], rb_d.partition_broadcast(P)).then_inc(got_r, 16)
            sp.wait_ge(mod_step, 8)
            sp.dma_start(mod_d, mod[:, :]).then_inc(mod_out, 16)
            sp.wait_ge(pad_s, 3)
            sp.dma_start(list_d[DUMMY:DUMMY + TOK, :].rearrange("(p r) d -> p r d", r=TH), pad[:, :, :]).then_inc(pad_out, 16)
            sp.wait_ge(mod_out, 16)
            sp.wait_ge(mod_ps, 1)

            def load_cs(s, q):
                wait_past(sp, h2_s, s - 1)
                sp.dma_start(csB[:, q, :], mod_d[ds(s, 1), SB * D:(CB + 1) * D].partition_broadcast(P)
                             if not isinstance(s, int) else
                             mod_d[s, SB * D:(CB + 1) * D].partition_broadcast(P)).then_inc(got_cs[q], 16)

            def step(i, half, r):
                if isinstance(i, int) and i == 0:
                    load_w1(0)
                    load_w2(0)
                load_x(i, half, r)
                wait_past(sp, wog_s, i - 1)
                sp.dma_start(gaB[:, r, :], mod_d[ds(i, 1), GA * D:(GA + 1) * D].partition_broadcast(H)
                             if not isinstance(i, int) else
                             mod_d[i, GA * D:(GA + 1) * D].partition_broadcast(H)).then_inc(got_ga[r], 16)
                if not isinstance(i, int) or i >= 1:
                    load_cs(i - 1, 1 - r)
                if r == 1:
                    sp.wait_ge(rest1_s, NK * half + NK)
                    hold(sp, "sp")
                    sp.wait_ge(b1p_s, half + 1)
                    if not isinstance(half, int) or half + 1 < E:
                        load_w1(half + 1)
                    sp.wait_ge(b1r_s, half + 1)
                    for n in range(2):
                        sp.dma_start(b1r_d[half, n:n + 1, :] if isinstance(half, int) else b1r_d[ds(half, 1), n, :], b1row[n]).then_inc(b1_out, 16)
                    sp.dma_start(wsplit_d[half, :, 0:4096] if isinstance(half, int) else wsplit_d[ds(half, 1), :, 0:4096],
                                 wbuf[:, 0, 0:4096]).then_inc(w1_out, 16)
                elif not isinstance(i, int) or i > 0:
                    split_w2_out(half)
                    load_w2(half)

            def split_w2_out(half):
                sp.wait_ge(rest2_s, half)
                sp.dma_start(wsplit_d[half - 1, :, 4096:8192] if isinstance(half, int) else wsplit_d[ds(half - 1, 1), :, 4096:8192],
                             wbuf[:, 0, 4096:8192]).then_inc(w2_out, 16)

            def load_x(i, half, r):
                if isinstance(i, int):
                    if i + 2 < NB:
                        sp.wait_ge(got_x[r], 16 * (half + 1))
                        sp.dma_start(resid[:, (i + 2) * NC:(i + 3) * NC, :], x_v[i + 2]).then_inc(got_x[r], 16)
                else:
                    sp.wait_ge(got_x[r], 16 * half + 16)
                    sp.dma_start(resid[:, ds((i + 2) * NC, NC), :], x_v[ds(i + 2, 1)]).then_inc(got_x[r], 16)

            def load_w1(e):
                sp.dma_start(w1f, w1_v[e] if isinstance(e, int) else w1_v[ds(e, 1)]).then_inc(got_w1e, 16)

            def load_w2(e):
                sp.dma_start(w2f.rearrange("p (c d) -> p c d", c=NI), w2_v[e] if isinstance(e, int) else w2_v[ds(e, 1)]).then_inc(got_w2e, 16)

            for i in range(2):
                step(i, 0, i)
            with nc.sync.Fori(1, NB // 2 - 1) as j:
                for r in range(2):
                    step(2 * j + r, j, r)
            for i in range(NB - 2, NB):
                step(i, NB // 2 - 1, i % 2)
            load_cs(NB - 1, 1)
            split_w2_out(E)
            sp.wait_ge(b1_out, 32 * E)
            sp.dma_start(vrow[0:E * NI, :], b1r_d.rearrange("e n (i p) -> (e n i) p", p=P)).then_inc(got_b1v, 16)
            sp.wait_ge(b1f_s, 1)
            sp.dma_start(b1f_d.rearrange("e p i -> p e i"), b1f[:, :, :]).then_inc(b1_out, 16)

            sp.wait_ge(tab_s, 1)
            for e in range(E):
                row = nc.sync.value_load(padrow[0:1, e:e + 1], min_val=0, max_val=DUMMY)
                sp.dma_start(list_d[ds(row, TOK), :].rearrange("(p r) d -> p r d", r=TH), pad[:, :, :]).then_inc(pad_out, 16)
            sp.wait_ge(w1_out, 16 * E)
            sp.wait_ge(w2_out, 16 * E)
            sp.wait_ge(b1_out, 32 * E + 16)
            sp.wait_ge(tab_s, 2)

            def rows_load(j, r):
                row = nc.sync.value_load(table[0:1, 1, ds(j, 1)], min_val=0, max_val=DUMMY)
                wait_past(sp, tr_s, j - 1)
                wait_past(sp, yd_s, j - 1)
                sp.dma_start(xin[:, r, :, :].rearrange("p r d -> p (r d)"),
                             list_d[ds(row, TOK), :].rearrange("(p r) d -> p (r d)", r=TH)).then_inc(got_xin[r], 16)

            def which(j):
                return (nc.sync.value_load(table[0:1, 0, ds(j, 1)], min_val=0, max_val=E - 1),
                        nc.sync.value_load(table[0:1, 2, ds(j, 1)], min_val=0, max_val=1))

            def first_load(j, r, e, new):
                wait_past(sp, mm1_s, NI * (j - 1))
                sp.dma_start(wbuf[:, r, 0:4096], wsplit_d[ds(e, 1), :, 0:4096], cond=new).then_inc(got_w1[r], 16)
                wait_past(sp, gf_s, NI * (j - 1))
                sp.dma_start(b1t[:, r, :], b1f_d[ds(e, 1)]).then_inc(got_b1[r], 16)

            def second_load(j, r, e, new):
                wait_past(sp, mm2_s, NI * (j - 1))
                sp.dma_start(wbuf[:, r, 4096:8192], wsplit_d[ds(e, 1), :, 4096:8192], cond=new).then_inc(got_w2[r], 16)
                wait_past(sp, yt_s, j - 1)
                sp.dma_start(b2t[:, r, :], b2_d[ds(e, 1), :].partition_broadcast(P)).then_inc(got_b2[r], 16)

            def tile_loads(j, r):
                rows_load(j, r)
                e, new = which(j)
                first_load(j, r, e, new)
                second_load(j, r, e, new)

            e, new = which(0)
            first_load(0, 0, e, new)
            for r in range(2):
                sp.wait_ge(scat[r], 16 * 2 * NC * NB // 2)
            sp.wait_ge(pad_out, 16 * (E + 1))
            rows_load(0, 0)
            second_load(0, 0, e, new)
            tile_loads(1, 1)
            with nc.sync.Fori(1, TILES // 2) as h:
                for r in range(2):
                    tile_loads(2 * h + r, r)
            for j in range(TILES // 2 * 2, TILES):
                tile_loads(j, j % 2)

            for b in range(R):
                sp.dma_start(gbB[:, b, :], mod_d[b, GB * D:(GB + 1) * D].partition_broadcast(P)).then_inc(got_gb[b], 16)

            for r in range(2):
                sp.wait_ge(y_out[r], 16 * TH * ((TILES + 1 - r) // 2))

            def rows_in(b, r):
                wait_past(sp, res_s, b - R + 1)
                for t, (dst, got) in enumerate(((ya, got_ya), (yb, got_yb))):
                    sp.dma_start(dst[:, r, :, :], y_d[ds(t * NTOK + b * T, T), :].rearrange("(c p) d -> p c d", p=P)).then_inc(got[r], 16)
                if not isinstance(b, int):
                    sp.dma_start(gbB[:, r, :], mod_d[ds(b, 1), GB * D:(GB + 1) * D].partition_broadcast(P)).then_inc(got_gb[r], 16)

            def store(b):
                sp.wait_ge(res_s, b + 1)
                sp.dma_start(out_v[ds(b, 1)], resid[:, ds(NC * b, NC), :]).then_inc(o_out, 16)

            for b in range(R):
                rows_in(b, b)
            with nc.sync.Fori(0, NB // R - 1) as h:
                for r in range(R):
                    store(R * h + r)
                    rows_in(R * h + r + R, r)
            for b in range(NB - R, NB):
                store(b)
            sp.wait_ge(o_out, 16 * NB)

        @block.gpsimd
        def _(pool):
            g = nc.gpsimd
            g.memset(ident[:, :], 0.0).then_inc(consts, 1)
            g.memset(causal[:, :], 1.0).then_inc(consts, 1)
            g.memset(before[:, :], 1.0).then_inc(consts, 1)
            g.memset(allone[:, :], 1.0).then_inc(consts, 1)
            g.memset(onesf[:, :], 1.0).then_inc(consts, 1)
            g.memset(mhalf[:, :], -0.5).then_inc(consts, 1)
            g.iota(experts[:, :], pattern=[[1, E]], base=0, channel_multiplier=0,
                   allow_small_or_imprecise_dtypes=True).then_inc(consts, 1)
            g.iota(offs[:, :], pattern=[[CAP, E]], base=0, channel_multiplier=0,
                   allow_small_or_imprecise_dtypes=True).then_inc(consts, 1)
            g.iota(steps[:, :, :], pattern=[[0, E], [TOK, MAXT]], base=0, channel_multiplier=0,
                   allow_small_or_imprecise_dtypes=True).then_inc(consts, 1)
            g.iota(tid[:, :, :], pattern=[[1, TILES], [0, E]], base=0, channel_multiplier=0,
                   allow_small_or_imprecise_dtypes=True).then_inc(consts, 1)
            g.iota(token[:, :], pattern=[[P, NC]], base=-T, channel_multiplier=1,
                   allow_small_or_imprecise_dtypes=True).then_inc(tok_s, 1)
            g.memset(pad[:, :, :], 0.0).then_inc(pad_s, 1)
            pool.wait_ge(pad_s, 1)
            g.iota(pad[:, :, D:D + 1], pattern=[[1, TH], [0, 1]], base=DUMP - NTOK, channel_multiplier=TH,
                   allow_small_or_imprecise_dtypes=True).then_inc(pad_s, 1)
            g.memset(pad[:, :, D + 1:D + 2], -1.0).then_inc(pad_s, 1)
            pool.wait_ge(consts, 10)
            g.affine_select(out=ident[:, :], in_=ident[:, :], compare_op=ALU.not_equal, fill=1.0,
                            base=0, pattern=[[-1, P]], channel_multiplier=1).then_inc(consts, 1)
            g.affine_select(out=causal[:, :], in_=causal[:, :], compare_op=ALU.is_ge, fill=0.0,
                            base=0, pattern=[[1, P]], channel_multiplier=-1).then_inc(consts, 1)
            g.affine_select(out=before[:, :], in_=before[:, :], compare_op=ALU.is_ge, fill=0.0,
                            base=-1, pattern=[[1, P]], channel_multiplier=-1).then_inc(consts, 1)

            def inverse_root(i, r):
                pool.wait_ge(ve_s, i + 1)
                wait_past(pool, xc_s, upto(i - 1))
                wait_past(pool, xn2_s, upto(i - 4))
                wait_past(pool, nrm_s, upto(i - 5))
                wait_past(pool, nm_s, i - 1)
                n = used(i)
                g.tensor_tensor(rs[:, r, n, :], ve[:, n, :], mhalf[:, n, :], ALU.pow).then_inc(rs_s, 1)

            inverse_root(0, 0)

            def scatter(q, chunks):
                for c in chunks:
                    for t in range(2):
                        g.indirect_dma_start(list_d, bass.IndirectOffsetOnAxis(ap=slot[:, q, c, t:t + 1], axis=0),
                                             nrm[:, q, c, :], None).then_inc(scat[q], 16)

            def step(i, half, r, project, attend, settle, norm, route, place):
                if attend:
                    b, q = i - 1, 1 - r
                    pool.wait_ge(got_ga[q], 16 * (half if q == 1 else half + 1))
                    wait_past(pool, owo_s, b - 1)
                    g.tensor_tensor(wog[0:H, q, 0:D], wo[:, :], gaB[:, q, :], ALU.mult).then_inc(wog_s, 1)
                if norm and (project or attend):
                    b, q = i - 3, 1 - r
                    pool.wait_ge(got_cs[q], 16 * (half if q == 0 else half - 1))
                    pool.wait_ge(xn2_s, b + 1)
                    wait_past(pool, nrm_s, b - 1)
                    g.tensor_tensor(h2[q], xn2, csB[:, q, D:2 * D].unsqueeze(1).to_broadcast([P, NC, D]), ALU.mult).then_inc(h2m_s, 1)
                    pool.wait_ge(h2m_s, b + 1)
                    g.tensor_tensor(h2[q], h2[q], csB[:, q, 0:D].unsqueeze(1).to_broadcast([P, NC, D]), ALU.add).then_inc(h2_s, 1)
                if place:
                    pool.wait_ge(slot_s, i - 4)
                    hold(pool, "pool")
                    scatter(1 - r, (0, 1))
                if project or attend or norm:
                    inverse_root(i + 1, 1 - r)
                if place:
                    scatter(1 - r, (2, 3))

            pipeline(g, step)

            def y_scatter(j, half, r):
                pool.wait_ge(yt_s, j + 1)
                pool.wait_ge(yd_s, j + 1)
                hold(pool, "pool")
                for h in range(TH):
                    g.indirect_dma_start(y_d, bass.IndirectOffsetOnAxis(ap=ydst[:, r, h:h + 1], axis=0),
                                         yt[:, r, h, :], None).then_inc(y_out[r], 16)

            with g.Fori(0, TILES // 2) as h:
                for r in range(2):
                    y_scatter(2 * h + r, h, r)
            for j in range(TILES // 2 * 2, TILES):
                y_scatter(j, j // 2, j % 2)

            def times_gb(b, turn, r):
                pool.wait_ge(got_gb[r], 16 * turn + 16)
                pool.wait_ge(cb_s, b + 1)
                g.tensor_tensor(ya[:, r, :, :], ya[:, r, :, :], gbB[:, r, :].unsqueeze(1).to_broadcast([P, NC, D]), ALU.mult).then_inc(cc_s, 1)

            with g.Fori(0, NB // R) as h:
                for r in range(R):
                    times_gb(R * h + r, h, r)

        @block.scalar
        def _(act):
            a = nc.scalar
            act.wait_ge(got_c, 16)
            a.activation(cex[:, :], cin[:, :], ACT.Exp, scale=-1.0).then_inc(c_exp, 1)

            def rows(b):
                return lambda c: resid[:, b * NC + c, :] if isinstance(b, int) else resid[:, ds(b * NC + c, 1), :]

            def normalise(out, src, r, n, done):
                hold(act, "act")
                for c in range(NC):
                    last = a.activation(out(c), src(c), ACT.Identity, bias=nm[:, r, n, c:c + 1], scale=rs[:, r, n, c:c + 1])
                last.then_inc(done, 1)

            def step(i, half, r, project, attend, settle, norm, route, place):
                if project or norm or route:
                    act.wait_ge(nm_s, i + 1)
                if project:
                    act.wait_ge(got_x[r], 16 * half + 16)
                    wait_past(act, xT_s, i)
                    normalise(lambda c: xc[:, c, :], rows(i), r, 0, xc_s)
                if norm:
                    b = i - 3
                    wait_past(act, h2m_s, b)
                    normalise(lambda c: xn2[:, c, :], rows(b), r, 1, xn2_s)
                if project and r == 1:
                    act.wait_ge(b1p_s, half + 1)
                    wait_past(act, b1_out, 32 * half)
                    hold(act, "act")
                    a.activation(b1row[0], Q[0:1, :], ACT.Copy)
                    a.activation(b1row[1], V[0:1, :], ACT.Copy).then_inc(b1r_s, 1)
                if project:
                    act.wait_ge(xT_s, i + 1)
                    act.wait_ge(modc_s, i + 1)
                    wait_past(act, proj_s, i)
                    hold(act, "act")
                    for k in range(NK):
                        last = a.activation(hT[:, k, :], TR[k][:, :], ACT.Identity,
                                            bias=modc[:, r, 2 + k:3 + k], scale=modc[:, r, k:k + 1])
                    last.then_inc(hT_s, 1)
                if attend:
                    b = i - 1
                    act.wait_ge(score_s, b + 1)
                    wait_past(act, pv_s, b)
                    for s in range(NC):
                        last = a.activation(pt[:, PO[s]:PO[s] + PW[s]],
                                            S[2][:, 256:384] if s == 3 else S[s][:, 0:PW[s]], ACT.Copy)
                    last.then_inc(strip_s, 1)
                if route:
                    b = i - 4
                    if not isinstance(i, int) or b >= 2:
                        act.wait_ge(scat[r], 16 * 2 * NC * (half - 2))
                    normalise(lambda c: nrm[:, r, c, 0:D], lambda c: h2[r][:, c, :], r, 2, nrm_s)
                if place:
                    b = i - 5
                    act.wait_ge(dl_s, b + 1)
                    wait_past(act, w1_s, b)
                    a.activation(dex[:, :], dl[:, :], ACT.Exp).then_inc(dex_s, 1)
                if project:
                    act.wait_ge(proj_s, i + 1)
                    wait_past(act, phi_s, i)
                    a.activation(ex[:, :], Q[:, :], ACT.Relu, scale=-1.0).then_inc(exn_s, 1)
                    wait_past(act, score_s, i - 1)
                    a.activation(vT[:, r, :], V[0:H, :], ACT.Copy).then_inc(vT_s, 1)
                    act.wait_ge(exn_s, i + 1)
                    a.activation(ex[:, :], ex[:, :], ACT.Exp, scale=-1.0).then_inc(ex_s, 1)
                if route:
                    b = i - 4
                    act.wait_ge(nTp_s, b + 1)
                    wait_past(act, log_s, b)
                    for k in range(NK):
                        last = a.activation(nT[:, k, :], TR[k][:, :], ACT.Copy)
                    last.then_inc(nT_s, 1)
                if attend:
                    b = i - 1
                    act.wait_ge(pv_s, b + 1)
                    wait_past(act, owo_s, b - 1)
                    a.activation(oz[0:H, 1 - r, :], O[0:H, :], ACT.Copy).then_inc(oT_s, 1)
                if project:
                    act.wait_ge(ktr_s, i + 1)
                    wait_past(act, pv_s, i - 1)
                    a.activation(ktok[:, r, :, :].rearrange("p c h -> p (c h)"), V[:, 0:NC * H], ACT.Copy).then_inc(ktok_s, 1)
                if project and r == 1:
                    act.wait_ge(got_w2e, 16 * half + 16)
                    wait_past(act, w2_out, 16 * half)
                    hold(act, "act")
                    a.activation(wbuf[:, 0, 4096:6144], w2f, ACT.Copy).then_inc(head2_s, 1)
                if project and r == 0:
                    act.wait_ge(got_w1e, 16 * half + 16)
                    act.wait_ge(lge_s, half + 1)
                    wait_past(act, w1_out, 16 * half)
                    hold(act, "act")
                    for k in range(NK):
                        a.activation(wbuf[:, 0, k * 1024:(k + 1) * 1024], w1f[:, k, :], ACT.Copy,
                                     scale=lge[:, k:k + 1]).then_inc(head1_s, 1)

            pipeline(a, step)

            def head_rows(j, r):
                act.wait_ge(tr_s, j + 1)
                wait_past(act, mm1_s, NI * (j - 1))
                a.activation(nh[:, r, :, :].rearrange("p k n -> p (k n)"), TR[r][:, :], ACT.Copy).then_inc(nh_s, 1)

            def gelu(j, half, r, last_tile=False):
                act.wait_ge(got_b1[r], 16 * half + 16)
                for c in range(NI):
                    if c == 5 and not last_tile:
                        head_rows(j + 1, 1 - r)
                    act.wait_ge(mm1_s, NI * j + c + 1)
                    wait_past(act, gl_s, NI * j + c - 1)
                    a.activation(gf[:, c % 2, :], MM[c % 2][:, 0:TOK], ACT.Gelu, bias=b1t[:, r, c:c + 1]).then_inc(gf_s, 1)

            head_rows(0, 0)
            for j in range(2):
                gelu(j, 0, j)
            with a.Fori(1, TILES // 2) as h:
                for r in range(2):
                    gelu(2 * h + r, h, r)
            for j in range(TILES // 2 * 2, TILES):
                gelu(j, j // 2, j % 2, j == TILES - 1)

            def weigh(b, turn, r):
                act.wait_ge(got_ya[r], 16 * turn + 16)
                hold(act, "act")
                for c in range(NC):
                    last = a.activation(ya[:, r, c, :], ya[:, r, c, :], ACT.Copy, scale=w_all[:, ds(NC * b + c, 1), 0])
                last.then_inc(ca_s, 1)

            with a.Fori(0, NB // R) as h:
                for r in range(R):
                    weigh(R * h + r, h, r)

        @block.vector
        def _(dve):
            v = nc.vector
            setc = [0]

            def chain(ins, s=None):
                setc[0] += 1
                ins.then_inc(set_step, 1)
                dve.wait_ge(set_step, setc[0])

            def rows(b):
                return lambda c: resid[:, b * NC + c, :] if isinstance(b, int) else resid[:, ds(b * NC + c, 1), :]

            def stats(src, n, k):
                for c in range(NC):
                    last = v.bn_stats(st[:, c, :], src(c))
                last.then_inc(st_s, 1)
                dve.wait_ge(st_s, k + 1)
                hold(dve, "dve")
                for c in range(NC):
                    last = v.bn_aggr(mv[:, n, c, :], st[:, c, :])
                last.then_inc(mv_s, 1)
                dve.wait_ge(mv_s, k + 1)

            def var_eps(i):
                v.tensor_scalar(ve[:, :, :], mv[:, :, :, 1], EPS, None, ALU.add).then_inc(ve_s, 1)

            def stats_before(i):
                if not isinstance(i, int):
                    return 3 * i - 4
                return min(i + 1, NB) + min(max(i - 2, 0), NB) + min(max(i - 3, 0), NB)

            def neg_mean_rstd(i, r):
                dve.wait_ge(rs_s, i + 1)
                wait_past(dve, xc_s, upto(i - 1))
                wait_past(dve, xn2_s, upto(i - 4))
                wait_past(dve, nrm_s, upto(i - 5))
                hold(dve, "dve")
                n = used(i)
                v.scalar_tensor_tensor(nm[:, r, n, :], mv[:, n, :, 0], -1.0, rs[:, r, n, :], ALU.mult, ALU.mult).then_inc(nm_s, 1)

            v.memset(mv[:, :, :, :], 0.0).then_inc(stat_set, 1)
            v.memset(nrm[:, :, :, :], 0.0).then_inc(stat_set, 1)
            v.memset(wog[0:H, :, D:D + 1], 0.0).then_inc(stat_set, 1)
            v.memset(wog[H:2 * H, :, 0:D], 0.0).then_inc(stat_set, 1)
            v.memset(wog[H:2 * H, :, D:D + 1], 1.0).then_inc(stat_set, 1)
            dve.wait_ge(c_exp, 1)
            chain(v.tensor_scalar_add(cex[:, :], cex[:, :], 1.0))
            chain(v.reciprocal(cex[:, :], cex[:, :]))
            v.tensor_tensor(cin[:, :], cin[:, :], cex[:, :], ALU.mult).then_inc(c_step, 1)
            dve.wait_ge(cT_ps, 1)
            v.tensor_copy(cT[:, :, :], Q[:, 0:NK * NB].rearrange("p (k b) -> p k b", k=NK)).then_inc(cT_sb, 1)
            dve.wait_ge(stat_set, 2)
            dve.wait_ge(got_x[0], 16)
            stats(rows(0), 0, 0)
            var_eps(0)
            dve.wait_ge(mod_ps, 1)
            for s in range(3):
                v.tensor_copy(mod[:, s * 512:(s + 1) * 512], S[s][0:NB, :]).then_inc(mod_step, 1)
            dve.wait_ge(mod_step, 3)
            v.tensor_scalar_add(mod[:, CA * D:(CA + 1) * D], mod[:, CA * D:(CA + 1) * D], 1.0).then_inc(mod_step, 1)
            v.tensor_scalar_add(mod[:, CB * D:(CB + 1) * D], mod[:, CB * D:(CB + 1) * D], 1.0).then_inc(mod_step, 1)
            neg_mean_rstd(0, 0)
            dve.wait_ge(modT_ps, 1)
            chain(v.tensor_copy(modT[:, :, :].rearrange("p b s -> p s b"),
                                Q[:, 64:64 + 4 * NB].rearrange("p (s b) -> p s b", b=NB)))
            v.tensor_copy(modc[:, 0, :], modT[:, 0, :]).then_inc(modc_s, 1)
            for n, sel in enumerate((GA, GB)):
                gg = mod[:, sel * D:(sel + 1) * D]
                chain(v.tensor_scalar(gneg[:, :], gg, -1.0, None, ALU.mult))
                chain(v.tensor_tensor(gneg[:, :], gneg[:, :], gg, ALU.max))
                chain(v.tensor_scalar(gneg[:, :], gneg[:, :], 0.25, None, ALU.max))
                chain(v.tensor_scalar(gsgn[:, :], gg, 0.0, 2.0, ALU.is_ge, ALU.mult))
                chain(v.scalar_tensor_tensor(gg, gsgn[:, :], -1.0, gneg[:, :], ALU.add, ALU.mult))
            chain(v.tensor_copy(gneg[:, 0:1], gsgn[:, 0:1]))
            v.tensor_copy(gsgn[:, 1:2], gneg[:, 0:1]).then_inc(mod_step, 3)
            dve.wait_ge(vec_ps, 1)
            chain(v.tensor_copy(vecs[:, :], S[0][:, 0:NVEC]))
            chain(v.tensor_copy(rT[:, :, :], S[0][:, 128:128 + NK * E].rearrange("p (k e) -> p k e", k=NK)))
            chain(v.tensor_copy(lngb[:, :, 0:2], vecs[:, VEC_G:VEC_B].rearrange("p (e k) -> p e k", k=NK)))
            chain(v.tensor_copy(lngb[:, :, 2:4], vecs[:, VEC_B:VEC_RG].rearrange("p (e k) -> p e k", k=NK)))
            dve.wait_ge(consts, 13)
            for k in range(NK):
                chain(v.tensor_scalar(rTg[:, k, :], rT[:, k, :], vecs[:, VEC_RG + k:VEC_RG + k + 1], None, ALU.mult))
                chain(v.tensor_scalar(rnbb[:, k, :], onesf[:, 0:P], vecs[:, VEC_RB + k:VEC_RB + k + 1], None, ALU.mult))
            chain(v.tensor_copy(base[:, :], offs[:, :]))
            v.tensor_copy(ef[:, 0, 0:1], base[:, 0:1]).then_inc(base_set, 1)
            dve.wait_ge(rb_ps, 1)
            dve.wait_ge(got_r, 32)
            dve.wait_ge(base_set, 1)
            v.tensor_tensor(rbias[:, :], rbias[:, :], S[1][:, 0:E], ALU.add).then_inc(setup_done, 1)
            dve.wait_ge(setup_done, 1)

            v.tensor_copy(lge[:, :], lngb[:, 0, :]).then_inc(lge_s, 1)

            def step(i, half, r, project, attend, settle, norm, route, place):
                taken = stats_before(i)
                dve.wait_ge(nm_s, i + 1 if not isinstance(i, int) else min(i + 1, NB + 4))
                if settle:
                    dve.wait_ge(x2_s, i - 1)
                    hold(dve, "dve")
                    stats(rows(i - 2), 1, taken)
                    taken = taken + 1
                if place:
                    slots(i - 5, 1 - r)
                if attend:
                    b = i - 1
                    dve.wait_ge(strip_s, b + 1)
                    diag = pt[:, :].rearrange("p (a t) -> p a t", a=NC)[:, :, 0:P]
                    v.tensor_tensor(diag, diag, causal[:, :].unsqueeze(1).to_broadcast([P, NC, P]), ALU.mult).then_inc(diag_s, 1)
                if project and not (isinstance(i, int) and i == NB - 1):
                    if r == 0:
                        dve.wait_ge(got_x[1], 16 * half + 16)
                    else:
                        dve.wait_ge(got_x[0], 16 * half + 32)
                    hold(dve, "dve")
                    stats(rows(i + 1), 0, taken)
                    taken = taken + 1
                if norm and not project and not attend:
                    b, q = i - 3, 1 - r
                    dve.wait_ge(got_cs[q], 16 * (b // 2 + 1))
                    dve.wait_ge(xn2_s, b + 1)
                    dve.wait_ge(nrm_s, b - 1)
                    v.tensor_tensor(h2[q], xn2, csB[:, q, D:2 * D].unsqueeze(1).to_broadcast([P, NC, D]), ALU.mult).then_inc(h2m_s, 1)
                    dve.wait_ge(h2m_s, b + 1)
                    v.tensor_tensor(h2[q], h2[q], csB[:, q, 0:D].unsqueeze(1).to_broadcast([P, NC, D]), ALU.add).then_inc(h2_s, 1)
                if norm:
                    dve.wait_ge(h2_s, i - 2)
                    hold(dve, "dve")
                    stats(lambda c: h2[1 - r][:, c, :], 2, taken)
                if project or attend or norm:
                    var_eps(i + 1)
                if project:
                    dve.wait_ge(ex_s, i + 1)
                    wait_past(dve, score_s, i - 1)
                    wait_past(dve, ktr_s, i - 1)
                    v.scalar_tensor_tensor(qk[:, r, :], Q[:, :], 1.0, ex[:, :], ALU.add, ALU.max).then_inc(phi_s, 1)
                    dve.wait_ge(phi_s, i + 1)
                    wait_past(dve, owo_s, i - 1)
                    v.tensor_tensor_scan(zT[:, :], onesf[H:2 * H, :], qk[H:2 * H, r, :], 0.0, ALU.mult, ALU.add).then_inc(scan_s, 1)
                    dve.wait_ge(scan_s, i + 1)
                    v.tensor_tensor(oz[H:2 * H, r, :], qk[0:H, r, :], zT[:, :], ALU.mult).then_inc(qz_s, 1)
                if project or attend or norm:
                    neg_mean_rstd(i + 1, 1 - r)
                if project and not (isinstance(i, int) and i == NB - 1):
                    wait_past(dve, hT_s, i)
                    hold(dve, "dve")
                    v.tensor_copy(modc[:, 1 - r, :], modT[:, i + 1, :] if isinstance(i, int) else modT[:, ds(i + 1, 1), :]).then_inc(modc_s, 1)
                if place:
                    weights(i - 5)
                if project and r == 1:
                    dve.wait_ge(head1_s, NK * half + NK)
                    hold(dve, "dve")
                    for k in range(NK):
                        v.scalar_tensor_tensor(wbuf[:, 0, 2048 + k * 1024:2048 + (k + 1) * 1024], w1f[:, k, :], lge[:, k:k + 1],
                                               wbuf[:, 0, k * 1024:(k + 1) * 1024], ALU.mult, ALU.subtract).then_inc(rest1_s, 1)
                if r == 0 and (not isinstance(i, int) or 0 < i <= NB):
                    dve.wait_ge(head2_s, half)
                    hold(dve, "dve")
                    v.tensor_tensor(wbuf[:, 0, 6144:8192], w2f, wbuf[:, 0, 4096:6144], ALU.subtract).then_inc(rest2_s, 1)
                if attend:
                    b = i - 1
                    dve.wait_ge(owo_s, b + 1)
                    wait_past(dve, x2_s, b)
                    for c in range(NC):
                        last = v.tensor_scalar(den[:, c:c + 1], SO[c][:, D:D + 1], 1e-6, None, ALU.max)
                    last.then_inc(den_s, 1)
                if route:
                    dve.wait_ge(log_s, i - 3)
                    wait_past(dve, ix_s, i - 4)
                    v.tensor_tensor(lg[:, :, :], LOG.rearrange("p (c e) -> p c e", c=NC),
                                    rbias[:, :].unsqueeze(1).to_broadcast([P, NC, E]), ALU.add).then_inc(lg_s, 1)
                if attend:
                    b = i - 1
                    dve.wait_ge(den_s, b + 1)
                    v.reciprocal(rden[:, :], den[:, :]).then_inc(rden_s, 1)
                    dve.wait_ge(rden_s, b + 1)
                    for c in range(NC):
                        last = v.scalar_tensor_tensor(rows(b)(c), SO[c][:, 0:D],
                                                      rden[:, c:c + 1], rows(b)(c), ALU.mult, ALU.add)
                    last.then_inc(x2_s, 1)
                if route:
                    choose(i - 4, r)
                if project and r == 1 and not (isinstance(i, int) and i == NB - 1):
                    dve.wait_ge(rest1_s, NK * half + NK)
                    dve.wait_ge(b1p_s, half + 1)
                    hold(dve, "dve")
                    v.tensor_copy(lge[:, :], lngb[:, half + 1, :] if isinstance(half, int) else lngb[:, ds(half + 1, 1), :]).then_inc(lge_s, 1)

            def cols(t, b):
                return t[:, b * NC:(b + 1) * NC, :] if isinstance(b, int) else t[:, ds(b * NC, NC), :]

            def choose(b, q):
                wait_past(dve, dex_s, b)
                dve.wait_ge(lg_s, b + 1)
                hold(dve, "dve")
                for c in range(NC):
                    last = v.max(mx[:, c, :], lg[:, c, :])
                last.then_inc(mx_s, 1)
                dve.wait_ge(mx_s, b + 1)
                v.tensor_tensor(dl[:, :], mx[:, :, 1], mx[:, :, 0], ALU.subtract).then_inc(dl_s, 1)
                for c in range(NC):
                    last = v.max_index(ix[:, c, :], mx[:, c, :], lg[:, c, :])
                last.then_inc(ix_s, 1)
                dve.wait_ge(ix_s, b + 1)
                v.tensor_copy(ef[:, :, :], ix[:, :, 0:2]).then_inc(ef_s, 1)
                dve.wait_ge(ef_s, b + 1)
                dve.wait_ge(pick_s, b) if not isinstance(b, int) or b > 0 else None
                for t in range(2):
                    last = v.tensor_tensor(oh[:, t, :, :], experts[:, :].unsqueeze(1).to_broadcast([P, NC, E]),
                                           ef[:, :, t:t + 1].to_broadcast([P, NC, E]), ALU.is_equal)
                last.then_inc(oh_s, 1)
                dve.wait_ge(oh_s, b + 1)
                v.tensor_tensor(ohs[:, :, :], oh[:, 0, :, :], oh[:, 1, :, :], ALU.add).then_inc(ohs_s, 1)
                v.tensor_scalar(token[:, :], token[:, :], float(T), None, ALU.add).then_inc(tok_s, 1)
                v.tensor_copy(nrm[:, q, :, D + 1], ef[:, :, 0])
                dve.wait_ge(tok_s, b + 2)
                hold(dve, "dve")
                v.tensor_copy(nrm[:, q, :, D], token[:, :])

            def weights(b):
                dve.wait_ge(dex_s, b + 1)
                v.tensor_scalar(d1[:, :], dex[:, :], 1.0, None, ALU.add).then_inc(d1_s, 1)
                dve.wait_ge(d1_s, b + 1)
                v.reciprocal(d1[:, :], d1[:, :]).then_inc(w0_s, 1)
                dve.wait_ge(w0_s, b + 1)
                hold(dve, "dve")
                v.tensor_copy(cols(w_all, b)[:, :, 0], d1[:, :])
                v.tensor_tensor(cols(w_all, b)[:, :, 1], d1[:, :], dex[:, :], ALU.mult).then_inc(w1_s, 1)

            def slots(b, q):
                dve.wait_ge(rank_s, b + 1)
                wait_past(dve, base_s, b)
                hold(dve, "dve")
                v.tensor_copy(rt[:, :], RT).then_inc(rt_s, 1)
                dve.wait_ge(rt_s, b + 1)
                v.tensor_tensor(cnt[:, :, :], rt[:, 0:NC * E].rearrange("p (c e) -> p c e", c=NC),
                                base[:, :].unsqueeze(1).to_broadcast([P, NC, E]), ALU.add).then_inc(cnt_s, 1)
                dve.wait_ge(cnt_s, b + 1)
                v.tensor_tensor(base[:, :], base[:, :], rt[:, NC * E:NC * E + E], ALU.add).then_inc(base_s, 1)
                for t in range(2):
                    last = v.tensor_tensor(pick[:, t, :, :], oh[:, t, :, :], cnt[:, :, :], ALU.mult)
                last.then_inc(pick_s, 1)
                dve.wait_ge(pick_s, b + 1)
                hold(dve, "dve")
                for t in range(2):
                    last = v.tensor_reduce(slotf[:, :, t], pick[:, t, :, :], axis=AX.X, op=ALU.add)
                last.then_inc(slotf_s, 1)
                dve.wait_ge(slotf_s, b + 1)
                v.tensor_copy(slot[:, q, :, :], slotf[:, :, :]).then_inc(slot_s, 1)

            pipeline(v, step)

            tc = [0]

            def tchain(ins):
                tc[0] += 1
                ins.then_inc(tstep, 1)
                dve.wait_ge(tstep, tc[0])

            dve.wait_ge(base_s, NB)
            tchain(v.tensor_copy(padrow[:, :], base[:, :]))
            v.tensor_copy(counti[:, :], padrow[:, :]).then_inc(tab_s, 1)
            tchain(v.tensor_tensor(count[:, :], base[:, :], offs[:, :], ALU.subtract))
            tchain(v.tensor_tensor(need[:, :, :], count[:, :].unsqueeze(2).to_broadcast([P, E, MAXT]), steps[:, :, :], ALU.is_gt))
            dve.wait_ge(b1v_ps, 1)
            v.tensor_tensor(b1f[:, :, :].rearrange("p e i -> p (e i)"), vecs[:, VEC_B1:VEC_G], V[:, 0:E * NI], ALU.add).then_inc(b1f_s, 1)
            tchain(v.tensor_reduce(ntile[:, :], need[:, :, :], axis=AX.X, op=ALU.add))
            tchain(v.tensor_tensor_scan(tend[:, :], onesf[:, 0:E], ntile[:, :], 0.0, ALU.mult, ALU.add))
            tchain(v.tensor_tensor(tstart[:, :], tend[:, :], ntile[:, :], ALU.subtract))
            tchain(v.scalar_tensor_tensor(delta[:, :], tstart[:, :], float(TOK), offs[:, :], ALU.mult, ALU.subtract))
            tchain(v.tensor_tensor(ge[:, :, :], tid[:, :, :], tend[:, :].unsqueeze(1).to_broadcast([P, TILES, E]), ALU.is_ge))
            tchain(v.tensor_tensor(hop[:, 0:E - 1], delta[:, 1:E], delta[:, 0:E - 1], ALU.subtract))
            tchain(v.tensor_tensor(hop[:, E - 1:E], delta[:, 0:1], delta[:, 0:1], ALU.subtract))
            tchain(v.tensor_reduce(tab_e[:, :], ge[:, :, :], axis=AX.X, op=ALU.add))
            tchain(v.tensor_scalar(tab_e[:, :], tab_e[:, :], float(E - 1), None, ALU.min))
            tchain(v.tensor_tensor(gs[:, :, :], ge[:, :, :], hop[:, :].unsqueeze(1).to_broadcast([P, TILES, E]), ALU.mult))
            tchain(v.tensor_reduce(tab_r[:, :], gs[:, :, :], axis=AX.X, op=ALU.add))
            tchain(v.scalar_tensor_tensor(tab_r[:, :], tid[:, :, 0], float(TOK), tab_r[:, :], ALU.mult, ALU.subtract))
            tchain(v.tensor_scalar(tab_d[:, :], tab_r[:, :], -1.0, float(DUMMY), ALU.mult, ALU.add))
            tchain(v.tensor_tensor(tab_d[:, :], tab_d[:, :], ge[:, :, E - 1], ALU.mult))
            tchain(v.tensor_tensor(tab_r[:, :], tab_r[:, :], tab_d[:, :], ALU.add))
            tchain(v.tensor_copy(table[:, 0, :], tab_e[:, :]))
            tchain(v.tensor_copy(table[:, 1, :], tab_r[:, :]))
            tchain(v.memset(table[:, 2, 0:2], 1))
            v.tensor_tensor(table[:, 2, 2:TILES], tab_e[:, 2:TILES], tab_e[:, 0:TILES - 2], ALU.not_equal).then_inc(tab_s, 1)
            dve.wait_ge(tab_s, 2)

            def split_rows(j, half, r):
                dve.wait_ge(nh_s, j + 1)
                v.tensor_tensor(nl[:, r, :, :], TR[r][:, :].rearrange("p (k n) -> p k n", k=NK),
                                nh[:, r, :, :], ALU.subtract).then_inc(nl_s, 1)

            def destinations(j, half, r):
                dve.wait_ge(got_xin[r], 16 * half + 16)
                if not isinstance(j, int) or j >= 2:
                    dve.wait_ge(y_out[r], 16 * TH * half)
                hold(dve, "dve")
                v.tensor_scalar(ydf[:, r, :], xin[:, r, :, D + 1], tab_e[:, ds(j, 1)], float(NTOK), ALU.not_equal, ALU.mult)
                v.tensor_scalar(ydp[:, r, :], xin[:, r, :, D + 1], -1.0, float(TOK * r), ALU.is_equal, ALU.mult).then_inc(yd_a, 1)
                dve.wait_ge(yd_a, j + 1)
                v.tensor_tensor(ydf[:, r, :], ydf[:, r, :], ydp[:, r, :], ALU.add).then_inc(yd_b, 1)
                dve.wait_ge(yd_b, j + 1)
                v.tensor_tensor(ydst[:, r, :], ydf[:, r, :], xin[:, r, :, D], ALU.add).then_inc(yd_s, 1)

            def evacuate(j, half, r):
                dve.wait_ge(mm2_s, NI * j + NI)
                dve.wait_ge(got_b2[r], 16 * half + 16)
                if not isinstance(j, int) or j >= 2:
                    dve.wait_ge(y_out[r], 16 * TH * half)
                for h in range(TH):
                    last = v.tensor_tensor(yt[:, r, h, :], ACC[r][h][:, 0:D], b2t[:, r, :], ALU.add)
                last.then_inc(yt_s, 1)

            def tile(j, half, r, first, last_tile):
                for c in range(NI):
                    n = NI * j + c
                    dve.wait_ge(gf_s, n + 1)
                    wait_past(dve, mm2_s, n - 3)
                    v.tensor_copy(gh[:, c % 4, :], gf[:, c % 2, :]).then_inc(gh_s, 1)
                    dve.wait_ge(gh_s, n + 1)
                    v.tensor_tensor(gl[:, c % 4, :], gf[:, c % 2, :], gh[:, c % 4, :], ALU.subtract).then_inc(gl_s, 1)
                    if c == 1 and not first:
                        evacuate(j - 1, half - 1 + r, 1 - r)
                    if c == 5 and not last_tile:
                        split_rows(j + 1, half + r, 1 - r)
                    if c == 7 and not last_tile:
                        destinations(j + 1, half + r, 1 - r)

            split_rows(0, 0, 0)
            destinations(0, 0, 0)
            tile(0, 0, 0, True, False)
            for j in range(1, 3):
                tile(j, j // 2, j % 2, False, False)
            with v.Fori(1, (TILES - 1) // 2 - 1) as h:
                tile(2 * h + 1, h, 1, False, False)
                tile(2 * h + 2, h + 1, 0, False, False)
            for j in range((TILES - 1) // 2 * 2 - 1, TILES):
                tile(j, j // 2, j % 2, False, j == TILES - 1)
            evacuate(TILES - 1, (TILES - 1) // 2, (TILES - 1) % 2)

            def mix(b, turn, r):
                dve.wait_ge(ca_s, b + 1)
                dve.wait_ge(got_yb[r], 16 * turn + 16)
                hold(dve, "dve")
                for c in range(NC):
                    last = v.scalar_tensor_tensor(ya[:, r, c, :], yb[:, r, c, :], w_all[:, ds(NC * b + c, 1), 1],
                                                  ya[:, r, c, :], ALU.mult, ALU.add)
                last.then_inc(cb_s, 1)

            def add(b, r):
                dve.wait_ge(cc_s, b + 1)
                hold(dve, "dve")
                v.tensor_tensor(resid[:, ds(NC * b, NC), :], ya[:, r, :, :], resid[:, ds(NC * b, NC), :], ALU.add).then_inc(res_s, 1)

            mix(0, 0, 0)
            with v.Fori(0, NB // R - 1) as h:
                for r in range(R):
                    mix(R * h + r + 1, h if r + 1 < R else h + 1, (r + 1) % R)
                    add(R * h + r, r)
            for b in range(NB - R, NB):
                if b + 1 < NB:
                    mix(b + 1, NB // R - 1, (b + 1) % R)
                add(b, b % R)

        @block.tensor
        def _(pe):
            t = nc.tensor
            pe.wait_ge(consts, 13)
            pe.wait_ge(stat_set, 5)
            pe.wait_ge(c_step, 1)
            for k in range(NK):
                last = t.transpose(Q[:, k * NB:(k + 1) * NB], cin[:, k * P:(k + 1) * P], ident[0:NB, 0:NB])
            last.then_inc(cT_ps, 1)
            pe.wait_ge(cT_sb, 1)
            pe.wait_ge(got_wmod, 16)
            for s in range(3):
                for k in range(NK):
                    last = t.matmul(S[s][0:NB, :], cT[:, k, :], wmod[:, k, s * 512:(s + 1) * 512], start=k == 0, stop=k == NK - 1)
            last.then_inc(mod_ps, 1)
            pe.wait_ge(mod_step, 5)
            for n, (sel, k) in enumerate(((CA, 0), (CA, 1), (SA, 0), (SA, 1))):
                last = t.transpose(Q[:, 64 + n * NB:64 + (n + 1) * NB], mod[:, sel * D + k * P:sel * D + (k + 1) * P], ident[0:NB, 0:NB])
            last.then_inc(modT_ps, 1)
            pe.wait_ge(got_vec, 80)
            pe.wait_ge(got_r, 32)
            pe.wait_ge(mod_step, 3)
            t.transpose(S[0][:, 0:NVEC], vrow[:, :], ident[0:NVEC, 0:NVEC])
            for k in range(NK):
                last = t.transpose(S[0][:, 128 + k * E:128 + (k + 1) * E], rrow[:, k * P:(k + 1) * P], ident[0:E, 0:E])
            last.then_inc(vec_ps, 1)
            pe.wait_ge(got_w, 64)

            def router_bias():
                pe.wait_ge(base_set, 1)
                for k in range(NK):
                    last = t.matmul(S[1][:, 0:E], rnbb[:, k, :], rT[:, k, :], start=k == 0, stop=k == NK - 1)
                last.then_inc(rb_ps, 1)
                pe.wait_ge(setup_done, 1)

            def step(i, half, r, project, attend, settle, norm, route, place):
                if project and r == 1:
                    pe.wait_ge(got_w1e, 16 * half + 16)
                    pe.wait_ge(lge_s, half + 1)
                    pe.wait_ge(phi_s, i)
                    pe.wait_ge(ktok_s, i)
                    hold(pe, "pe")
                    for n, row in enumerate((Q, V)):
                        for k in range(NK):
                            last = t.matmul(row[0:1, :], lge[:, 2 + k:3 + k], w1f[:, k, n * 512:(n + 1) * 512], start=k == 0, stop=k == NK - 1)
                    last.then_inc(b1p_s, 1)
                if project:
                    pe.wait_ge(xc_s, i + 1)
                    wait_past(pe, nT_s, i - 4)
                    for k in range(NK):
                        for c in range(NC):
                            last = t.transpose(TR[k][:, c * P:(c + 1) * P], xc[:, c, k * P:(k + 1) * P], ident[:, :])
                    last.then_inc(xT_s, 1)
                if attend:
                    b, q = i - 1, 1 - r
                    pe.wait_ge(phi_s, b + 1)
                    pe.wait_ge(vT_s, b + 1)
                    wait_past(pe, x2_s, b)
                    wait_past(pe, lg_s, i - 4)
                    for s in range(NC):
                        dst = S[2][:, 256:384] if s == 3 else S[s][:, 0:PW[s]]
                        last = t.matmul(dst, vT[:, q, s * P:(s + 1) * P], qk[0:H, q, s * P:T], start=True, stop=True)
                    last.then_inc(score_s, 1)
                if place:
                    b = i - 5
                    pe.wait_ge(ohs_s, b + 1)
                    pe.wait_ge(x2_s, upto(i - 1))
                    flat = ohs[:, :, :].rearrange("p c e -> p (c e)")
                    t.matmul(RANK, before[:, :], flat, start=True, stop=False)
                    for back in range(1, NC):
                        t.matmul(O[:, back * E:NC * E], allone[:, :], flat[:, 0:(NC - back) * E], start=False, stop=back == NC - 1)
                    for c in range(NC):
                        last = t.matmul(TOT, allone[:, :], flat[:, c * E:(c + 1) * E], start=c == 0, stop=c == NC - 1)
                    last.then_inc(rank_s, 1)
                if project:
                    pe.wait_ge(hT_s, i + 1)
                    if r == 0:
                        wait_past(pe, phi_s, i)
                        wait_past(pe, ktok_s, i)
                    else:
                        pe.wait_ge(b1r_s, half + 1)
                    for k in range(NK):
                        t.matmul(Q[:, :], wqk[:, k, :], hT[:, k, :], start=k == 0, stop=k == NK - 1)
                    for k in range(NK):
                        last = t.matmul(V[0:H, :], wv[:, k, :], hT[:, k, :], start=k == 0, stop=k == NK - 1)
                    last.then_inc(proj_s, 1)
                if isinstance(i, int) and i == 0:
                    router_bias()
                if route:
                    b = i - 4
                    pe.wait_ge(nrm_s, b + 1)
                    wait_past(pe, hT_s, i + 1 if project else NB)
                    wait_past(pe, nT_s, b)
                    for k in range(NK):
                        for c in range(NC):
                            last = t.transpose(TR[k][:, c * P:(c + 1) * P], nrm[:, r, c, k * P:(k + 1) * P], ident[:, :])
                    last.then_inc(nTp_s, 1)
                if attend:
                    b, q = i - 1, 1 - r
                    pe.wait_ge(diag_s, b + 1)
                    pe.wait_ge(ktok_s, b + 1)
                    wait_past(pe, x2_s, b)
                    if place:
                        pe.wait_ge(rt_s, i - 4)
                    for s in range(NC):
                        last = t.matmul(O[0:H, s * P:T], ktok[:, q, s, :], pt[:, PO[s]:PO[s] + PW[s]], start=s == 0, stop=s == NC - 1)
                    last.then_inc(pv_s, 1)
                if project:
                    pe.wait_ge(phi_s, i + 1)
                    pe.wait_ge(vT_s, i + 1)
                    hold(pe, "pe")
                    for c in range(NC):
                        last = t.transpose(V[:, c * H:(c + 1) * H], qk[H:2 * H, r, c * P:(c + 1) * P], ident[H:2 * H, H:2 * H])
                    last.then_inc(ktr_s, 1)
                if route:
                    b = i - 4
                    if attend:
                        pe.wait_ge(strip_s, i)
                    else:
                        pe.wait_ge(lg_s, b)
                    pe.wait_ge(nT_s, b + 1)
                    for c in range(NC):
                        for k in range(NK):
                            last = t.matmul(LOG[:, c * E:(c + 1) * E], nT[:, k, c * P:(c + 1) * P], rTg[:, k, :], start=k == 0, stop=k == NK - 1)
                    last.then_inc(log_s, 1)
                if attend:
                    b, q = i - 1, 1 - r
                    pe.wait_ge(strip_s, i)
                    pe.wait_ge(qz_s, b + 1)
                    pe.wait_ge(oT_s, b + 1)
                    pe.wait_ge(wog_s, b + 1)
                    for c in range(NC):
                        last = t.matmul(SO[c][:, 0:D + 1], oz[:, q, c * P:(c + 1) * P], wog[:, q, :], start=True, stop=True)
                    last.then_inc(owo_s, 1)

            pipeline(t, step)
            pe.wait_ge(got_b1v, 16)
            t.transpose(V[:, 0:E * NI], vrow[0:E * NI, :], ident[0:E * NI, 0:E * NI]).then_inc(b1v_ps, 1)

            def turn(j, half, r):
                pe.wait_ge(got_xin[r], 16 * half + 16)
                wait_past(pe, nl_s, j - 1)
                for k in range(NK):
                    for h in range(TH):
                        last = t.transpose(TR[r][:, k * TOK + h * P:k * TOK + (h + 1) * P], xin[:, r, h, k * P:(k + 1) * P], ident[:, :])
                last.then_inc(tr_s, 1)

            def first(j, r, c):
                wait_past(pe, gf_s, NI * j + c - 1)
                n = 0
                for k in range(NK):
                    head = wbuf[:, r, k * I + c * P:k * I + (c + 1) * P]
                    rest = wbuf[:, r, 2048 + k * I + c * P:2048 + k * I + (c + 1) * P]
                    for w, m in ((head, nh), (head, nl), (rest, nh)):
                        last = t.matmul(MM[c % 2][:, 0:TOK], w, m[:, r, k, :], start=n == 0, stop=n == 5)
                        n += 1
                last.then_inc(mm1_s, 1)

            def second(j, r, c):
                pe.wait_ge(gl_s, NI * j + c + 1)
                head = wbuf[:, r, 4096 + c * D:4096 + (c + 1) * D]
                rest = wbuf[:, r, 6144 + c * D:6144 + (c + 1) * D]
                for h in range(TH):
                    n = 0
                    for g, w in ((gh, head), (gh, rest), (gl, head)):
                        last = t.matmul(ACC[r][h][:, 0:D], g[:, c % 4, h * P:(h + 1) * P], w,
                                        start=c == 0 and n == 0, stop=c == NI - 1 and n == 2)
                        n += 1
                last.then_inc(mm2_s, 1)

            def tile(j, half, r, is_first, is_last):
                pe.wait_ge(nl_s, j + 1)
                pe.wait_ge(got_w1[r], 16 * half + 16)
                for c in range(NI):
                    first(j, r, c)
                    if c >= 2:
                        if c == 2:
                            pe.wait_ge(got_w2[r], 16 * half + 16)
                            wait_past(pe, yt_s, j - 1)
                        second(j, r, c - 2)
                    elif not is_first:
                        second(j - 1, 1 - r, NI - 2 + c)
                    if c == 4 and not is_last:
                        turn(j + 1, half + r, 1 - r)

            turn(0, 0, 0)
            for j in range(3):
                tile(j, j // 2, j % 2, j == 0, False)
            with t.Fori(1, (TILES - 1) // 2 - 1) as h:
                tile(2 * h + 1, h, 1, False, False)
                tile(2 * h + 2, h + 1, 0, False, False)
            for j in range((TILES - 1) // 2 * 2 - 1, TILES):
                tile(j, j // 2, j % 2, False, j == TILES - 1)
            second(TILES - 1, (TILES - 1) % 2, NI - 2)
            second(TILES - 1, (TILES - 1) % 2, NI - 1)


_INS = ['L0_attn_x', 'L0_attn_W_q', 'L0_attn_W_k', 'L0_attn_W_v', 'L0_attn_W_o', 'L0_ffn_rn_g', 'L0_ffn_rn_b',
        'L0_ffn_router_w', 'L0_ffn_router_b', 'L0_ffn_ln_g', 'L0_ffn_ln_b', 'L0_ffn_w1', 'L0_ffn_b1',
        'L0_ffn_w2', 'L0_ffn_b2', 'L0_c', 'L0_wmod']


def kernel(**inputs):
    import numpy as _np
    import concourse.bacc as _bacc
    from concourse import mybir as _mybir
    from concourse.bass_utils import run_bass_kernel_spmd as _run

    nc = _bacc.Bacc("TRN2", target_bir_lowering=False, num_devices=1)
    f32, bf16 = _mybir.dt.float32, _mybir.dt.bfloat16
    arrays, args = {}, []
    for name in _INS:
        a = _np.ascontiguousarray(inputs[name])
        arrays[f"in_{name}"] = a
        args.append(nc.dram_tensor(f"in_{name}", a.shape, _mybir.dt.from_np(a.dtype), kind="ExternalInput").ap())
    for name, shape, dt in (("mod_rows", (NB, 6 * D), f32), ("lists", (DUMMY + TOK, RW), f32),
                            ("wsplit", (E, P, 4 * NI * D), bf16), ("b1_rows", (E, 2, I // 2), f32), ("b1_folded", (E, P, NI), f32),
                            ("y_rows", (DUMP + 2 * TOK, D), f32)):
        args.append(nc.dram_tensor(name, shape, dt, kind="Internal").ap())
    args.append(nc.dram_tensor("out_0", (NB, T, D), f32, kind="ExternalOutput").ap())
    adaln_moe_kernel(nc, *args)
    r = _run(nc, [arrays], core_ids=[0])
    return r.results[0]["out_0"]
```
